# Optimizing a Trainium2 kernel written in Bass

```python
import numpy as np
import jax
import jax.numpy as jnp

def _softmax(x, axis=-1):
    return jax.nn.softmax(x, axis=axis)

def _gelu(x):
    return jax.nn.gelu(x, approximate=True)

def _silu(x):
    return jax.nn.silu(x)

def _sigmoid(x):
    return jax.nn.sigmoid(x)

def _layernorm(x, axis=-1, eps=1e-05):
    m = jnp.mean(x, axis=axis, keepdims=True)
    v = jnp.var(x, axis=axis, keepdims=True)
    return (x - m) / jnp.sqrt(v + eps)

def _scatter_add(tgt, idx, src, axis=0):
    return tgt.at[idx].add(src)

def _segment_sum(src, seg, n):
    return jax.ops.segment_sum(src, seg, n)
kernel_name = 'mk_flamingo_gated_d1_seqx_r4_7b7fe6'

def setup_inputs(seed: int=0):
    np.random.seed(seed)
    _w = jnp.asarray

    def _rec_inputs():
        import jax
        import jax.numpy as jnp
        _rk = jax.random.key(seed)
        x = -0.000125 + 0.9999 * jax.random.normal(jax.random.fold_in(_rk, 1), (2, 1024, 256), jnp.float32)
        _lenS = 1024 - jax.random.randint(jax.random.fold_in(_rk, 7), (2,), 0, max(1, 1024 // 4) + 1, jnp.int32)
        _lenS2 = 154 - jax.random.randint(jax.random.fold_in(_rk, 8), (2,), 0, max(1, 154 // 4) + 1, jnp.int32)
        _ctx_768P = jax.random.normal(jax.random.fold_in(_rk, 11), (2, 16, 192), jnp.float32)
        _ctx_768c = jax.random.dirichlet(jax.random.fold_in(_rk, 511), 0.3 * jnp.ones((16,), jnp.float32), (2, 154))
        _ctx_768t = jnp.einsum('bsk,bkd->bsd', _ctx_768c, _ctx_768P)
        _ctx_768t = _ctx_768t * jax.lax.rsqrt(jnp.mean(jnp.square(_ctx_768t)) + 1e-12) * 0.953939
        ctx_768 = 0.00272024 + 0.999456 * (_ctx_768t + 0.3 * jax.random.normal(jax.random.fold_in(_rk, 611), (2, 154, 192), jnp.float32))
        _g = jax.random.normal(jax.random.fold_in(_rk, 9001), (2, 1), jnp.float32)
        _g = jnp.sign(_g) * jnp.maximum(jnp.abs(_g), 1.0) + (_g == 0) * 1.0
        g_xattn = _g[0]
        g_ffn = _g[1]
        return (x, ctx_768, g_xattn, g_ffn)
    x, ctx_768, g_xattn, g_ffn = _rec_inputs()

    def _L0_xattn_setup():
        import jax, jax.numpy as jnp
        import numpy as np
        HEADS = 16
        DIM_HEAD = 64
        SCALE = DIM_HEAD ** (-0.5)
        QUERY_DIM = 256
        CONTEXT_DIM = 192
        INNER_DIM = HEADS * DIM_HEAD
        key = jax.random.key(seed)
        ks = jax.random.split(key, 7)
        B, Nq, Nk = (8, 1024, 77)
        x = jax.random.normal(ks[0], (B, Nq, QUERY_DIM), dtype=jnp.float32)
        context = jax.random.normal(ks[1], (B, Nk, CONTEXT_DIM), dtype=jnp.float32)
        Wq = jax.random.normal(ks[2], (QUERY_DIM, INNER_DIM), dtype=jnp.float32) * QUERY_DIM ** (-0.5)
        Wk = jax.random.normal(ks[3], (CONTEXT_DIM, INNER_DIM), dtype=jnp.float32) * CONTEXT_DIM ** (-0.5)
        Wv = jax.random.normal(ks[4], (CONTEXT_DIM, INNER_DIM), dtype=jnp.float32) * CONTEXT_DIM ** (-0.5)
        Wo = jax.random.normal(ks[5], (INNER_DIM, QUERY_DIM), dtype=jnp.float32) * INNER_DIM ** (-0.5)
        bo = jnp.zeros((QUERY_DIM,), dtype=jnp.float32)
        return {'x': x, 'context': context, 'Wq': Wq, 'Wk': Wk, 'Wv': Wv, 'Wo': Wo, 'bo': bo}
    _L0_xattn_all = _L0_xattn_setup()
    _L0_xattn_in = {k: v for k, v in _L0_xattn_all.items() if k in ('Wq', 'Wk', 'Wv', 'Wo', 'bo')}
    del _L0_xattn_all

    def _L0_ffn_setup():
        import jax, jax.numpy as jnp
        import numpy as np
        D_MODEL = 256
        D_FF = 512
        N_EXPERTS = 8
        TOP_K = 2
        CLAMP = 10000.0
        ROUTER_EPS = 1e-08
        LN_EPS = 1e-05

        def _layernorm(x, g, b):
            mu = jnp.mean(x, axis=-1, keepdims=True)
            var = jnp.mean(jnp.square(x - mu), axis=-1, keepdims=True)
            return (x - mu) * jax.lax.rsqrt(var + LN_EPS) * g + b
        key = jax.random.key(seed)
        k1, k2, k3, k4 = jax.random.split(key, 4)
        B, S = (8, 256)
        x = jax.random.normal(k1, (B, S, D_MODEL), dtype=jnp.float32)
        ln_gamma = jnp.ones((D_MODEL,), jnp.float32)
        ln_beta = jnp.zeros((D_MODEL,), jnp.float32)
        bound = 0.02 * float(np.sqrt(3.0))
        router_w = jax.random.uniform(k2, (N_EXPERTS, D_MODEL), jnp.float32, -bound, bound)
        gate_up_w = jax.random.normal(k3, (N_EXPERTS, 2 * D_FF, D_MODEL), jnp.float32) * (1.0 / np.sqrt(D_MODEL))
        down_w = jax.random.normal(k4, (N_EXPERTS, D_MODEL, D_FF), jnp.float32) * (1.0 / np.sqrt(D_FF))
        return {'x': x, 'ln_gamma': ln_gamma, 'ln_beta': ln_beta, 'router_w': router_w, 'gate_up_w': gate_up_w, 'down_w': down_w}
    _L0_ffn_all = _L0_ffn_setup()
    _L0_ffn_in = {k: v for k, v in _L0_ffn_all.items() if k in ('ln_gamma', 'ln_beta', 'router_w', 'gate_up_w', 'down_w')}
    del _L0_ffn_all
    return {'x': x, 'ctx_768': ctx_768, 'g_xattn': g_xattn, 'g_ffn': g_ffn, 'L0_xattn_Wq': _L0_xattn_in['Wq'], 'L0_xattn_Wk': _L0_xattn_in['Wk'], 'L0_xattn_Wv': _L0_xattn_in['Wv'], 'L0_xattn_Wo': _L0_xattn_in['Wo'], 'L0_xattn_bo': _L0_xattn_in['bo'], 'L0_ffn_ln_gamma': _L0_ffn_in['ln_gamma'], 'L0_ffn_ln_beta': _L0_ffn_in['ln_beta'], 'L0_ffn_router_w': _L0_ffn_in['router_w'], 'L0_ffn_gate_up_w': _L0_ffn_in['gate_up_w'], 'L0_ffn_down_w': _L0_ffn_in['down_w']}

def reference(x, ctx_768, g_xattn, g_ffn, L0_xattn_Wq, L0_xattn_Wk, L0_xattn_Wv, L0_xattn_Wo, L0_xattn_bo, L0_ffn_ln_gamma, L0_ffn_ln_beta, L0_ffn_router_w, L0_ffn_gate_up_w, L0_ffn_down_w):
    import jax
    import jax.numpy as jnp

    def _L0_xattn_ref(x, context, Wq, Wk, Wv, Wo, bo):
        import jax, jax.numpy as jnp
        import numpy as np
        HEADS = 16
        DIM_HEAD = 64
        SCALE = DIM_HEAD ** (-0.5)
        QUERY_DIM = 256
        CONTEXT_DIM = 192
        INNER_DIM = HEADS * DIM_HEAD
        B, Nq, _ = x.shape
        Nk = context.shape[1]
        q = x @ Wq
        k = context @ Wk
        v = context @ Wv
        q = q.reshape(B, Nq, HEADS, DIM_HEAD).transpose(0, 2, 1, 3)
        k = k.reshape(B, Nk, HEADS, DIM_HEAD).transpose(0, 2, 1, 3)
        v = v.reshape(B, Nk, HEADS, DIM_HEAD).transpose(0, 2, 1, 3)
        sim = jnp.einsum('bhid,bhjd->bhij', q, k) * SCALE
        attn = jax.nn.softmax(sim, axis=-1)
        out = jnp.einsum('bhij,bhjd->bhid', attn, v)
        out = out.transpose(0, 2, 1, 3).reshape(B, Nq, INNER_DIM)
        return out @ Wo + bo

    def _L0_ffn_ref(x, ln_gamma, ln_beta, router_w, gate_up_w, down_w):
        import jax, jax.numpy as jnp
        import numpy as np
        D_MODEL = 256
        D_FF = 512
        N_EXPERTS = 8
        TOP_K = 2
        CLAMP = 10000.0
        ROUTER_EPS = 1e-08
        LN_EPS = 1e-05

        def _layernorm(x, g, b):
            mu = jnp.mean(x, axis=-1, keepdims=True)
            var = jnp.mean(jnp.square(x - mu), axis=-1, keepdims=True)
            return (x - mu) * jax.lax.rsqrt(var + LN_EPS) * g + b
        B, S, D = x.shape
        xn = _layernorm(x, ln_gamma, ln_beta)
        xf = xn.reshape(-1, D)
        N = xf.shape[0]
        logits = jnp.clip(xf @ router_w.T, -CLAMP, CLAMP)
        m = jnp.max(logits, axis=-1, keepdims=True)
        e = jnp.exp(logits - m)
        probs = e / (jnp.sum(e, axis=-1, keepdims=True) + ROUTER_EPS)
        probs = jnp.clip(probs, ROUTER_EPS, 1.0)
        topk_p, topk_i = jax.lax.top_k(probs, TOP_K)
        dense_gate = jnp.zeros((N, N_EXPERTS), probs.dtype).at[jnp.arange(N)[:, None], topk_i].add(topk_p)
        out = jnp.zeros_like(xf)
        for eid in range(N_EXPERTS):
            xe = xf * dense_gate[:, eid:eid + 1]
            gu = xe @ gate_up_w[eid].T
            gate, up = jnp.split(gu, 2, axis=-1)
            hidden = jax.nn.silu(gate) * up
            out = out + hidden @ down_w[eid].T
        return x + out.reshape(B, S, D)
    x = x + jnp.tanh(g_xattn[0]) * _L0_xattn_ref(_layernorm(x, axis=-1), ctx_768, L0_xattn_Wq, L0_xattn_Wk, L0_xattn_Wv, L0_xattn_Wo, L0_xattn_bo)
    x = x + jnp.tanh(g_ffn[0]) * _L0_ffn_ref(_layernorm(x, axis=-1), L0_ffn_ln_gamma, L0_ffn_ln_beta, L0_ffn_router_w, L0_ffn_gate_up_w, L0_ffn_down_w)
    return x

_drawn_inputs = setup_inputs


def setup_inputs(seed=0):
    import zlib

    import numpy as np

    out = dict(_drawn_inputs(seed))
    spreads = {'L0_xattn_bo': (0.0, 0.1), 'L0_ffn_ln_gamma': (1.0, 0.2), 'L0_ffn_ln_beta': (0.0, 0.1)}
    factors = {}
    for name, (base, spread) in spreads.items():
        noise = np.random.default_rng([zlib.crc32(name.encode()), seed]).standard_normal(out[name].shape)
        drawn = base * np.exp(spread * noise) if base else spread * noise
        out[name] = jnp.asarray(drawn.astype(out[name].dtype))
    for name, factor in factors.items():
        out[name] = (out[name] * factor).astype(out[name].dtype)
    return out
```

```python
from contextlib import ExitStack

import concourse.bass as bass
from concourse import mybir

ALU = mybir.AluOpType
ACT = mybir.ActivationFunctionType
F32 = mybir.dt.float32
F32R = mybir.dt.float32r
BF16 = mybir.dt.bfloat16
I32 = mybir.dt.int32
U32 = mybir.dt.uint32
AX_X = mybir.AxisListType.X

P = 128
LN_EPS = 1e-5
ROUTER_EPS = 1e-8
CLAMP = 10000.0


def at_least(eng, sem, value):
    if not isinstance(value, int) or value > 0:
        eng.wait_ge(sem, value)


def pick(buf, t):
    if isinstance(t, int):
        return buf[:, t, :]
    return buf[:, bass.ds(t, 1), :].rearrange("p a d -> p (a d)")


def gated_xattn_moe(nc, x, ctxT, g_x, g_f, Wq, Wk, Wv, Wo, bo, gamma, beta, rwT, guT, dnT, out):
    B, SEQ, D = x.shape
    CD, NKB = ctxT.shape[1], ctxT.shape[2]
    INNER = Wq.shape[1]
    DH = 64
    H = INNER // DH
    E = rwT.shape[1]
    FF2 = guT.shape[2]
    FF = FF2 // 2
    N = B * SEQ
    NT = N // P
    CK = CD // 2
    KD = D // P
    KF = FF // P
    HQ = 4
    UPT = H // HQ
    TPI, GPI = 4, 2
    UPI = UPT * TPI
    NI = NT // TPI
    NU = NT * UPT
    GT = 2 * P
    NG = N // GT
    SCALE = float(DH) ** -0.5
    PW = HQ * NKB
    NBLK = -(-PW // P)
    LASTB = PW - (NBLK - 1) * P

    pieces = [(b, j) for b in range(NBLK) for j in range(HQ) if j * NKB < min((b + 1) * P, PW) and (j + 1) * NKB > b * P]
    blk_cols = [[k for k, pc in enumerate(pieces) if pc[0] == b] for b in range(NBLK)]
    VC = len(pieces) * DH

    REG = N + P
    MT = (2 * N - E) // P + E
    DUMMY = E * REG
    RW = D + 1

    with ExitStack() as ctx:
        def sb(name, shape, dt=F32):
            return ctx.enter_context(nc.sbuf_tensor(name, shape, dt))

        def sem(name):
            return ctx.enter_context(nc.semaphore(name))

        bank = [ctx.enter_context(nc.psum_tensor(f"bank{n}", [P, 512], F32)) for n in range(8)]
        S_BANK, TA, TB, O_BANK, M_BANK = bank[0:2], bank[2], bank[3], bank[4:6], bank[6:8]

        queue = nc.dram_tensor("expert_queue", [E * REG + P, RW], F32)

        ident = sb("ident", [P, P])
        before = sb("before", [P, P], BF16)
        ones = sb("ones", [P, P], BF16)
        neg_half = sb("neg_half", [P, 8])
        eps = sb("eps", [P, 8])
        tie_rank = sb("tie_rank", [P, TPI, E])
        region0 = sb("region0", [P, TPI, E])
        token_no = sb("token_no", [P, NT], I32)
        gx = sb("gx", [P, 1]); gf = sb("gf", [P, 1])
        tgx = sb("tgx", [P, 1]); tgf = sb("tgf", [P, 1])
        bo_b = sb("bo_b", [P, D]); gamma_b = sb("gamma_b", [P, D]); beta_b = sb("beta_b", [P, D])
        rw = sb("rw", [P, KD, E])
        x1 = sb("x1", [P, NT, D])
        base_cnt = sb("base_cnt", [P, E])

        s = {}
        for name in ("const ctx_in wk_in wv_in wq_in wo_in small_in ffn_in tanh wq_hi wq_lo kp k_hi k_lo vp vdone "
                     "ptA ptB ptA_sb ptB_sb pv y y_sb "
                     "xstat xrstd xn xres").split():
            s[name] = sem("s_" + name)
        for name, n in dict(x_in=4, scores=2, smax=2, exp=2, o_sb=2, ot_ps=2, ot_sb=2, proj=5, proj_hi=5, proj_sb=5).items():
            s[name] = [sem(f"s_{name}{k}") for k in range(n)]

        with ExitStack() as actx:
            def asb(name, shape, dt=F32):
                return actx.enter_context(nc.sbuf_tensor(name, shape, dt))

            ctx_pad = asb("ctx_pad", [CK, B, 2, P + NKB + P])
            wv = asb("wv", [CK, 2, INNER])
            wq_raw = asb("wq_raw", [P, KD, INNER])
            wq_hi = asb("wq_hi", [P, KD, INNER], F32R)
            wq_lo = asb("wq_lo", [P, KD, INNER], F32R)
            wo = asb("wo", [P, INNER // P, D])
            k_hi = asb("k_hi", [P, H, B, NKB], F32R)
            k_lo = asb("k_lo", [P, H, B, NKB], F32R)
            vdiag = asb("vdiag", [P, B, H // HQ, VC])
            mv = asb("mv", [P, 2, 2, 2]); stat6 = asb("stat6", [P, 2, 2, 6])
            rstd = asb("rstd", [P, 2, 2]); vare = asb("vare", [P, 2, 2])
            xn = asb("xn", [P, 2, 2, D])
            xT_hi = asb("xT_hi", [P, KD, GT], F32R)
            xT_lo = asb("xT_lo", [P, KD, GT], F32R)
            with nc.sbuf_tensor("wk", [CK, 2, H, 2, DH], F32) as wk:
                pass
            qs = [asb(f"qs{n}", [P, H, GT], F32R) for n in (1, 0)][::-1]
            nmax = asb("nmax", [P, 4, HQ])
            probs = [asb(f"probs{n}", [P, PW]) for n in range(4)]
            psum_row = asb("psum_row", [P, 2, H])
            rsum = asb("rsum", [P, H // 2])
            pT = [asb(f"pT{n}", [P, NBLK, P]) for n in range(2)]
            o_sb = asb("o_sb", [P, INNER])
            oT = asb("oT", [P, INNER // P, P])

            block = actx.enter_context(nc.Block())

            JOB_SLOT = {0: 0, 1: 1, 2: 2, 4: 3, 5: 4}
            JOB_BANK = [0, 1, 0, 0, 1]
            FIRST_BANK = [0, 1, 0, 1, 0]

            def tile_at(i, n):
                k, r = divmod(n, TPI)
                return (r // 2) * (SEQ // P) + 2 * (i + k) + r % 2

            @block.sync
            def _(sp):
                for b in range(B):
                    sp.dma_start(ctx_pad[:, b, :, P:P + NKB], ctxT[b].rearrange("(c p) k -> p c k", p=CK)).then_inc(s["ctx_in"], 16)
                for j in range(2):
                    for c in range(2):
                        sp.dma_start(wk[:, c, :, j, :], Wk[c * CK:(c + 1) * CK, :].rearrange("p (h d) -> p h d", h=H)).then_inc(s["wk_in"], 16)
                for n in (0, 2, 1, 3):
                    sp.dma_start(x1[:, 4 * n:4 * n + 4, :], x.rearrange("b (t p) d -> p (b t) d", p=P)[:, 4 * n:4 * n + 4, :]).then_inc(s["x_in"][n], 16)
                    if n == 0:
                        sp.dma_start(wq_raw[:, :, :], Wq.rearrange("(c p) n -> p c n", p=P)).then_inc(s["wq_in"], 16)
                        sp.dma_start(wv[:, :, :], Wv.rearrange("(c p) n -> p c n", p=CK)).then_inc(s["wv_in"], 16)
                for dst, src in ((gx, g_x), (gf, g_f), (bo_b, bo), (gamma_b, gamma), (beta_b, beta)):
                    sp.dma_start(dst[:, :], src.partition_broadcast(P)).then_inc(s["small_in"], 16)
                sp.dma_start(rw[:, :, :], rwT.rearrange("(c p) e -> p c e", p=P)).then_inc(s["small_in"], 16)
                sp.dma_start(wo[:, :, :], Wo.rearrange("(c p) n -> p c n", p=P)).then_inc(s["wo_in"], 16)

            @block.gpsimd
            def _(pool):
                nc.gpsimd.memset(ctx_pad[:, :, :, 0:P], 0.0)
                nc.gpsimd.memset(ctx_pad[:, :, :, P + NKB:], 0.0).then_inc(s["const"], 1)
                nc.gpsimd.memset(ident[:, :], 0.0)
                nc.gpsimd.memset(before[:, :], 1.0)
                nc.gpsimd.memset(ones[:, :], 1.0)
                nc.gpsimd.memset(neg_half[:, :], -0.5)
                nc.gpsimd.memset(eps[:, :], LN_EPS)
                nc.gpsimd.memset(base_cnt[:, :], 0.0)
                nc.gpsimd.iota(token_no[:, :], [[P, NT]], base=0, channel_multiplier=1)
                nc.gpsimd.iota(tie_rank[:, :, :], [[0, TPI], [-1, E]], base=E, channel_multiplier=0, allow_small_or_imprecise_dtypes=True)
                nc.gpsimd.iota(region0[:, :, :], [[0, TPI], [REG, E]], base=0, channel_multiplier=0, allow_small_or_imprecise_dtypes=True)
                nc.gpsimd.drain()
                nc.gpsimd.affine_select(out=ident[:, :], in_=ident[:, :], compare_op=ALU.not_equal, fill=1.0,
                                        base=0, pattern=[[-1, P]], channel_multiplier=1)
                nc.gpsimd.affine_select(out=before[:, :], in_=before[:, :], compare_op=ALU.is_gt, fill=0.0,
                                        base=0, pattern=[[1, P]], channel_multiplier=-1).then_inc(s["const"], 1)

                def rstd_step(i, par):
                    g = GPI * i + par
                    pool.wait_ge(s["xstat"], g + 1)
                    nc.gpsimd.tensor_tensor(vare[:, par, :], mv[:, par, :, 1], eps[:, 0:2], ALU.add)
                    nc.gpsimd.drain()
                    nc.gpsimd.tensor_tensor(rstd[:, par, :], vare[:, par, :], neg_half[:, 0:2], ALU.pow).then_inc(s["xrstd"], 1)

                rstd_step(0, 0)
                rstd_step(0, 1)
                pool.wait_ge(s["wq_in"], 16)
                for c in range(KD):
                    nc.gpsimd.tensor_copy(wq_hi[:, c, :], wq_raw[:, c, :]).then_inc(s["wq_hi"], 1)
                    pool.wait_ge(s["wq_hi"], c + 1)
                    nc.gpsimd.tensor_tensor(wq_lo[:, c, :], wq_raw[:, c, :], wq_hi[:, c, :].bitcast(F32), ALU.subtract).then_inc(s["wq_lo"], 1)
                pool.wait_ge(s["tanh"], 1)
                nc.gpsimd.tensor_scalar(bo_b[:, :], bo_b[:, :], tgx[:, 0:1], None, ALU.mult)
                nc.gpsimd.drain()

                def add_bias(i, gl):
                    pool.wait_ge(s["xn"], GPI * i + gl + 1)
                    for j in range(2):
                        tile = pick(x1, tile_at(i, 2 * gl + j))
                        last = nc.gpsimd.tensor_tensor(tile, tile, bo_b[:, :], ALU.add)
                    last.then_inc(s["xres"], 1)

                add_bias(0, 0)
                add_bias(0, 1)

                def body(i):
                    for gl in range(GPI):
                        rstd_step(i + 1, gl)
                        add_bias(i + 1, gl)

                body(0)
                with pool.Fori(1, NI - 1) as i:
                    body(i)

            @block.tensor
            def _(pe):
                pe.wait_ge(s["ctx_in"], 32)
                pe.wait_ge(s["wk_in"], 64)
                for h in range(H):
                    if h >= 4:
                        pe.wait_ge(s["k_lo"], h - 3)
                    for c in range(2):
                        last = nc.tensor.matmul(bank[h % 4][:, 0:B * NKB].rearrange("p (b k) -> p b k", b=B),
                                                wk[:, c, h, :, :].rearrange("p a d -> p (a d)"), ctx_pad[:, :, c, P:P + NKB],
                                                start=(c == 0), stop=(c == 1))
                    last.then_inc(s["kp"], 1)

                def group_job(g, par, k, banks, free):
                    at = M_BANK[banks[k]]
                    free()
                    if k == 0:
                        pe.wait_ge(s["xn"], g + 1)
                        if isinstance(g, int) and g == 0:
                            pe.wait_ge(s["const"], 2)
                        for j in range(2):
                            for c in range(KD):
                                last = nc.tensor.transpose(at[:, (2 * j + c) * P:(2 * j + c + 1) * P],
                                                           xn[:, par, j, c * P:(c + 1) * P], ident[:, :])
                    else:
                        if k == 1:
                            pe.wait_ge(s["proj_sb"][0], g + 1)
                        for m in range(2):
                            pair = 2 * (k - 1) + m
                            cols = slice(pair * P, (pair + 1) * P)
                            n = 0
                            for c in range(KD):
                                for w, v in ((wq_hi, xT_hi), (wq_lo, xT_hi), (wq_hi, xT_lo)):
                                    last = nc.tensor.matmul(at[:, m * GT:(m + 1) * GT], w[:, c, cols], v[:, c, :],
                                                            start=(n == 0), stop=(n == 5))
                                    n += 1
                    last.then_inc(s["proj"][k], 1)

                def scores(i, u):
                    par, w = (u // 8) % 2, u % 8
                    for hf in range(2):
                        at_least(pe, s["exp"][hf], UPI * i + u)
                        if w < UPT and hf == 0:
                            pe.wait_ge(s["proj_sb"][w + 1], GPI * i + u // 8 + 1)
                        for m in range(2):
                            j = 2 * hf + m
                            h = (u % UPT) * HQ + j
                            tok = ((u // UPT) % 2) * P
                            q = qs[par][:, h, tok:tok + P]
                            cols = slice(m * NKB, (m + 1) * NKB)
                            nc.tensor.matmul(S_BANK[hf][:, cols], q, k_hi[:, h, par, :], start=True, stop=False)
                            last = nc.tensor.matmul(S_BANK[hf][:, cols], q, k_lo[:, h, par, :], start=False, stop=True)
                        last.then_inc(s["scores"][hf], 1)
                        yield

                def transpose_probs(i, u):
                    U = UPI * i + u
                    pe.wait_ge(s["exp"][1], U + 1)
                    at_least(pe, s["ptA_sb"], U)
                    at_least(pe, s["ptB_sb"], U)
                    for b in range(NBLK):
                        rows = P if b < NBLK - 1 else LASTB
                        dst = (TA if b < 3 else TB)[0:rows, (b % 3) * P:(b % 3 + 1) * P]
                        last = nc.tensor.transpose(dst, probs[u % 4][:, b * P:b * P + rows], ident[:, :])
                        if b == 2:
                            last.then_inc(s["ptA"], 1)
                    last.then_inc(s["ptB"], 1)

                def attend(i, u, waits=False):
                    U = UPI * i + u
                    batch = (u // 8) % 2
                    if waits:
                        pe.wait_ge(s["ptA_sb"], U + 1)
                        pe.wait_ge(s["ptB_sb"], U + 1)
                    if u % 2 == 0:
                        at_least(pe, s["ot_sb"][(u % UPT) // 2], TPI * i + u // UPT)
                    at = O_BANK[(u % UPT) // 2]
                    col0 = (u % 2) * HQ * DH
                    g = u % UPT
                    for b in range(NBLK):
                        rows = P if b < NBLK - 1 else LASTB
                        ks = blk_cols[b]
                        j0 = pieces[ks[0]][1]
                        n = len(ks) * DH
                        v = vdiag[0:rows, batch, g, ks[0] * DH:ks[0] * DH + n]
                        last = nc.tensor.matmul(at[:, col0 + j0 * DH:col0 + j0 * DH + n], pT[u % 2][0:rows, b, :],
                                                v, start=(b == 0), stop=(b == NBLK - 1), skip_group_check=True)
                    last.then_inc(s["pv"], 1)

                def transpose_out(i, u):
                    half = (u % UPT) // 2
                    pe.wait_ge(s["o_sb"][half], TPI * i + u // UPT)
                    for c in range(4):
                        last = nc.tensor.transpose(O_BANK[half][:, c * P:(c + 1) * P],
                                                   o_sb[:, (4 * half + c) * P:(4 * half + c + 1) * P], ident[:, :])
                    last.then_inc(s["ot_ps"][half], 1)

                def project_out(i, u):
                    for half in range(2):
                        pe.wait_ge(s["ot_sb"][half], TPI * i + u // UPT)
                    if isinstance(i, int) and TPI * i + u // UPT == 1:
                        pe.wait_ge(s["wo_in"], 16)
                    KO = INNER // P
                    for c in range(KO):
                        last = nc.tensor.matmul(M_BANK[1][:, 0:D], oT[:, c, :], wo[:, c, :], start=(c == 0), stop=(c == KO - 1))
                    last.then_inc(s["y"], 1)

                def slot(i, u):
                    first = isinstance(i, int) and i == 0
                    last = isinstance(i, int) and i == NI - 1
                    ahead = scores(i, u + 2) if not (last and u + 2 >= UPI) else iter(())
                    next(ahead, None)
                    transpose_probs(i, u)
                    if u % 2 == 0 and not (first and u < UPT):
                        transpose_out(i, u)
                    next(ahead, None)
                    w, g = u % 8, GPI * i + u // 8 + 1
                    par = (u // 8 + 1) % 2
                    if w in JOB_SLOT and not (last and u >= 8):
                        k = JOB_SLOT[w]

                        def free():
                            if k == 0:
                                pe.wait_ge(s["proj_sb"][3], g)
                            elif k in (1, 4):
                                at_least(pe, s["y_sb"], TPI * i + u // UPT - 1)
                            else:
                                pe.wait_ge(s["proj_sb"][k - 1 if k == 3 else 0], g + 1)
                        group_job(g, par, k, JOB_BANK, free)
                    if w % UPT == UPT - 1 and not (first and u < UPT):
                        if not (last and u >= 8):
                            pe.wait_ge(s["proj_sb"][1 if w == 3 else 4], g + 1)
                        at_least(pe, s["y_sb"], TPI * i + u // UPT - 1)
                        project_out(i, u)
                    if not (first and u == 0):
                        attend(i, u - 1)

                pe.wait_ge(s["wq_lo"], KD)
                for k in range(5):
                    group_job(0, 0, k, FIRST_BANK, lambda: k >= 2 and pe.wait_ge(s["proj_sb"][k - 2], 1))
                pe.wait_ge(s["k_lo"], H)
                for u in range(2):
                    for _ in scores(0, u):
                        pass
                pe.wait_ge(s["const"], 1)
                pe.wait_ge(s["wv_in"], 16)
                n = 0
                for b in range(B):
                    for m in range(len(pieces) // 2):
                        at = bank[2 + n % 4]
                        if n >= 4:
                            pe.wait_ge(s["vdone"], n - 3)
                        for a in range(2):
                            blk, j = pieces[2 * m + a]
                            lo = P + blk * P - j * NKB
                            for c in range(2):
                                last = nc.tensor.matmul(at[:, :].rearrange("p (g a d) -> p g a d", g=H // HQ, a=2)[:, :, a, :],
                                                        ctx_pad[:, b, c, lo:lo + P],
                                                        wv[:, c, :].rearrange("p (g j d) -> p g j d", j=HQ, d=DH)[:, :, j, :],
                                                        start=(c == 0 and a == 0), stop=(c == 1), skip_group_check=True)
                        last.then_inc(s["vp"], 1)
                        n += 1
                pe.wait_ge(s["vdone"], n + 1)
                for u in range(UPI):
                    slot(0, u)
                with pe.Fori(1, NI - 1) as i:
                    for u in range(UPI):
                        slot(i, u)
                for u in range(UPI):
                    slot(NI - 1, u)
                attend(NI, -1, waits=True)
                transpose_out(NI, 0)
                transpose_out(NI, 2)
                at_least(pe, s["y_sb"], NT - 1)
                project_out(NI, 3)

            @block.scalar
            def _(act):
                act.wait_ge(s["small_in"], 96)
                nc.scalar.activation(tgx[:, :], gx[:, :], ACT.Tanh)
                nc.scalar.activation(tgf[:, :], gf[:, :], ACT.Tanh).then_inc(s["tanh"], 1)
                for h in range(H):
                    act.wait_ge(s["kp"], h + 1)
                    nc.scalar.activation(k_hi[:, h, :, :].rearrange("p b k -> p (b k)"), bank[h % 4][:, 0:B * NKB],
                                         ACT.Copy, scale=SCALE).then_inc(s["k_hi"], 1)

                def high_part(g, k, banks, par):
                    act.wait_ge(s["proj"][k], g + 1)
                    at = M_BANK[banks[k]]
                    if k == 0:
                        last = nc.scalar.copy(xT_hi[:, :, :].rearrange("p c (j t) -> p j c t", j=2),
                                              at[:, :].rearrange("p (j c t) -> p j c t", j=2, c=KD))
                    else:
                        h0 = HQ * (k - 1)
                        for r in range(2):
                            last = nc.scalar.copy(qs[par][0:DH, h0 + r:h0 + r + 3:2, :],
                                                  at[r * DH:(r + 1) * DH, :].rearrange("p (m t) -> p m t", m=2))
                    last.then_inc(s["proj_hi"][k], 1)

                def exps(i, u):
                    for hf in range(2):
                        act.wait_ge(s["smax"][hf], UPI * i + u + 1)
                        for m in range(2):
                            j = 2 * hf + m
                            h = (u % UPT) * HQ + j
                            last = nc.scalar.activation(probs[u % 4][:, j * NKB:(j + 1) * NKB], S_BANK[hf][:, m * NKB:(m + 1) * NKB],
                                                        ACT.Exp, bias=nmax[:, u % 4, j:j + 1], scale=1.0,
                                                        accum_out=psum_row[:, (u // UPT) % 2, h:h + 1])
                        last.then_inc(s["exp"][hf], 1)
                        yield

                def transposed_out(i, u):
                    half = (u % UPT) // 2
                    act.wait_ge(s["ot_ps"][half], TPI * i + u // UPT)
                    nc.scalar.copy(oT[:, 4 * half:4 * half + 4, :].rearrange("p c t -> p (c t)"), O_BANK[half][:, :]).then_inc(s["ot_sb"][half], 1)

                def slot(i, u):
                    first = isinstance(i, int) and i == 0
                    last = isinstance(i, int) and i == NI - 1
                    ahead = exps(i, u + 2) if not (last and u + 2 >= UPI) else iter(())
                    next(ahead, None)
                    act.wait_ge(s["ptA"], UPI * i + u + 1)
                    nc.scalar.copy(pT[u % 2][:, 0:3, :].rearrange("p b t -> p (b t)"), TA[:, 0:3 * P]).then_inc(s["ptA_sb"], 1)
                    if u % 2 == 0 and not (first and u < UPT):
                        transposed_out(i, u)
                    next(ahead, None)
                    w, g = u % 8, GPI * i + u // 8 + 1
                    if w in JOB_SLOT and not (last and u >= 8):
                        high_part(g, JOB_SLOT[w], JOB_BANK, (u // 8 + 1) % 2)

                for k in range(5):
                    high_part(0, k, FIRST_BANK, 0)
                for u in range(2):
                    for _ in exps(0, u):
                        pass
                for u in range(UPI):
                    slot(0, u)
                with act.Fori(1, NI - 1) as i:
                    for u in range(UPI):
                        slot(i, u)
                for u in range(UPI):
                    slot(NI - 1, u)
                transposed_out(NI, 0)
                transposed_out(NI, 2)

            @block.vector
            def _(dve):
                def token_stats(i, gl):
                    par = gl % 2
                    for j in range(2):
                        nc.vector.bn_stats(stat6[:, par, j, :], pick(x1, tile_at(i, 2 * gl + j)))
                    nc.vector.drain()
                    for j in range(2):
                        last = nc.vector.bn_aggr(mv[:, par, j, :], stat6[:, par, j, :])
                    last.then_inc(s["xstat"], 1)

                def normalise(i, gl):
                    par = gl % 2
                    dve.wait_ge(s["xrstd"], GPI * i + gl + 1)
                    for j in range(2):
                        last = nc.vector.tensor_scalar(xn[:, par, j, :], pick(x1, tile_at(i, 2 * gl + j)), mv[:, par, j, 0:1], rstd[:, par, j:j + 1],
                                                       ALU.subtract, ALU.mult)
                    last.then_inc(s["xn"], 1)

                def low_part(g, k, banks, par):
                    dve.wait_ge(s["proj_hi"][k], g + 1)
                    at = M_BANK[banks[k]]
                    if k == 0:
                        last = nc.vector.tensor_tensor(xT_lo[:, :, :].rearrange("p c (j t) -> p j c t", j=2),
                                                       at[:, :].rearrange("p (j c t) -> p j c t", j=2, c=KD),
                                                       xT_hi[:, :, :].rearrange("p c (j t) -> p j c t", j=2).bitcast(F32), ALU.subtract)
                    else:
                        h0 = HQ * (k - 1)
                        for r in range(2):
                            last = nc.vector.tensor_tensor(qs[par][DH:P, h0 + r:h0 + r + 3:2, :],
                                                           at[r * DH:(r + 1) * DH, :].rearrange("p (m t) -> p m t", m=2),
                                                           qs[par][0:DH, h0 + r:h0 + r + 3:2, :].bitcast(F32), ALU.subtract)
                    last.then_inc(s["proj_sb"][k], 1)

                def maxima(i, u):
                    for hf in range(2):
                        dve.wait_ge(s["scores"][hf], UPI * i + u + 1)
                        nc.vector.tensor_reduce(nmax[:, u % 4, 2 * hf:2 * hf + 2], S_BANK[hf][:, 0:2 * NKB].rearrange("p (m k) -> p m k", m=2),
                                                AX_X, ALU.max, negate=True).then_inc(s["smax"][hf], 1)
                        yield

                def scale_out(i, u):
                    half = (u % UPT) // 2
                    U = UPI * i + u
                    dve.wait_ge(s["pv"], U + 1)
                    nc.vector.reciprocal(rsum[:, :], psum_row[:, (u // UPT) % 2, 8 * half:8 * half + 8])
                    nc.vector.drain()
                    nc.vector.tensor_tensor(o_sb[:, half * 512:(half + 1) * 512].rearrange("p (h d) -> p h d", h=8),
                                            O_BANK[half][:, :].rearrange("p (h d) -> p h d", h=8),
                                            rsum[:, :].unsqueeze(2).to_broadcast([P, 8, DH]), ALU.mult).then_inc(s["o_sb"][half], 1)

                def residual_group(i, u):
                    return GPI * i + (u // UPT - 1) // 2

                def add_residual(i, u):
                    dve.wait_ge(s["y"], TPI * i + u // UPT)
                    dve.wait_ge(s["xres"], residual_group(i, u) + 1)
                    tile = pick(x1, tile_at(i, u // UPT - 1))
                    nc.vector.scalar_tensor_tensor(tile, M_BANK[1][:, 0:D], tgx[:, 0:1], tile, ALU.mult, ALU.add).then_inc(s["y_sb"], 1)

                def slot(i, u):
                    first = isinstance(i, int) and i == 0
                    last = isinstance(i, int) and i == NI - 1
                    ahead = maxima(i, u + 2) if not (last and u + 2 >= UPI) else iter(())
                    next(ahead, None)
                    if u % 2 == 1 and not (first and u < 2):
                        scale_out(i, u - 2)
                    dve.wait_ge(s["ptB"], UPI * i + u + 1)
                    nc.vector.tensor_copy(pT[u % 2][:, 3:5, :].rearrange("p b t -> p (b t)"), TB[:, 0:2 * P]).then_inc(s["ptB_sb"], 1)
                    next(ahead, None)
                    w, g = u % 8, GPI * i + u // 8 + 1
                    if w in JOB_SLOT and not (last and u >= 8):
                        low_part(g, JOB_SLOT[w], JOB_BANK, (u // 8 + 1) % 2)
                    if w % UPT == UPT - 1 and not (first and u < UPT):
                        add_residual(i, u)
                    if w == 3 and not last:
                        token_stats(i + 1, u // 8)
                    if w == 6 and not last:
                        normalise(i + 1, u // 8)

                for g in range(2):
                    dve.wait_ge(s["x_in"][2 * g], 16)
                    token_stats(0, g)
                    if g == 1:
                        normalise(0, 0)
                for h in range(H):
                    dve.wait_ge(s["k_hi"], h + 1)
                    nc.vector.scalar_tensor_tensor(k_lo[:, h, :, :].rearrange("p b k -> p (b k)"), bank[h % 4][:, 0:B * NKB], SCALE,
                                                   k_hi[:, h, :, :].rearrange("p b k -> p (b k)").bitcast(F32),
                                                   ALU.mult, ALU.subtract).then_inc(s["k_lo"], 1)
                normalise(0, 1)
                for k in range(5):
                    low_part(0, k, FIRST_BANK, 0)
                for u in range(2):
                    for _ in maxima(0, u):
                        pass
                n = 0
                for b in range(B):
                    for m in range(len(pieces) // 2):
                        dve.wait_ge(s["vp"], n + 1)
                        nc.vector.tensor_copy(vdiag[:, b, :, 2 * m * DH:(2 * m + 2) * DH],
                                              bank[2 + n % 4][:, :].rearrange("p (g c) -> p g c", g=H // HQ)).then_inc(s["vdone"], 1)
                        n += 1
                nc.vector.drain()
                nc.vector.memset(TB[96:P, P:2 * P], 0.0).then_inc(s["vdone"], 1)
                for n in range(4):
                    dve.wait_ge(s["x_in"][n], 16)
                for u in range(UPI):
                    slot(0, u)
                with dve.Fori(1, NI - 1) as i:
                    for u in range(UPI):
                        slot(i, u)
                for u in range(UPI):
                    slot(NI - 1, u)
                scale_out(NI, -1)
                add_residual(NI, 3)

        with ExitStack() as fctx:
            def fsb(name, shape, dt=F32):
                return fctx.enter_context(nc.sbuf_tensor(name, shape, dt))

            gu_w = fsb("gu_w", [P, E * KD, FF2])
            dn_w = fsb("dn_w", [P, E * KF, D])
            table = fsb("table", [P, 2, MT], I32)

            with ExitStack() as rctx:
                def rsb(name, shape, dt=F32):
                    return rctx.enter_context(nc.sbuf_tensor(name, shape, dt))

                stat_b = rsb("stat_b", [P, 2, TPI, 6]); mv_b = rsb("mv_b", [P, 2, TPI, 2])
                vare_b = rsb("vare_b", [P, 2, TPI]); rstd_b = rsb("rstd_b", [P, 2, TPI])
                xin = rsb("xin", [P, TPI, D]); out0 = rsb("out0", [P, TPI, D]); xf = rsb("xf", [P, TPI, D])
                xfT = rsb("xfT", [P, TPI * KD, P])
                lg = rsb("lg", [P, TPI, E]); lmax = rsb("lmax", [P, TPI]); lsh = rsb("lsh", [P, TPI, E]); ex = rsb("ex", [P, TPI, E])
                esum = rsb("esum", [P, TPI]); erec = rsb("erec", [P, TPI]); pr = [rsb(f"pr{n}", [P, TPI, E]) for n in range(2)]
                gate = rsb("gate", [P, 2, TPI]); pick1 = rsb("pick1", [P, 2, TPI, E]); top = rsb("top", [P, TPI, E]); topm = rsb("topm", [P, TPI])
                chosen = rsb("chosen", [P, TPI, E], BF16)
                pos = rsb("pos", [P, TPI, E]); posm = rsb("posm", [P, 2, TPI, E]); rowf = rsb("rowf", [P, 2, TPI]); row = rsb("row", [P, 2, TPI], U32)
                rows = rsb("rows", [P, 2, TPI, RW])
                padf = rsb("padf", [P, E]); pad = rsb("pad", [P, E], U32); lane = rsb("lane", [P, 1]); zrow = rsb("zrow", [P, RW])
                cnt1 = rsb("cnt1", [P, E]); cnti = rsb("cnti", [P, E], I32); tiles = rsb("tiles", [P, E]); cum = rsb("cum", [P, E]); one8 = rsb("one8", [P, E])
                slot_no = rsb("slot_no", [P, MT]); past = rsb("past", [P, MT, E]); pastt = rsb("pastt", [P, MT, E])
                ej = rsb("ej", [P, MT]); sj = rsb("sj", [P, MT]); rj = rsb("rj", [P, MT])
                for name in ("stat1 rs1 stat2 rs2 xin out0 out0_q xf0 xf xfT_ps xfT_sb logits lsh ex chosen pos_ps row_sb rows_q "
                             "zero pads table guw_in dnw_in zero_q").split():
                    s[name] = sem("s_" + name)
                block = rctx.enter_context(nc.Block())

                def four(buf, i):
                    return buf.rearrange("p (b t) d -> p b t d", b=B)[:, :, bass.ds(2 * i, 2) if not isinstance(i, int) else slice(2 * i, 2 * i + 2), :]

                def halves(buf):
                    return buf.rearrange("p (b t) d -> p b t d", b=B)

                @block.sync
                def _(sp):
                    for e in range(E):
                        sp.dma_start(gu_w[:, e * KD:(e + 1) * KD, :], guT[e].rearrange("(c p) f -> p c f", p=P)).then_inc(s["guw_in"], 16)
                        sp.dma_start(dn_w[:, e * KF:(e + 1) * KF, :], dnT[e].rearrange("(c p) d -> p c d", p=P)).then_inc(s["dnw_in"], 16)
                    sp.wait_ge(s["zero"], 1)
                    sp.dma_start(queue[DUMMY:DUMMY + P, :], zrow[:, :]).then_inc(s["zero_q"], 16)
                    sp.dma_start(out[N:N + P, :], zrow[:, 0:D]).then_inc(s["zero_q"], 16)
                    with sp.Fori(0, NI) as i:
                        sp.wait_ge(s["out0"], i + 1)
                        for b in range(B):
                            dst = out[bass.ds((b * (SEQ // P) + 2 * i) * P, 2 * P), :].rearrange("(t p) d -> p t d", p=P)
                            sp.dma_start(dst, out0[:, 2 * b:2 * b + 2, :]).then_inc(s["out0_q"], 16)
                    sp.wait_ge(s["out0_q"], 32 * NI)
                    sp.wait_ge(s["zero_q"], 32)

                @block.gpsimd
                def _(pool):
                    nc.gpsimd.iota(lane[:, :], [[0, 1]], base=0, channel_multiplier=1, allow_small_or_imprecise_dtypes=True)
                    nc.gpsimd.iota(slot_no[:, :], [[1, MT]], base=0, channel_multiplier=0, allow_small_or_imprecise_dtypes=True)
                    nc.gpsimd.memset(one8[:, :], 1.0)
                    nc.gpsimd.memset(zrow[:, 0:D], 0.0)
                    nc.gpsimd.iota(zrow[:, D:RW].bitcast(I32), [[0, 1]], base=N, channel_multiplier=1).then_inc(s["zero"], 1)
                    with pool.Fori(0, NI) as i:
                        for k, (st, rs) in enumerate((("stat1", "rs1"), ("stat2", "rs2"))):
                            pool.wait_ge(s[st], i + 1)
                            nc.gpsimd.tensor_tensor(vare_b[:, k, :], mv_b[:, k, :, 1], eps[:, 0:TPI], ALU.add)
                            nc.gpsimd.drain()
                            nc.gpsimd.tensor_tensor(rstd_b[:, k, :], vare_b[:, k, :], neg_half[:, 0:TPI], ALU.pow).then_inc(s[rs], 1)
                        pool.wait_ge(s["xf0"], i + 1)
                        nc.gpsimd.tensor_tensor(xf[:, :, :], xf[:, :, :], gamma_b[:, :].unsqueeze(1).to_broadcast([P, TPI, D]), ALU.mult)
                        nc.gpsimd.drain()
                        nc.gpsimd.tensor_tensor(xf[:, :, :], xf[:, :, :], beta_b[:, :].unsqueeze(1).to_broadcast([P, TPI, D]), ALU.add).then_inc(s["xf"], 1)
                        pool.wait_ge(s["row_sb"], i + 1)
                        for k in range(2):
                            for j in range(TPI):
                                if k == 0 and j == 0:
                                    nc.gpsimd.tensor_tensor(rows[:, 0, 0, 0:D], xf[:, 0, :], gate[:, 0, 0:1].to_broadcast([P, D]), ALU.mult)
                                    continue
                                nc.gpsimd.tensor_scalar(rows[:, k, j, 0:D], xf[:, j, :], gate[:, k, j:j + 1], None, ALU.mult)
                            nc.gpsimd.tensor_copy(rows[:, k, :, D:RW].bitcast(I32).rearrange("p (b t) o -> p b (t o)", b=B),
                                                  token_no[:, :].rearrange("p (b t) -> p b t", b=B)[:, :, bass.ds(2 * i, 2)])
                        nc.gpsimd.drain()
                        for k in range(2):
                            for j in range(TPI):
                                nc.gpsimd.indirect_dma_start(queue[:, :], bass.IndirectOffsetOnAxis(row[:, k, j:j + 1], 0),
                                                             rows[:, k, j, :], None).then_inc(s["rows_q"], 16)
                        pool.wait_ge(s["rows_q"], 16 * 2 * TPI * (i + 1))
                    pool.wait_ge(s["pads"], 1)
                    for e in range(E):
                        nc.gpsimd.indirect_dma_start(queue[:, :], bass.IndirectOffsetOnAxis(pad[:, e:e + 1], 0),
                                                     zrow[:, :], None).then_inc(s["rows_q"], 16)
                    pool.wait_ge(s["rows_q"], 16 * (2 * NT + E))

                @block.tensor
                def _(pe):
                    with pe.Fori(0, NI) as i:
                        pe.wait_ge(s["xf"], i + 1)
                        for m in range(2):
                            for a in range(4):
                                j, c = 2 * m + a // 2, a % 2
                                last = nc.tensor.transpose(M_BANK[m][:, a * P:(a + 1) * P], xf[:, j, c * P:(c + 1) * P], ident[:, :])
                            last.then_inc(s["xfT_ps"], 1)
                        pe.wait_ge(s["xfT_sb"], 2 * i + 2)
                        for j in range(TPI):
                            for c in range(KD):
                                last = nc.tensor.matmul(TA[:, j * E:(j + 1) * E], xfT[:, j * KD + c, :], rw[:, c, :],
                                                        start=(c == 0), stop=(c == KD - 1))
                        last.then_inc(s["logits"], 1)
                        pe.wait_ge(s["chosen"], i + 1)
                        flat = chosen[:, :, :].rearrange("p t e -> p (t e)")
                        nc.tensor.matmul(TB[:, 0:TPI * E], before[:, :], flat, start=True, stop=False, skip_group_check=True)
                        for j in range(TPI - 1):
                            for jj in range(j + 1, TPI):
                                nc.tensor.matmul(TB[:, jj * E:(jj + 1) * E], ones[:, :], chosen[:, j, :], start=False, stop=(jj == j + 1), skip_group_check=True)
                        for j in range(TPI):
                            last = nc.tensor.matmul(TB[:, TPI * E:(TPI + 1) * E], ones[:, :], chosen[:, j, :], start=False, stop=(j == TPI - 1), skip_group_check=True)
                        last.then_inc(s["pos_ps"], 1)

                @block.scalar
                def _(act):
                    with act.Fori(0, NI) as i:
                        for m in range(2):
                            act.wait_ge(s["xfT_ps"], 2 * i + m + 1)
                            nc.scalar.copy(xfT[:, 4 * m:4 * m + 4, :].rearrange("p c t -> p (c t)"), M_BANK[m][:, :]).then_inc(s["xfT_sb"], 1)
                        act.wait_ge(s["lsh"], i + 1)
                        nc.scalar.activation(ex[:, :, :], lsh[:, :, :], ACT.Exp).then_inc(s["ex"], 1)

                @block.vector
                def _(dve):
                    v = nc.vector

                    def then(ins):
                        v.drain()
                        return ins

                    def over_experts(ap):
                        return ap.unsqueeze(2).to_broadcast([P, TPI, E])

                    with dve.Fori(0, NI) as i:
                        x4 = four(x1, i)
                        for j in range(TPI):
                            v.bn_stats(stat_b[:, 0, j, :], pick(x1, tile_at(i, j)))
                        v.drain()
                        for j in range(TPI):
                            last = v.bn_aggr(mv_b[:, 0, j, :], stat_b[:, 0, j, :])
                        last.then_inc(s["stat1"], 1)
                        dve.wait_ge(s["rs1"], i + 1)
                        for j in range(TPI):
                            v.tensor_scalar(xin[:, j, :], pick(x1, tile_at(i, j)), mv_b[:, 0, j, 0:1], rstd_b[:, 0, j:j + 1], ALU.subtract, ALU.mult)
                        v.drain()
                        for j in range(TPI):
                            v.bn_stats(stat_b[:, 1, j, :], xin[:, j, :])
                        v.drain()
                        for j in range(TPI):
                            last = v.bn_aggr(mv_b[:, 1, j, :], stat_b[:, 1, j, :])
                        last.then_inc(s["stat2"], 1)
                        at_least(dve, s["out0_q"], 32 * i)
                        v.scalar_tensor_tensor(out0[:, :, :].rearrange("p (b t) d -> p b t d", b=B), halves(xin[:, :, :]), tgf[:, 0:1], x4,
                                               ALU.mult, ALU.add).then_inc(s["out0"], 1)
                        dve.wait_ge(s["rs2"], i + 1)
                        at_least(dve, s["rows_q"], 16 * 2 * TPI * i)
                        for j in range(TPI):
                            last = v.tensor_scalar(xf[:, j, :], xin[:, j, :], mv_b[:, 1, j, 0:1], rstd_b[:, 1, j:j + 1], ALU.subtract, ALU.mult)
                        last.then_inc(s["xf0"], 1)
                        dve.wait_ge(s["logits"], i + 1)
                        then(v.tensor_scalar(lg[:, :, :], TA[:, 0:TPI * E].rearrange("p (t e) -> p t e", t=TPI), CLAMP, -CLAMP, ALU.min, ALU.max))
                        then(v.tensor_reduce(lmax[:, :], lg[:, :, :], AX_X, ALU.max))
                        v.tensor_tensor(lsh[:, :, :], lg[:, :, :], over_experts(lmax[:, :]), ALU.subtract).then_inc(s["lsh"], 1)
                        dve.wait_ge(s["ex"], i + 1)
                        then(v.tensor_reduce(esum[:, :], ex[:, :, :], AX_X, ALU.add))
                        then(v.tensor_scalar(esum[:, :], esum[:, :], ROUTER_EPS, None, ALU.add))
                        then(v.reciprocal(erec[:, :], esum[:, :]))
                        then(v.tensor_tensor(pr[0][:, :, :], ex[:, :, :], over_experts(erec[:, :]), ALU.mult))
                        then(v.tensor_scalar(pr[0][:, :, :], pr[0][:, :, :], ROUTER_EPS, 1.0, ALU.max, ALU.min))
                        for k in range(2):
                            then(v.tensor_reduce(gate[:, k, :], pr[k][:, :, :], AX_X, ALU.max))
                            then(v.tensor_tensor(top[:, :, :], pr[k][:, :, :], over_experts(gate[:, k, :]), ALU.is_ge))
                            then(v.tensor_tensor(top[:, :, :], top[:, :, :], tie_rank[:, :, :], ALU.mult))
                            then(v.tensor_reduce(topm[:, :], top[:, :, :], AX_X, ALU.max))
                            then(v.tensor_tensor(pick1[:, k, :, :], top[:, :, :], over_experts(topm[:, :]), ALU.is_equal))
                            if k == 0:
                                then(v.scalar_tensor_tensor(pr[1][:, :, :], pick1[:, 0, :, :], -4.0, pr[0][:, :, :], ALU.mult, ALU.add))
                        v.tensor_tensor(chosen[:, :, :], pick1[:, 0, :, :], pick1[:, 1, :, :], ALU.add).then_inc(s["chosen"], 1)
                        dve.wait_ge(s["pos_ps"], i + 1)
                        then(v.tensor_tensor(pos[:, :, :], TB[:, 0:TPI * E].rearrange("p (t e) -> p t e", t=TPI),
                                             base_cnt[:, :].unsqueeze(1).to_broadcast([P, TPI, E]), ALU.add))
                        v.tensor_tensor(base_cnt[:, :], base_cnt[:, :], TB[:, TPI * E:(TPI + 1) * E], ALU.add)
                        then(v.tensor_tensor(pos[:, :, :], pos[:, :, :], region0[:, :, :], ALU.add))
                        then(v.tensor_tensor(posm[:, :, :, :], pick1[:, :, :, :], pos[:, :, :].unsqueeze(1).to_broadcast([P, 2, TPI, E]), ALU.mult))
                        then(v.tensor_reduce(rowf[:, :, :], posm[:, :, :, :], AX_X, ALU.add))
                        v.tensor_copy(row[:, :, :], rowf[:, :, :]).then_inc(s["row_sb"], 1)
                    v.drain()
                    dve.wait_ge(s["zero"], 1)
                    then(v.tensor_tensor(padf[:, :], base_cnt[:, :], region0[:, 0, :], ALU.add))
                    then(v.tensor_scalar(padf[:, :], padf[:, :], lane[:, 0:1], None, ALU.add))
                    v.tensor_copy(pad[:, :], padf[:, :]).then_inc(s["pads"], 1)
                    then(v.tensor_scalar(cnt1[:, :], base_cnt[:, :], float(P - 1), None, ALU.add))
                    then(v.tensor_copy(cnti[:, :], cnt1[:, :]))
                    then(v.tensor_scalar(cnti[:, :], cnti[:, :], P.bit_length() - 1, None, ALU.logical_shift_right))
                    then(v.tensor_copy(tiles[:, :], cnti[:, :]))
                    then(v.tensor_tensor_scan(cum[:, :], one8[:, :], tiles[:, :], 0.0, ALU.mult, ALU.add))
                    by_slot = [P, MT, E]
                    then(v.tensor_tensor(past[:, :, :], slot_no[:, :].unsqueeze(2).to_broadcast(by_slot), cum[:, :].unsqueeze(1).to_broadcast(by_slot), ALU.is_ge))
                    then(v.tensor_reduce(ej[:, :], past[:, :, :], AX_X, ALU.add))
                    then(v.tensor_tensor(pastt[:, :, :], past[:, :, :], tiles[:, :].unsqueeze(1).to_broadcast(by_slot), ALU.mult))
                    then(v.tensor_reduce(sj[:, :], pastt[:, :, :], AX_X, ALU.add))
                    then(v.tensor_tensor(rj[:, :], slot_no[:, :], sj[:, :], ALU.subtract))
                    then(v.tensor_scalar(rj[:, :], rj[:, :], float(P), None, ALU.mult))
                    then(v.scalar_tensor_tensor(rj[:, :], ej[:, :], float(REG), rj[:, :], ALU.mult, ALU.add))
                    then(v.tensor_scalar(rj[:, :], rj[:, :], float(DUMMY), None, ALU.min))
                    then(v.tensor_scalar(ej[:, :], ej[:, :], float(E - 1), None, ALU.min))
                    v.tensor_copy(table[:, 0, :], ej[:, :])
                    v.tensor_copy(table[:, 1, :], rj[:, :]).then_inc(s["table"], 1)

            xq = [fsb(f"xq{n}", [P, RW]) for n in range(2)]
            tok = [fsb(f"tok{n}", [P, 1], U32) for n in range(2)]
            to_row = fsb("to_row", [P, 1], U32); no_offset = fsb("no_offset", [P, 1], U32)
            xqT = [fsb(f"xqT{n}", [P, KD, P]) for n in range(2)]
            act_g = [fsb(f"act_g{n}", [P, FF]) for n in range(2)]
            hid = [fsb(f"hid{n}", [P, FF]) for n in range(2)]
            hidT = fsb("hidT", [P, KF, P])
            yq = [fsb(f"yq{n}", [P, D]) for n in range(2)]
            for name in "eT_ps eT_sb e_gate e_silu e_up e_hid e_hT_ps e_hT_sb e_y e_ysb e_tok e_idx".split():
                s[name] = sem("s_" + name)
            s["xq_in"] = [sem(f"s_xq_in{n}") for n in range(2)]
            s["e_add"] = sem("s_e_add")
            G_BANK, U_BANK, XT_BANK, HT_BANK, Y_BANK = bank[0:2], bank[2:4], bank[4], bank[5], bank[6]
            LOOPS = (MT - 1) // 2
            block = fctx.enter_context(nc.Block())

            @block.sync
            def _(sp):
                sp.wait_ge(s["table"], 1)

                def load(i, p, free=True):
                    j = 2 * i + p
                    r = sp.value_load(table[0:1, 1, bass.ds(j, 1)] if not isinstance(j, int) else table[0:1, 1, j:j + 1], min_val=0, max_val=DUMMY)
                    if free:
                        sp.wait_ge(s["eT_ps"], j - 1)
                        sp.wait_ge(s["e_tok"], j - 1)
                    sp.dma_start(xq[p][:, :], queue[bass.ds(r, P), :]).then_inc(s["xq_in"][p], 16)

                load(0, 0, False)
                load(0, 1, False)
                with sp.Fori(1, LOOPS) as i:
                    for p in range(2):
                        load(i, p)
                load(LOOPS, 0)

            @block.gpsimd
            def _(pool):
                def tokens(i, p):
                    j = 2 * i + p
                    pool.wait_ge(s["xq_in"][p], 16 * (i + 1))
                    at_least(pool, s["e_idx"], j - 1)
                    nc.gpsimd.tensor_tensor(tok[p][:, :], xq[p][:, D:RW].bitcast(U32), no_offset[:, :], ALU.add).then_inc(s["e_tok"], 1)

                def scatter_add(i, p):
                    j = 2 * i + p
                    pool.wait_ge(s["e_ysb"], j + 1)
                    pool.wait_ge(s["e_tok"], j + 1)
                    at_least(pool, s["e_add"], 16 * j)
                    nc.gpsimd.tensor_tensor(to_row[:, :], tok[p][:, :], no_offset[:, :], ALU.add).then_inc(s["e_idx"], 1)
                    nc.gpsimd.drain()
                    nc.gpsimd.indirect_dma_start(out[:, :], bass.IndirectOffsetOnAxis(to_row[:, 0:1], 0), yq[p][:, :], None,
                                                 compute_op=ALU.add).then_inc(s["e_add"], 16)

                nc.gpsimd.memset(no_offset[:, :], 0)
                nc.gpsimd.drain()
                tokens(0, 0)
                tokens(0, 1)
                scatter_add(0, 0)
                with pool.Fori(1, LOOPS) as i:
                    tokens(i, 0)
                    scatter_add(i - 1, 1)
                    tokens(i, 1)
                    scatter_add(i, 0)
                tokens(LOOPS, 0)
                scatter_add(LOOPS - 1, 1)
                scatter_add(LOOPS, 0)
                pool.wait_ge(s["e_add"], 16 * MT)

            @block.tensor
            def _(pe):
                pe.wait_ge(s["table"], 1)
                pe.wait_ge(s["guw_in"], 16 * E)
                pe.wait_ge(s["dnw_in"], 16 * E)

                def transpose_rows(i, p):
                    j = 2 * i + p
                    pe.wait_ge(s["xq_in"][p], 16 * (i + 1))
                    at_least(pe, s["eT_sb"], j)
                    for c in range(KD):
                        last = nc.tensor.transpose(XT_BANK[:, c * P:(c + 1) * P], xq[p][:, c * P:(c + 1) * P], ident[:, :])
                    last.then_inc(s["eT_ps"], 1)

                def expert_of(j):
                    return pe.value_load(table[0:1, 0, bass.ds(j, 1)] if not isinstance(j, int) else table[0:1, 0, j:j + 1], min_val=0, max_val=E - 1)

                def up(i, p, e, half, at, done, free):
                    j = 2 * i + p
                    pe.wait_ge(s["eT_sb"], j + 1)
                    at_least(pe, s[free], j - 1)
                    for c in range(KD):
                        w = gu_w[:, bass.ds(e * KD + c, 1), half * FF:(half + 1) * FF].rearrange("p a f -> p (a f)")
                        last = nc.tensor.matmul(at[p][:, :], xqT[p][:, c, :], w, start=(c == 0), stop=(c == KD - 1))
                    last.then_inc(s[done], 1)

                def transpose_hidden(i, p):
                    j = 2 * i + p
                    pe.wait_ge(s["e_hid"], j + 1)
                    at_least(pe, s["e_hT_sb"], j)
                    for c in range(KF):
                        last = nc.tensor.transpose(HT_BANK[:, c * P:(c + 1) * P], hid[p][:, c * P:(c + 1) * P], ident[:, :])
                    last.then_inc(s["e_hT_ps"], 1)

                def down(i, p, e):
                    j = 2 * i + p
                    pe.wait_ge(s["e_hT_sb"], j + 1)
                    at_least(pe, s["e_ysb"], j)
                    for c in range(KF):
                        w = dn_w[:, bass.ds(e * KF + c, 1), :].rearrange("p a d -> p (a d)")
                        last = nc.tensor.matmul(Y_BANK[:, 0:D], hidT[:, c, :], w, start=(c == 0), stop=(c == KF - 1))
                    last.then_inc(s["e_y"], 1)

                def slot(i, p, more=True):
                    e = expert_of(2 * i + p)
                    before_it = (i - 1 + p, 1 - p)
                    behind = not (isinstance(i, int) and i == 0 and p == 0)
                    if more:
                        transpose_rows(i + p, 1 - p)
                    up(i, p, e, 0, G_BANK, "e_gate", "e_silu")
                    if behind:
                        transpose_hidden(*before_it)
                    up(i, p, e, 1, U_BANK, "e_up", "e_hid")
                    if behind:
                        down(*before_it, expert_of(2 * i + p - 1))

                transpose_rows(0, 0)
                slot(0, 0)
                slot(0, 1)
                with pe.Fori(1, LOOPS) as i:
                    slot(i, 0)
                    slot(i, 1)
                slot(LOOPS, 0, more=False)
                transpose_hidden(LOOPS, 0)
                down(LOOPS, 0, expert_of(2 * LOOPS))

            @block.scalar
            def _(act):
                def rows_T(i, p):
                    j = 2 * i + p
                    act.wait_ge(s["eT_ps"], j + 1)
                    nc.scalar.copy(xqT[p][:, :, :].rearrange("p c t -> p (c t)"), XT_BANK[:, 0:KD * P]).then_inc(s["eT_sb"], 1)

                def silu(i, p):
                    j = 2 * i + p
                    act.wait_ge(s["e_gate"], j + 1)
                    at_least(act, s["e_hid"], j - 1)
                    nc.scalar.activation(act_g[p][:, :], G_BANK[p][:, :], ACT.Silu).then_inc(s["e_silu"], 1)

                def scaled(i, p):
                    j = 2 * i + p
                    act.wait_ge(s["e_y"], j + 1)
                    at_least(act, s["e_add"], 16 * (j - 1))
                    nc.scalar.activation(yq[p][:, :], Y_BANK[:, 0:D], ACT.Copy, scale=tgf[:, 0:1]).then_inc(s["e_ysb"], 1)

                rows_T(0, 0)
                rows_T(0, 1)
                silu(0, 0)
                rows_T(1, 0)
                silu(0, 1)
                scaled(0, 0)
                with act.Fori(1, LOOPS) as i:
                    rows_T(i, 1)
                    silu(i, 0)
                    scaled(i - 1, 1)
                    rows_T(i + 1, 0)
                    silu(i, 1)
                    scaled(i, 0)
                silu(LOOPS, 0)
                scaled(LOOPS - 1, 1)
                scaled(LOOPS, 0)

            @block.vector
            def _(dve):
                def gated(i, p):
                    j = 2 * i + p
                    dve.wait_ge(s["e_silu"], j + 1)
                    dve.wait_ge(s["e_up"], j + 1)
                    nc.vector.tensor_tensor(hid[p][:, :], act_g[p][:, :], U_BANK[p][:, :], ALU.mult).then_inc(s["e_hid"], 1)

                def hidden_T(i, p):
                    j = 2 * i + p
                    dve.wait_ge(s["e_hT_ps"], j + 1)
                    at_least(dve, s["e_y"], j)
                    nc.vector.tensor_copy(hidT[:, :, :].rearrange("p c t -> p (c t)"), HT_BANK[:, :]).then_inc(s["e_hT_sb"], 1)

                gated(0, 0)
                hidden_T(0, 0)
                gated(0, 1)
                with dve.Fori(1, LOOPS) as i:
                    hidden_T(i - 1, 1)
                    gated(i, 0)
                    hidden_T(i, 0)
                    gated(i, 1)
                hidden_T(LOOPS - 1, 1)
                gated(LOOPS, 0)
                hidden_T(LOOPS, 0)

_INS = ['x', 'ctxT', 'g_xattn', 'g_ffn', 'L0_xattn_Wq', 'L0_xattn_Wk', 'L0_xattn_Wv', 'L0_xattn_Wo', 'L0_xattn_bo',
        'L0_ffn_ln_gamma', 'L0_ffn_ln_beta', 'router_wT', 'gate_up_wT', 'down_wT']


def kernel(**inputs):
    import numpy as _np
    import concourse.bacc as _bacc
    from concourse import mybir as _mybir
    from concourse.bass_utils import run_bass_kernel_spmd as _run

    laid = {k: _np.asarray(v) for k, v in inputs.items()}
    laid['ctxT'] = laid['ctx_768'].transpose(0, 2, 1)
    laid['router_wT'] = laid['L0_ffn_router_w'].transpose(1, 0)
    laid['gate_up_wT'] = laid['L0_ffn_gate_up_w'].transpose(0, 2, 1)
    laid['down_wT'] = laid['L0_ffn_down_w'].transpose(0, 2, 1)
    B, SEQ, D = laid['x'].shape
    nc = _bacc.Bacc("TRN2", target_bir_lowering=False, num_devices=1)
    arrays, args = {}, []
    for name in _INS:
        a = _np.ascontiguousarray(laid[name])
        arrays[f"in_{name}_dram"] = a
        args.append(nc.dram_tensor(f"in_{name}_dram", a.shape, _mybir.dt.from_np(a.dtype), kind="ExternalInput").ap())
    out = nc.dram_tensor("out_dram", (B * SEQ + 128, D), _mybir.dt.float32, kind="ExternalOutput").ap()
    gated_xattn_moe(nc, *args, out)
    r = _run(nc, [arrays], core_ids=[0])
    return r.results[0]["out_dram"][:B * SEQ].reshape(B, SEQ, D)
```

```python
from contextlib import ExitStack

import concourse.bass as bass
from concourse import mybir

ALU = mybir.AluOpType
ACT = mybir.ActivationFunctionType
F32 = mybir.dt.float32
F32R = mybir.dt.float32r
BF16 = mybir.dt.bfloat16
I32 = mybir.dt.int32
U32 = mybir.dt.uint32
U16 = mybir.dt.uint16
AX_X = mybir.AxisListType.X

P = 128
LN_EPS = 1e-5
ROUTER_EPS = 1e-8
CLAMP = 10000.0


def at_least(eng, sem, value):
    if not isinstance(value, int) or value > 0:
        eng.wait_ge(sem, value)


def pick(buf, t):
    if isinstance(t, int):
        return buf[:, t, :]
    return buf[:, bass.ds(t, 1), :].rearrange("p a d -> p (a d)")


def pick_cols(buf, t, col, n):
    if isinstance(t, int):
        return buf[:, t, col:col + n]
    return buf[:, bass.ds(t, 1), col:col + n].rearrange("p a d -> p (a d)")


def gated_xattn_moe(nc, x, ctxT, g_x, g_f, Wq, Wk, Wv, Wo, bo, gamma, beta, rwT, guT, dnT, out):
    B, SEQ, D = x.shape
    CD, NKB = ctxT.shape[1], ctxT.shape[2]
    INNER = Wq.shape[1]
    DH = 64
    H = INNER // DH
    E = rwT.shape[1]
    FF2 = guT.shape[2]
    FF = FF2 // 2
    N = B * SEQ
    NT = N // P
    CK = CD // 2
    KD = D // P
    KF = FF // P
    HQ = 4
    UPT = H // HQ
    TPI, GPI = 4, 2
    UPI = UPT * TPI
    NI = NT // TPI
    NU = NT * UPT
    GT = 2 * P
    NG = N // GT
    SCALE = float(DH) ** -0.5
    PW = HQ * NKB
    NBLK = -(-PW // P)
    LASTB = PW - (NBLK - 1) * P

    pieces = [(b, j) for b in range(NBLK) for j in range(HQ) if j * NKB < min((b + 1) * P, PW) and (j + 1) * NKB > b * P]
    blk_cols = [[k for k, pc in enumerate(pieces) if pc[0] == b] for b in range(NBLK)]
    VC = len(pieces) * DH

    REG = N + P
    MT = (2 * N - E) // P + E
    DUMMY = E * REG
    RW = D + 1

    RT = 2 * N // P // E
    LOOPS = MT // RT
    CHUNK = KF * D
    FIRST_CHUNKS = [(), (), (0, 1), (2,)]

    with ExitStack() as ctx:
        def sb(name, shape, dt=F32):
            return ctx.enter_context(nc.sbuf_tensor(name, shape, dt))

        def sem(name):
            return ctx.enter_context(nc.semaphore(name))

        bank = [ctx.enter_context(nc.psum_tensor(f"bank{n}", [P, 512], F32)) for n in range(8)]
        S_BANK, TA, TB, O_BANK, M_BANK = bank[0:2], bank[2], bank[3], bank[4:6], bank[6:8]

        queue = nc.dram_tensor("expert_queue", [E * REG + P, RW], F32)

        s = {}
        for name in ("const ctx_in wk_in wv_in wq_in wo_in small_in ffn_in tanh wq_hi wq_lo kp k_hi k_lo vp vdone "
                     "stat1 rs1 stat2 rs2 xin out0 out0_q xf0 xf xfT_ps logits lg_read lsh ex chosen pos_ps row_sb rows_q "
                     "k_zero zero pads order zero_q wo_split "
                     "ptA ptB ptA_sb ptB_sb pv y y_sb "
                     "xstat xrstd xn xres "
                     "w_in w_hi w_lo eT_ps eT_hi eT_lo e_gate e_silu e_up e_hid e_hT_ps e_hT_hi e_hT_lo e_y e_ysb e_tok e_idx e_add").split():
            s[name] = sem("s_" + name)
        for name, n in dict(xq_in=2, xfT_sb=2, ot_hi=2, x_in=4, scores=2, smax=2, exp=2, o_sb=2, ot_ps=2, ot_sb=2, proj=5, proj_hi=5, proj_sb=5).items():
            s[name] = [sem(f"s_{name}{k}") for k in range(n)]

        ident = sb("ident", [P, P])
        gx = sb("gx", [P, 1]); gf = sb("gf", [P, 1])
        tgx = sb("tgx", [P, 1]); tgf = sb("tgf", [P, 1])
        table = sb("table", [P, 2, MT], U16)
        order = sb("order", [P, E], U16)

        with ExitStack() as fctx:
            def fsb(name, shape, dt=F32):
                return fctx.enter_context(nc.sbuf_tensor(name, shape, dt))

            with ExitStack() as early:
                gu_raw = early.enter_context(nc.sbuf_tensor("gu_raw", [P, E, KD * FF2], F32))
                dn_raw = early.enter_context(nc.sbuf_tensor("dn_raw", [P, E, KF * D], F32))
            gu_lo = fsb("gu_lo", [P, E, KD * FF2], F32R)
            dn_lo = fsb("dn_lo", [P, E, KF * D], F32R)
            gu_hi = fsb("gu_hi", [P, E, KD * FF2], F32R)
            dn_hi = fsb("dn_hi", [P, E, KF * D], F32R)
            xq = [fsb(f"xq{n}", [P, RW]) for n in range(2)]
            tok = [fsb(f"tok{n}", [P, 1], U32) for n in range(2)]
            to_row = fsb("to_row", [P, 1], U32); no_offset = fsb("no_offset", [P, 1], U32)
            xqT_hi = fsb("xqT_hi", [P, KD, P], F32R)
            xqT_lo = fsb("xqT_lo", [P, KD, P], F32R)
            hid = [fsb(f"hid{n}", [P, FF]) for n in range(2)]
            hidT_hi = fsb("hidT_hi", [P, KF, P], F32R)
            hidT_lo = fsb("hidT_lo", [P, KF, P], F32R)
            yq = [fsb(f"yq{n}", [P, D]) for n in range(2)]
        G_BANK, U_BANK, XT_BANK, HT_BANK, Y_BANK = bank[0:2], bank[2:4], bank[4], bank[5], bank[6:8]

        def load_weights(sp, rank):
            e = sp.value_load(order[0:1, rank:rank + 1] if isinstance(rank, int) else order[0:1, bass.ds(rank, 1)], min_val=0, max_val=E - 1)
            for src, raw in ((guT, gu_raw), (dnT, dn_raw)):
                w = src[bass.ds(e, 1)].rearrange("a (c p) f -> p (a c) f", p=P)
                sp.dma_start(pick(raw, rank).rearrange("p (c f) -> p c f", f=src.shape[2]), w).then_inc(s["w_in"], 16)

        CHUNKS = [(gu_raw, gu_hi, gu_lo, 0), (gu_raw, gu_hi, gu_lo, CHUNK), (dn_raw, dn_hi, dn_lo, 0)]

        def split_high(act, rank, n):
            raw, hi, _, col = CHUNKS[n]
            act.wait_ge(s["w_in"], 32 * (rank + 1))
            nc.scalar.copy(pick_cols(hi, rank, col, CHUNK), pick_cols(raw, rank, col, CHUNK)).then_inc(s["w_hi"], 1)

        def split_low(dve, rank, n):
            raw, hi, lo, col = CHUNKS[n]
            dve.wait_ge(s["w_hi"], len(CHUNKS) * rank + n + 1)
            nc.vector.tensor_tensor(pick_cols(lo, rank, col, CHUNK), pick_cols(raw, rank, col, CHUNK),
                                    pick_cols(hi, rank, col, CHUNK).bitcast(F32), ALU.subtract).then_inc(s["w_lo"], 1)

        with ExitStack() as actx:
            def asb(name, shape, dt=F32):
                return actx.enter_context(nc.sbuf_tensor(name, shape, dt))

            wq_hi = asb("wq_hi", [P, KD, INNER], F32R)
            wq_lo = asb("wq_lo", [P, KD, INNER], F32R)
            wo_hi = asb("wo_hi", [P, INNER // P, D], F32R)
            wo_lo = asb("wo_lo", [P, INNER // P, D], F32R)
            k_hi = asb("k_hi", [P, H // 2, B, 2 * NKB], F32R)
            k_lo = asb("k_lo", [P, H // 2, B, 2 * NKB], F32R)
            vdiag = asb("vdiag", [P, B, H // HQ, VC])
            mv = asb("mv", [P, 2, 2, 2]); stat6 = asb("stat6", [P, 2, 2, 6])
            rstd = asb("rstd", [P, 2, 2]); vare = asb("vare", [P, 2, 2])
            xn = asb("xn", [P, 2, 2, D])
            xT_hi = asb("xT_hi", [P, KD, GT], F32R)
            xT_lo = asb("xT_lo", [P, KD, GT], F32R)
            with ExitStack() as early:
                wk = early.enter_context(nc.sbuf_tensor("wk", [CK, 2, INNER], F32))
                wq_raw = early.enter_context(nc.sbuf_tensor("wq_raw", [P, KD, INNER], F32))
            q_hi, q_lo = [None, None], [None, None]
            for n in (1, 0):
                q_hi[n] = asb(f"q_hi{n}", [P, H // 2, GT], F32R)
                q_lo[n] = asb(f"q_lo{n}", [P, H // 2, GT], F32R)
            before = asb("before", [P, P], BF16)
            ones = asb("ones", [P, P], BF16)
            neg_half = asb("neg_half", [P, 8])
            eps = asb("eps", [P, 8])
            tie_rank = asb("tie_rank", [P, TPI, E])
            region0 = asb("region0", [P, TPI, E])
            token_no = asb("token_no", [P, NT], I32)
            bo_b = asb("bo_b", [P, D]); gamma_b = asb("gamma_b", [P, D]); beta_b = asb("beta_b", [P, D])
            rw = asb("rw", [P, KD, E])
            x1 = asb("x1", [P, NT, D])
            base_cnt = asb("base_cnt", [P, E])
            nmax = asb("nmax", [P, 4, HQ])
            probs = [asb(f"probs{n}", [P, PW]) for n in range(4)]
            psum_row = asb("psum_row", [P, 2, H])
            rsum = asb("rsum", [P, H // 2])
            pT = [asb(f"pT{n}", [P, NBLK, P]) for n in range(2)]
            o_sb = asb("o_sb", [P, INNER])
            oT_hi = asb("oT_hi", [P, INNER // P, P], F32R)
            oT_lo = asb("oT_lo", [P, INNER // P, P], F32R)
            with ExitStack() as early:
                ctx_pad = early.enter_context(nc.sbuf_tensor("ctx_pad", [CK, B, 2, P + NKB + P], F32))
                wv = early.enter_context(nc.sbuf_tensor("wv", [CK, 2, INNER], F32))
                wo_raw = early.enter_context(nc.sbuf_tensor("wo_raw", [P, INNER // P, D], F32))
            stat_b = asb("stat_b", [P, 2, TPI, 6]); mv_b = asb("mv_b", [P, 2, TPI, 2])
            vare_b = asb("vare_b", [P, 2, TPI]); rstd_b = asb("rstd_b", [P, 2, TPI])
            xin = asb("xin", [P, TPI, D]); out0 = asb("out0", [P, TPI, D]); xf = asb("xf", [P, TPI, D])
            xfT = asb("xfT", [P, TPI * KD, P])
            lg = asb("lg", [P, TPI, E]); lmax = asb("lmax", [P, TPI]); lsh = asb("lsh", [P, TPI, E]); ex = asb("ex", [P, TPI, E])
            esum = asb("esum", [P, TPI]); erec = asb("erec", [P, TPI]); pr = [asb(f"pr{n}", [P, TPI, E]) for n in range(2)]
            gate = asb("gate", [P, 2, TPI]); pick1 = asb("pick1", [P, 2, TPI, E]); top = asb("top", [P, TPI, E]); topm = asb("topm", [P, TPI])
            chosen = asb("chosen", [P, TPI, E], BF16)
            pos = asb("pos", [P, TPI, E]); posm = asb("posm", [P, 2, TPI, E]); rowf = asb("rowf", [P, 2, TPI]); row = asb("row", [P, 2, TPI], U32)
            rows = asb("rows", [P, 2, TPI, RW])
            padf = asb("padf", [P, E]); pad = asb("pad", [P, E], U32); lane = asb("lane", [P, 1]); zrow = asb("zrow", [P, RW])
            cnt1 = asb("cnt1", [P, E]); cnti = asb("cnti", [P, E], I32); tiles = asb("tiles", [P, E]); key = asb("key", [P, E])
            rank_e = asb("rank_e", [P, E]); order_f = asb("order_f", [P, E]); start = asb("start", [P, E]); end = asb("end", [P, E])
            expert_no = asb("expert_no", [P, E]); ahead_of = asb("ahead_of", [P, E, E]); at_rank = asb("at_rank", [P, E, E])
            slot_no = asb("slot_no", [P, MT]); past = asb("past", [P, MT, E]); within = asb("within", [P, MT, E])
            rank_j = asb("rank_j", [P, MT]); row_j = asb("row_j", [P, MT]); none_left = asb("none_left", [P, MT])

            block = actx.enter_context(nc.Block())

            JOB_SLOT = {0: 0, 1: 1, 2: 2, 4: 3, 5: 4}
            JOB_BANK = [0, 1, 0, 0, 1]
            FIRST_BANK = [0, 1, 0, 1, 0]

            TURN, LOGIT, COUNT = 11, 12, 14
            LG0 = 2 * P

            def tile_at(i, n):
                k, r = divmod(n, TPI)
                return (r // 2) * (SEQ // P) + 2 * (i + k) + r % 2

            @block.sync
            def _(sp):
                for b in range(B):
                    sp.dma_start(ctx_pad[:, b, :, P:P + NKB], ctxT[b].rearrange("(c p) k -> p c k", p=CK)).then_inc(s["ctx_in"], 16)
                sp.dma_start(wk[:, :, :], Wk.rearrange("(c p) n -> p c n", p=CK)).then_inc(s["wk_in"], 16)
                for n in (0, 2, 1, 3):
                    sp.dma_start(x1[:, 4 * n:4 * n + 4, :], x.rearrange("b (t p) d -> p (b t) d", p=P)[:, 4 * n:4 * n + 4, :]).then_inc(s["x_in"][n], 16)
                    if n == 0:
                        sp.dma_start(wq_raw[:, :, :], Wq.rearrange("(c p) n -> p c n", p=P)).then_inc(s["wq_in"], 16)
                        sp.dma_start(wv[:, :, :], Wv.rearrange("(c p) n -> p c n", p=CK)).then_inc(s["wv_in"], 16)
                for dst, src in ((gx, g_x), (gf, g_f), (bo_b, bo), (gamma_b, gamma), (beta_b, beta)):
                    sp.dma_start(dst[:, :], src.partition_broadcast(P)).then_inc(s["small_in"], 16)
                sp.dma_start(rw[:, :, :], rwT.rearrange("(c p) e -> p c e", p=P)).then_inc(s["small_in"], 16)
                sp.dma_start(wo_raw[:, :, :], Wo.rearrange("(c p) n -> p c n", p=P)).then_inc(s["wo_in"], 16)
                sp.wait_ge(s["zero"], 1)
                sp.dma_start(queue[DUMMY:DUMMY + P, :], zrow[:, :]).then_inc(s["zero_q"], 16)
                sp.dma_start(out[N:N + P, :], zrow[:, 0:D]).then_inc(s["zero_q"], 16)
                with sp.Fori(0, NI) as i:
                    sp.wait_ge(s["out0"], i + 1)
                    for b in range(B):
                        dst = out[bass.ds((b * (SEQ // P) + 2 * i) * P, 2 * P), :].rearrange("(t p) d -> p t d", p=P)
                        sp.dma_start(dst, out0[:, 2 * b:2 * b + 2, :]).then_inc(s["out0_q"], 16)
                sp.wait_ge(s["out0_q"], 32 * NI)
                sp.wait_ge(s["zero_q"], 32)
                sp.wait_ge(s["order"], 1)
                sp.wait_ge(s["pos_ps"], NI)
                for rank in range(2):
                    if rank > 0:
                        sp.wait_ge(s["w_in"], 32 * rank)
                    load_weights(sp, rank)

            @block.gpsimd
            def _(pool):
                nc.gpsimd.memset(ctx_pad[:, :, :, 0:P], 0.0)
                nc.gpsimd.memset(ctx_pad[:, :, :, P + NKB:], 0.0).then_inc(s["const"], 1)
                nc.gpsimd.memset(ident[:, :], 0.0)
                nc.gpsimd.memset(before[:, :], 1.0)
                nc.gpsimd.memset(ones[:, :], 1.0)
                nc.gpsimd.memset(neg_half[:, :], -0.5)
                nc.gpsimd.memset(eps[:, :], LN_EPS)
                nc.gpsimd.memset(base_cnt[:, :], 0.0)
                nc.gpsimd.iota(token_no[:, :], [[P, NT]], base=0, channel_multiplier=1)
                nc.gpsimd.iota(tie_rank[:, :, :], [[0, TPI], [-1, E]], base=E, channel_multiplier=0, allow_small_or_imprecise_dtypes=True)
                nc.gpsimd.iota(region0[:, :, :], [[0, TPI], [REG, E]], base=0, channel_multiplier=0, allow_small_or_imprecise_dtypes=True)
                nc.gpsimd.drain()
                nc.gpsimd.affine_select(out=ident[:, :], in_=ident[:, :], compare_op=ALU.not_equal, fill=1.0,
                                        base=0, pattern=[[-1, P]], channel_multiplier=1)
                nc.gpsimd.affine_select(out=before[:, :], in_=before[:, :], compare_op=ALU.is_gt, fill=0.0,
                                        base=0, pattern=[[1, P]], channel_multiplier=-1).then_inc(s["const"], 1)

                nc.gpsimd.iota(lane[:, :], [[0, 1]], base=0, channel_multiplier=1, allow_small_or_imprecise_dtypes=True)
                nc.gpsimd.iota(slot_no[:, :], [[1, MT]], base=0, channel_multiplier=0, allow_small_or_imprecise_dtypes=True)
                nc.gpsimd.iota(expert_no[:, :], [[1, E]], base=0, channel_multiplier=0, allow_small_or_imprecise_dtypes=True)

                def rstd_step(i, par):
                    g = GPI * i + par
                    pool.wait_ge(s["xstat"], g + 1)
                    nc.gpsimd.tensor_tensor(vare[:, par, :], mv[:, par, :, 1], eps[:, 0:2], ALU.add)
                    nc.gpsimd.drain()
                    nc.gpsimd.tensor_tensor(rstd[:, par, :], vare[:, par, :], neg_half[:, 0:2], ALU.pow).then_inc(s["xrstd"], 1)

                rstd_step(0, 0)
                rstd_step(0, 1)
                pool.wait_ge(s["wq_in"], 16)
                for c in range(KD):
                    nc.gpsimd.tensor_copy(wq_hi[:, c, :], wq_raw[:, c, :]).then_inc(s["wq_hi"], 1)
                    pool.wait_ge(s["wq_hi"], c + 1)
                    nc.gpsimd.tensor_tensor(wq_lo[:, c, :], wq_raw[:, c, :], wq_hi[:, c, :].bitcast(F32), ALU.subtract).then_inc(s["wq_lo"], 1)
                pool.wait_ge(s["tanh"], 1)
                nc.gpsimd.tensor_scalar(bo_b[:, :], bo_b[:, :], tgx[:, 0:1], None, ALU.mult)
                nc.gpsimd.drain()

                def add_bias(i, gl):
                    pool.wait_ge(s["xn"], GPI * i + gl + 1)
                    for j in range(2):
                        tile = pick(x1, tile_at(i, 2 * gl + j))
                        last = nc.gpsimd.tensor_tensor(tile, tile, bo_b[:, :], ALU.add)
                    last.then_inc(s["xres"], 1)

                add_bias(0, 0)
                add_bias(0, 1)
                pool.wait_ge(s["wo_in"], 16)
                for c in range(4):
                    part = slice(2 * c, 2 * c + 2)
                    nc.gpsimd.tensor_copy(wo_hi[:, part, :], wo_raw[:, part, :]).then_inc(s["wo_split"], 1)
                    pool.wait_ge(s["wo_split"], 2 * c + 1)
                    nc.gpsimd.tensor_tensor(wo_lo[:, part, :], wo_raw[:, part, :], wo_hi[:, part, :].bitcast(F32), ALU.subtract).then_inc(s["wo_split"], 1)

                def route_rstd(i, k):
                    pool.wait_ge(s[("stat1", "stat2")[k]], i)
                    nc.gpsimd.tensor_tensor(vare_b[:, k, :], mv_b[:, k, :, 1], eps[:, 0:TPI], ALU.add)
                    nc.gpsimd.drain()
                    nc.gpsimd.tensor_tensor(rstd_b[:, k, :], vare_b[:, k, :], neg_half[:, 0:TPI], ALU.pow).then_inc(s[("rs1", "rs2")[k]], 1)

                def gain_and_offset(i):
                    pool.wait_ge(s["xf0"], i)
                    nc.gpsimd.tensor_tensor(xf[:, :, :], xf[:, :, :], gamma_b[:, :].unsqueeze(1).to_broadcast([P, TPI, D]), ALU.mult)
                    nc.gpsimd.drain()
                    nc.gpsimd.tensor_tensor(xf[:, :, :], xf[:, :, :], beta_b[:, :].unsqueeze(1).to_broadcast([P, TPI, D]), ALU.add).then_inc(s["xf"], 1)

                def queue_rows(i):
                    pool.wait_ge(s["row_sb"], i)
                    at_least(pool, s["rows_q"], 16 * 2 * TPI * (i - 1))
                    for k in range(2):
                        for j in range(TPI):
                            if k == 0 and j == 0:
                                nc.gpsimd.tensor_tensor(rows[:, 0, 0, 0:D], xf[:, 0, :], gate[:, 0, 0:1].to_broadcast([P, D]), ALU.mult)
                                continue
                            nc.gpsimd.tensor_scalar(rows[:, k, j, 0:D], xf[:, j, :], gate[:, k, j:j + 1], None, ALU.mult)
                        of_batch = token_no[:, :].rearrange("p (b t) -> p b t", b=B)
                        first = 2 * (i - 1)
                        of_batch = of_batch[:, :, first:first + 2] if isinstance(i, int) else of_batch[:, :, bass.ds(first, 2)]
                        nc.gpsimd.tensor_copy(rows[:, k, :, D:RW].bitcast(I32).rearrange("p (b t) o -> p b (t o)", b=B), of_batch)
                    nc.gpsimd.drain()
                    for k in range(2):
                        for j in range(TPI):
                            nc.gpsimd.indirect_dma_start(queue[:, :], bass.IndirectOffsetOnAxis(row[:, k, j:j + 1], 0),
                                                         rows[:, k, j, :], None).then_inc(s["rows_q"], 16)

                def body(i, more=True):
                    if more:
                        rstd_step(i + 1, 0)
                    if not (isinstance(i, int) and i == 0):
                        route_rstd(i, 0)
                    if more:
                        add_bias(i + 1, 0)
                    if not (isinstance(i, int) and i == 0):
                        route_rstd(i, 1)
                        gain_and_offset(i)
                    if more:
                        rstd_step(i + 1, 1)
                        add_bias(i + 1, 1)
                    if not (isinstance(i, int) and i == 0):
                        queue_rows(i)

                body(0)
                pool.wait_ge(s["vdone"], B * len(pieces) // 2)
                nc.gpsimd.drain()
                nc.gpsimd.memset(zrow[:, 0:D], 0.0)
                nc.gpsimd.iota(zrow[:, D:RW].bitcast(I32), [[0, 1]], base=N, channel_multiplier=1).then_inc(s["zero"], 1)
                with pool.Fori(1, NI - 1) as i:
                    body(i)
                body(NI - 1, more=False)
                route_rstd(NI, 0)
                route_rstd(NI, 1)
                gain_and_offset(NI)
                queue_rows(NI)
                pool.wait_ge(s["pads"], 1)
                for e in range(E):
                    nc.gpsimd.indirect_dma_start(queue[:, :], bass.IndirectOffsetOnAxis(pad[:, e:e + 1], 0),
                                                 zrow[:, :], None).then_inc(s["rows_q"], 16)
                pool.wait_ge(s["rows_q"], 16 * (2 * NT + E))

            @block.tensor
            def _(pe):
                pe.wait_ge(s["ctx_in"], 32)
                pe.wait_ge(s["wk_in"], 16)
                for m in range(H // 2):
                    if m >= 4:
                        pe.wait_ge(s["k_lo"], m - 3)
                    for c in range(2):
                        last = nc.tensor.matmul(bank[m % 4][:, 0:B * NKB].rearrange("p (b k) -> p b k", b=B),
                                                wk[:, c, m * P:(m + 1) * P], ctx_pad[:, :, c, P:P + NKB],
                                                start=(c == 0), stop=(c == 1))
                    last.then_inc(s["kp"], 1)

                def group_job(g, par, k, banks, free):
                    at = M_BANK[banks[k]]
                    free()
                    if k == 0:
                        pe.wait_ge(s["xn"], g + 1)
                        if isinstance(g, int) and g == 0:
                            pe.wait_ge(s["const"], 2)
                        for j in range(2):
                            for c in range(KD):
                                last = nc.tensor.transpose(at[:, (2 * j + c) * P:(2 * j + c + 1) * P],
                                                           xn[:, par, j, c * P:(c + 1) * P], ident[:, :])
                    else:
                        if k == 1:
                            pe.wait_ge(s["proj_sb"][0], g + 1)
                        for m in range(2):
                            pair = 2 * (k - 1) + m
                            cols = slice(pair * P, (pair + 1) * P)
                            n = 0
                            for c in range(KD):
                                for w, v in ((wq_hi, xT_hi), (wq_lo, xT_hi), (wq_hi, xT_lo)):
                                    last = nc.tensor.matmul(at[:, m * GT:(m + 1) * GT], w[:, c, cols], v[:, c, :],
                                                            start=(n == 0), stop=(n == 5))
                                    n += 1
                    last.then_inc(s["proj"][k], 1)

                def scores(i, u):
                    par, w = (u // 8) % 2, u % 8
                    for hf in range(2):
                        at_least(pe, s["exp"][hf], UPI * i + u)
                        if w < UPT and hf == 0:
                            pe.wait_ge(s["proj_sb"][w + 1], GPI * i + u // 8 + 1)
                        pair = (u % UPT) * 2 + hf
                        tok = ((u // UPT) % 2) * P
                        n = 0
                        for q, k in ((q_hi, k_hi), (q_hi, k_lo), (q_lo, k_hi)):
                            last = nc.tensor.matmul(S_BANK[hf][:, 0:2 * NKB], q[par][:, pair, tok:tok + P], k[:, pair, par, :],
                                                    start=(n == 0), stop=(n == 2))
                            n += 1
                        last.then_inc(s["scores"][hf], 1)
                        yield

                def transpose_probs(i, u):
                    U = UPI * i + u
                    pe.wait_ge(s["exp"][1], U + 1)
                    at_least(pe, s["ptA_sb"], U)
                    at_least(pe, s["ptB_sb"], U)
                    for b in range(NBLK):
                        rows = P if b < NBLK - 1 else LASTB
                        dst = (TA if b < 3 else TB)[0:rows, (b % 3) * P:(b % 3 + 1) * P]
                        last = nc.tensor.transpose(dst, probs[u % 4][:, b * P:b * P + rows], ident[:, :])
                        if b == 2:
                            last.then_inc(s["ptA"], 1)
                    last.then_inc(s["ptB"], 1)

                def attend(i, u, waits=False):
                    U = UPI * i + u
                    batch = (u // 8) % 2
                    if waits:
                        pe.wait_ge(s["ptA_sb"], U + 1)
                        pe.wait_ge(s["ptB_sb"], U + 1)
                    if u % 2 == 0:
                        at_least(pe, s["ot_sb"][(u % UPT) // 2], TPI * i + u // UPT)
                    at = O_BANK[(u % UPT) // 2]
                    col0 = (u % 2) * HQ * DH
                    g = u % UPT
                    for b in range(NBLK):
                        rows = P if b < NBLK - 1 else LASTB
                        ks = blk_cols[b]
                        j0 = pieces[ks[0]][1]
                        n = len(ks) * DH
                        v = vdiag[0:rows, batch, g, ks[0] * DH:ks[0] * DH + n]
                        last = nc.tensor.matmul(at[:, col0 + j0 * DH:col0 + j0 * DH + n], pT[u % 2][0:rows, b, :],
                                                v, start=(b == 0), stop=(b == NBLK - 1), skip_group_check=True)
                    last.then_inc(s["pv"], 1)

                def transpose_out(i, u):
                    half = (u % UPT) // 2
                    pe.wait_ge(s["o_sb"][half], TPI * i + u // UPT)
                    for c in range(4):
                        last = nc.tensor.transpose(O_BANK[half][:, c * P:(c + 1) * P],
                                                   o_sb[:, (4 * half + c) * P:(4 * half + c + 1) * P], ident[:, :])
                    last.then_inc(s["ot_ps"][half], 1)

                def project_out(i, u):
                    for half in range(2):
                        pe.wait_ge(s["ot_sb"][half], TPI * i + u // UPT)
                    if isinstance(i, int) and TPI * i + u // UPT == 1:
                        pe.wait_ge(s["wo_split"], 8)
                    n, most = 0, 3 * INNER // P
                    for c in range(INNER // P):
                        for o, w in ((oT_hi, wo_hi), (oT_lo, wo_hi), (oT_hi, wo_lo)):
                            last = nc.tensor.matmul(M_BANK[1][:, 0:D], o[:, c, :], w[:, c, :], start=(n == 0), stop=(n == most - 1))
                            n += 1
                    last.then_inc(s["y"], 1)

                def turn_features(i):
                    pe.wait_ge(s["xf"], i)
                    for m, at in enumerate((TA, TB)):
                        for a in range(4):
                            j, c = 2 * m + a // 2, a % 2
                            last = nc.tensor.transpose(at[:, a * P:(a + 1) * P], xf[:, j, c * P:(c + 1) * P], ident[:, :])
                        last.then_inc(s["xfT_ps"], 1)

                def router_logits(i):
                    for m in range(2):
                        pe.wait_ge(s["xfT_sb"][m], i)
                    for j in range(TPI):
                        for c in range(KD):
                            last = nc.tensor.matmul(TB[:, LG0 + j * E:LG0 + (j + 1) * E], xfT[:, j * KD + c, :], rw[:, c, :],
                                                    start=(c == 0), stop=(c == KD - 1))
                    last.then_inc(s["logits"], 1)

                def rows_before(i):
                    pe.wait_ge(s["chosen"], i)
                    flat = chosen[:, :, :].rearrange("p t e -> p (t e)")
                    nc.tensor.matmul(TB[:, LG0:LG0 + TPI * E], before[:, :], flat, start=True, stop=False, skip_group_check=True)
                    for j in range(TPI - 1):
                        for jj in range(j + 1, TPI):
                            nc.tensor.matmul(TB[:, LG0 + jj * E:LG0 + (jj + 1) * E], ones[:, :], chosen[:, j, :],
                                             start=False, stop=(jj == j + 1), skip_group_check=True)
                    for j in range(TPI):
                        last = nc.tensor.matmul(TB[:, LG0 + TPI * E:LG0 + (TPI + 1) * E], ones[:, :], chosen[:, j, :],
                                                start=False, stop=(j == TPI - 1), skip_group_check=True)
                    last.then_inc(s["pos_ps"], 1)

                def route_step(i, u):
                    if u in (TURN, LOGIT, COUNT):
                        pe.wait_ge(s["ptB_sb"], UPI * i + u + 1)
                    if u == TURN:
                        pe.wait_ge(s["ptA_sb"], UPI * i + u + 1)
                        turn_features(i)
                    if u == LOGIT:
                        router_logits(i)
                    if u == COUNT:
                        rows_before(i)

                def slot(i, u):
                    first = isinstance(i, int) and i == 0
                    last = isinstance(i, int) and i == NI - 1
                    ahead = scores(i, u + 2) if not (last and u + 2 >= UPI) else iter(())
                    next(ahead, None)
                    if not first and u == TURN + 1:
                        for m in range(2):
                            pe.wait_ge(s["xfT_sb"][m], i)
                    if not first and u == LOGIT + 1:
                        pe.wait_ge(s["lg_read"], i)
                    if not first and u == COUNT + 1:
                        pe.wait_ge(s["row_sb"], i)
                    transpose_probs(i, u)
                    if u % 2 == 0 and not (first and u < UPT):
                        transpose_out(i, u)
                    next(ahead, None)
                    w, g = u % 8, GPI * i + u // 8 + 1
                    par = (u // 8 + 1) % 2
                    if w in JOB_SLOT and not (last and u >= 8):
                        k = JOB_SLOT[w]

                        def free():
                            if k == 0:
                                pe.wait_ge(s["proj_sb"][3], g)
                            elif k in (1, 4):
                                at_least(pe, s["y_sb"], TPI * i + u // UPT - 1)
                            else:
                                pe.wait_ge(s["proj_sb"][k - 1 if k == 3 else 0], g + 1)
                        group_job(g, par, k, JOB_BANK, free)
                    if w % UPT == UPT - 1 and not (first and u < UPT):
                        if not (last and u >= 8):
                            pe.wait_ge(s["proj_sb"][1 if w == 3 else 4], g + 1)
                        at_least(pe, s["y_sb"], TPI * i + u // UPT - 1)
                        project_out(i, u)
                    if not first:
                        route_step(i, u)
                    if not (first and u == 0):
                        attend(i, u - 1)

                pe.wait_ge(s["wq_lo"], KD)
                for k in range(5):
                    group_job(0, 0, k, FIRST_BANK, lambda: k >= 2 and pe.wait_ge(s["proj_sb"][k - 2], 1))
                pe.wait_ge(s["k_zero"], 1)
                pe.wait_ge(s["k_lo"], H // 2)
                for u in range(2):
                    for _ in scores(0, u):
                        pass
                pe.wait_ge(s["const"], 1)
                pe.wait_ge(s["wv_in"], 16)
                n = 0
                for b in range(B):
                    for m in range(len(pieces) // 2):
                        at = bank[2 + n % 4]
                        if n >= 4:
                            pe.wait_ge(s["vdone"], n - 3)
                        for a in range(2):
                            blk, j = pieces[2 * m + a]
                            lo = P + blk * P - j * NKB
                            for c in range(2):
                                last = nc.tensor.matmul(at[:, :].rearrange("p (g a d) -> p g a d", g=H // HQ, a=2)[:, :, a, :],
                                                        ctx_pad[:, b, c, lo:lo + P],
                                                        wv[:, c, :].rearrange("p (g j d) -> p g j d", j=HQ, d=DH)[:, :, j, :],
                                                        start=(c == 0 and a == 0), stop=(c == 1), skip_group_check=True)
                        last.then_inc(s["vp"], 1)
                        n += 1
                pe.wait_ge(s["vdone"], n + 1)
                for u in range(UPI):
                    slot(0, u)
                with pe.Fori(1, NI - 1) as i:
                    for u in range(UPI):
                        slot(i, u)
                for u in range(UPI):
                    slot(NI - 1, u)
                attend(NI, -1, waits=True)
                transpose_out(NI, 0)
                transpose_out(NI, 2)
                at_least(pe, s["y_sb"], NT - 1)
                project_out(NI, 3)
                turn_features(NI)
                router_logits(NI)
                rows_before(NI)

            @block.scalar
            def _(act):
                act.wait_ge(s["small_in"], 96)
                nc.scalar.activation(tgx[:, :], gx[:, :], ACT.Tanh)
                nc.scalar.activation(tgf[:, :], gf[:, :], ACT.Tanh).then_inc(s["tanh"], 1)
                for m in range(H // 2):
                    act.wait_ge(s["kp"], m + 1)
                    for a in range(2):
                        half = slice(a * DH, (a + 1) * DH)
                        last = nc.scalar.activation(k_hi[half, m, :, a * NKB:(a + 1) * NKB],
                                                    bank[m % 4][half, 0:B * NKB].rearrange("p (b k) -> p b k", b=B), ACT.Copy, scale=SCALE)
                    last.then_inc(s["k_hi"], 1)

                def high_part(g, k, banks, par):
                    act.wait_ge(s["proj"][k], g + 1)
                    at = M_BANK[banks[k]]
                    if k == 0:
                        last = nc.scalar.copy(xT_hi[:, :, :].rearrange("p c (j t) -> p j c t", j=2),
                                              at[:, :].rearrange("p (j c t) -> p j c t", j=2, c=KD))
                    else:
                        last = nc.scalar.copy(q_hi[par][:, 2 * k - 2:2 * k, :].rearrange("p m t -> p (m t)"), at[:, :])
                    last.then_inc(s["proj_hi"][k], 1)

                def exps(i, u):
                    for hf in range(2):
                        act.wait_ge(s["smax"][hf], UPI * i + u + 1)
                        for m in range(2):
                            j = 2 * hf + m
                            h = (u % UPT) * HQ + j
                            last = nc.scalar.activation(probs[u % 4][:, j * NKB:(j + 1) * NKB], S_BANK[hf][:, m * NKB:(m + 1) * NKB],
                                                        ACT.Exp, bias=nmax[:, u % 4, j:j + 1], scale=1.0,
                                                        accum_out=psum_row[:, (u // UPT) % 2, h:h + 1])
                        last.then_inc(s["exp"][hf], 1)
                        yield

                def transposed_out(i, u):
                    half = (u % UPT) // 2
                    act.wait_ge(s["ot_ps"][half], TPI * i + u // UPT)
                    nc.scalar.copy(oT_hi[:, 4 * half:4 * half + 4, :].rearrange("p c t -> p (c t)"), O_BANK[half][:, :]).then_inc(s["ot_hi"][half], 1)

                def turned_features(i):
                    act.wait_ge(s["xfT_ps"], 2 * i - 1)
                    nc.scalar.copy(xfT[:, 0:4, :].rearrange("p c t -> p (c t)"), TA[:, :]).then_inc(s["xfT_sb"][0], 1)

                def router_exp(i):
                    act.wait_ge(s["lsh"], i)
                    nc.scalar.activation(ex[:, :, :], lsh[:, :, :], ACT.Exp).then_inc(s["ex"], 1)

                def slot(i, u):
                    first = isinstance(i, int) and i == 0
                    last = isinstance(i, int) and i == NI - 1
                    if not first and u == TURN + 1:
                        turned_features(i)
                    if not first and u == LOGIT + 2:
                        router_exp(i)
                    ahead = exps(i, u + 2) if not (last and u + 2 >= UPI) else iter(())
                    next(ahead, None)
                    act.wait_ge(s["ptA"], UPI * i + u + 1)
                    nc.scalar.copy(pT[u % 2][:, 0:3, :].rearrange("p b t -> p (b t)"), TA[:, 0:3 * P]).then_inc(s["ptA_sb"], 1)
                    if u % 2 == 0 and not (first and u < UPT):
                        transposed_out(i, u)
                    next(ahead, None)
                    w, g = u % 8, GPI * i + u // 8 + 1
                    if w in JOB_SLOT and not (last and u >= 8):
                        high_part(g, JOB_SLOT[w], JOB_BANK, (u // 8 + 1) % 2)

                for k in range(5):
                    high_part(0, k, FIRST_BANK, 0)
                for u in range(2):
                    for _ in exps(0, u):
                        pass
                for u in range(UPI):
                    slot(0, u)
                with act.Fori(1, NI - 1) as i:
                    for u in range(UPI):
                        slot(i, u)
                for u in range(UPI):
                    slot(NI - 1, u)
                transposed_out(NI, 0)
                transposed_out(NI, 2)
                turned_features(NI)
                router_exp(NI)
                for n in range(len(CHUNKS)):
                    split_high(act, 0, n)

            @block.vector
            def _(dve):
                v = nc.vector

                def then(ins):
                    v.drain()
                    return ins

                for k in (k_hi, k_lo):
                    nc.vector.memset(k[DH:P, :, :, 0:NKB].bitcast(F32), 0.0)
                    last = nc.vector.memset(k[0:DH, :, :, NKB:2 * NKB].bitcast(F32), 0.0)
                last.then_inc(s["k_zero"], 1)

                def token_stats(i, gl):
                    par = gl % 2
                    for j in range(2):
                        nc.vector.bn_stats(stat6[:, par, j, :], pick(x1, tile_at(i, 2 * gl + j)))
                    nc.vector.drain()
                    for j in range(2):
                        last = nc.vector.bn_aggr(mv[:, par, j, :], stat6[:, par, j, :])
                    last.then_inc(s["xstat"], 1)

                def normalise(i, gl):
                    par = gl % 2
                    dve.wait_ge(s["xrstd"], GPI * i + gl + 1)
                    for j in range(2):
                        last = nc.vector.tensor_scalar(xn[:, par, j, :], pick(x1, tile_at(i, 2 * gl + j)), mv[:, par, j, 0:1], rstd[:, par, j:j + 1],
                                                       ALU.subtract, ALU.mult)
                    last.then_inc(s["xn"], 1)

                def low_part(g, k, banks, par):
                    dve.wait_ge(s["proj_hi"][k], g + 1)
                    at = M_BANK[banks[k]]
                    if k == 0:
                        last = nc.vector.tensor_tensor(xT_lo[:, :, :].rearrange("p c (j t) -> p j c t", j=2),
                                                       at[:, :].rearrange("p (j c t) -> p j c t", j=2, c=KD),
                                                       xT_hi[:, :, :].rearrange("p c (j t) -> p j c t", j=2).bitcast(F32), ALU.subtract)
                    else:
                        queries = slice(2 * k - 2, 2 * k)
                        last = nc.vector.tensor_tensor(q_lo[par][:, queries, :].rearrange("p m t -> p (m t)"), at[:, :],
                                                       q_hi[par][:, queries, :].rearrange("p m t -> p (m t)").bitcast(F32), ALU.subtract)
                    last.then_inc(s["proj_sb"][k], 1)

                def maxima(i, u):
                    for hf in range(2):
                        dve.wait_ge(s["scores"][hf], UPI * i + u + 1)
                        nc.vector.tensor_reduce(nmax[:, u % 4, 2 * hf:2 * hf + 2], S_BANK[hf][:, 0:2 * NKB].rearrange("p (m k) -> p m k", m=2),
                                                AX_X, ALU.max, negate=True).then_inc(s["smax"][hf], 1)
                        yield

                def scale_out(i, u):
                    half = (u % UPT) // 2
                    U = UPI * i + u
                    dve.wait_ge(s["pv"], U + 1)
                    nc.vector.reciprocal(rsum[:, :], psum_row[:, (u // UPT) % 2, 8 * half:8 * half + 8])
                    nc.vector.drain()
                    nc.vector.tensor_tensor(o_sb[:, half * 512:(half + 1) * 512].rearrange("p (h d) -> p h d", h=8),
                                            O_BANK[half][:, :].rearrange("p (h d) -> p h d", h=8),
                                            rsum[:, :].unsqueeze(2).to_broadcast([P, 8, DH]), ALU.mult).then_inc(s["o_sb"][half], 1)

                def residual_group(i, u):
                    return GPI * i + (u // UPT - 1) // 2

                def transposed_out(i, u):
                    half = (u % UPT) // 2
                    part = slice(4 * half, 4 * half + 4)
                    dve.wait_ge(s["ot_hi"][half], TPI * i + u // UPT)
                    nc.vector.tensor_tensor(oT_lo[:, part, :].rearrange("p c t -> p (c t)"), O_BANK[half][:, :],
                                            oT_hi[:, part, :].rearrange("p c t -> p (c t)").bitcast(F32), ALU.subtract).then_inc(s["ot_sb"][half], 1)

                def add_residual(i, u):
                    dve.wait_ge(s["y"], TPI * i + u // UPT)
                    dve.wait_ge(s["xres"], residual_group(i, u) + 1)
                    tile = pick(x1, tile_at(i, u // UPT - 1))
                    nc.vector.scalar_tensor_tensor(tile, M_BANK[1][:, 0:D], tgx[:, 0:1], tile, ALU.mult, ALU.add).then_inc(s["y_sb"], 1)

                def over_experts(ap):
                    return ap.unsqueeze(2).to_broadcast([P, TPI, E])

                def four(i):
                    first = 2 * (i - 1)
                    two = slice(first, first + 2) if isinstance(i, int) else bass.ds(first, 2)
                    return x1[:, :, :].rearrange("p (b t) d -> p b t d", b=B)[:, :, two, :]

                def halves(buf):
                    return buf.rearrange("p (b t) d -> p b t d", b=B)

                def block_stats(i, j):
                    v.drain()
                    v.bn_stats(stat_b[:, 0, j, :], pick(x1, tile_at(i, j - TPI)))
                    v.drain()
                    last = v.bn_aggr(mv_b[:, 0, j, :], stat_b[:, 0, j, :])
                    if j == TPI - 1:
                        last.then_inc(s["stat1"], 1)

                def first_norm(i):
                    dve.wait_ge(s["rs1"], i)
                    for j in range(TPI):
                        v.tensor_scalar(xin[:, j, :], pick(x1, tile_at(i, j - TPI)), mv_b[:, 0, j, 0:1], rstd_b[:, 0, j:j + 1], ALU.subtract, ALU.mult)
                    v.drain()

                def norm_stats(i, js):
                    for j in js:
                        v.bn_stats(stat_b[:, 1, j, :], xin[:, j, :])
                    v.drain()
                    for j in js:
                        last = v.bn_aggr(mv_b[:, 1, j, :], stat_b[:, 1, j, :])
                    if TPI - 1 in js:
                        last.then_inc(s["stat2"], 1)

                def start_output(i):
                    at_least(dve, s["out0_q"], 32 * (i - 1))
                    v.scalar_tensor_tensor(halves(out0[:, :, :]), halves(xin[:, :, :]), tgf[:, 0:1], four(i), ALU.mult, ALU.add).then_inc(s["out0"], 1)

                def second_norm(i):
                    dve.wait_ge(s["rs2"], i)
                    at_least(dve, s["rows_q"], 16 * 2 * TPI * (i - 1))
                    for j in range(TPI):
                        last = v.tensor_scalar(xf[:, j, :], xin[:, j, :], mv_b[:, 1, j, 0:1], rstd_b[:, 1, j:j + 1], ALU.subtract, ALU.mult)
                    last.then_inc(s["xf0"], 1)

                def turned_features(i):
                    dve.wait_ge(s["xfT_ps"], 2 * i)
                    v.tensor_copy(xfT[:, 4:8, :].rearrange("p c t -> p (c t)"), TB[:, :]).then_inc(s["xfT_sb"][1], 1)

                def shifted_logits(i):
                    dve.wait_ge(s["logits"], i)
                    then(v.tensor_scalar(lg[:, :, :], TB[:, LG0:LG0 + TPI * E].rearrange("p (t e) -> p t e", t=TPI), CLAMP, -CLAMP, ALU.min, ALU.max).then_inc(s["lg_read"], 1))
                    then(v.tensor_reduce(lmax[:, :], lg[:, :, :], AX_X, ALU.max))
                    v.tensor_tensor(lsh[:, :, :], lg[:, :, :], over_experts(lmax[:, :]), ALU.subtract).then_inc(s["lsh"], 1)

                def router_probs(i):
                    dve.wait_ge(s["ex"], i)
                    then(v.tensor_reduce(esum[:, :], ex[:, :, :], AX_X, ALU.add))
                    then(v.tensor_scalar(esum[:, :], esum[:, :], ROUTER_EPS, None, ALU.add))
                    then(v.reciprocal(erec[:, :], esum[:, :]))
                    then(v.tensor_tensor(pr[0][:, :, :], ex[:, :, :], over_experts(erec[:, :]), ALU.mult))
                    then(v.tensor_scalar(pr[0][:, :, :], pr[0][:, :, :], ROUTER_EPS, 1.0, ALU.max, ALU.min))

                def choose(i, which):
                    for k in (which,):
                        then(v.tensor_reduce(gate[:, k, :], pr[k][:, :, :], AX_X, ALU.max))
                        then(v.tensor_tensor(top[:, :, :], pr[k][:, :, :], over_experts(gate[:, k, :]), ALU.is_ge))
                        then(v.tensor_tensor(top[:, :, :], top[:, :, :], tie_rank[:, :, :], ALU.mult))
                        then(v.tensor_reduce(topm[:, :], top[:, :, :], AX_X, ALU.max))
                        then(v.tensor_tensor(pick1[:, k, :, :], top[:, :, :], over_experts(topm[:, :]), ALU.is_equal))
                        if k == 0:
                            then(v.scalar_tensor_tensor(pr[1][:, :, :], pick1[:, 0, :, :], -4.0, pr[0][:, :, :], ALU.mult, ALU.add))
                    if which == 1:
                        v.tensor_tensor(chosen[:, :, :], pick1[:, 0, :, :], pick1[:, 1, :, :], ALU.add).then_inc(s["chosen"], 1)

                def number_rows(i):
                    dve.wait_ge(s["pos_ps"], i)
                    then(v.tensor_tensor(pos[:, :, :], TB[:, LG0:LG0 + TPI * E].rearrange("p (t e) -> p t e", t=TPI),
                                         base_cnt[:, :].unsqueeze(1).to_broadcast([P, TPI, E]), ALU.add))
                    v.tensor_tensor(base_cnt[:, :], base_cnt[:, :], TB[:, LG0 + TPI * E:LG0 + (TPI + 1) * E], ALU.add)
                    then(v.tensor_tensor(pos[:, :, :], pos[:, :, :], region0[:, :, :], ALU.add))
                    then(v.tensor_tensor(posm[:, :, :, :], pick1[:, :, :, :], pos[:, :, :].unsqueeze(1).to_broadcast([P, 2, TPI, E]), ALU.mult))
                    then(v.tensor_reduce(rowf[:, :, :], posm[:, :, :, :], AX_X, ALU.add))
                    v.tensor_copy(row[:, :, :], rowf[:, :, :]).then_inc(s["row_sb"], 1)

                def route_step(i, u):
                    if u == 5:
                        first_norm(i)
                    if u in (6, 7):
                        norm_stats(i, (0, 1) if u == 6 else (2, 3))
                    if u == 8:
                        start_output(i)
                    if u == 9:
                        second_norm(i)

                def route_step_early(i, u):
                    if u == TURN + 1:
                        turned_features(i)
                    if u == LOGIT + 1:
                        shifted_logits(i)
                    if u == COUNT + 1:
                        number_rows(i)

                def route_step_late(i, u):
                    if u == LOGIT + 2:
                        router_probs(i)
                        choose(i, 0)
                        choose(i, 1)

                def slot(i, u):
                    first = isinstance(i, int) and i == 0
                    last = isinstance(i, int) and i == NI - 1
                    if not first:
                        route_step_early(i, u)
                    ahead = maxima(i, u + 2) if not (last and u + 2 >= UPI) else iter(())
                    next(ahead, None)
                    if u % 2 == 1 and not (first and u < 2):
                        scale_out(i, u - 2)
                    dve.wait_ge(s["ptB"], UPI * i + u + 1)
                    nc.vector.tensor_copy(pT[u % 2][:, 3:5, :].rearrange("p b t -> p (b t)"), TB[:, 0:2 * P]).then_inc(s["ptB_sb"], 1)
                    if u % 2 == 0 and not (first and u < UPT):
                        transposed_out(i, u)
                    next(ahead, None)
                    w, g = u % 8, GPI * i + u // 8 + 1
                    if w in JOB_SLOT and not (last and u >= 8):
                        low_part(g, JOB_SLOT[w], JOB_BANK, (u // 8 + 1) % 2)
                    if w % UPT == UPT - 1 and not (first and u < UPT):
                        add_residual(i, u)
                        if u == 3:
                            block_stats(i, TPI - 1)
                        else:
                            block_stats(i + 1, u // UPT - 1)
                    if w == 3 and not last:
                        token_stats(i + 1, u // 8)
                    if w == 6 and not last:
                        normalise(i + 1, u // 8)
                    if not first:
                        route_step(i, u)
                        route_step_late(i, u)

                for g in range(2):
                    dve.wait_ge(s["x_in"][2 * g], 16)
                    token_stats(0, g)
                    if g == 1:
                        normalise(0, 0)
                for m in range(H // 2):
                    dve.wait_ge(s["k_hi"], m + 1)
                    for a in range(2):
                        half, keys = slice(a * DH, (a + 1) * DH), slice(a * NKB, (a + 1) * NKB)
                        last = nc.vector.scalar_tensor_tensor(k_lo[half, m, :, keys], bank[m % 4][half, 0:B * NKB].rearrange("p (b k) -> p b k", b=B),
                                                              SCALE, k_hi[half, m, :, keys].bitcast(F32), ALU.mult, ALU.subtract)
                    last.then_inc(s["k_lo"], 1)
                normalise(0, 1)
                for k in range(5):
                    low_part(0, k, FIRST_BANK, 0)
                for u in range(2):
                    for _ in maxima(0, u):
                        pass
                n = 0
                for b in range(B):
                    for m in range(len(pieces) // 2):
                        dve.wait_ge(s["vp"], n + 1)
                        nc.vector.tensor_copy(vdiag[:, b, :, 2 * m * DH:(2 * m + 2) * DH],
                                              bank[2 + n % 4][:, :].rearrange("p (g c) -> p g c", g=H // HQ)).then_inc(s["vdone"], 1)
                        n += 1
                nc.vector.drain()
                nc.vector.memset(TB[96:P, P:2 * P], 0.0).then_inc(s["vdone"], 1)
                for n in range(4):
                    dve.wait_ge(s["x_in"][n], 16)
                for u in range(UPI):
                    slot(0, u)
                with dve.Fori(1, NI - 1) as i:
                    for u in range(UPI):
                        slot(i, u)
                for u in range(UPI):
                    slot(NI - 1, u)
                scale_out(NI, -1)
                for u in (0, 2):
                    transposed_out(NI, u)
                add_residual(NI, 3)
                block_stats(NI, 3)
                first_norm(NI)
                norm_stats(NI, range(TPI))
                second_norm(NI)
                start_output(NI)
                turned_features(NI)
                shifted_logits(NI)
                router_probs(NI)
                choose(NI, 0)
                choose(NI, 1)
                number_rows(NI)
                v.drain()
                dve.wait_ge(s["zero"], 1)
                then(v.tensor_tensor(padf[:, :], base_cnt[:, :], region0[:, 0, :], ALU.add))
                then(v.tensor_scalar(padf[:, :], padf[:, :], lane[:, 0:1], None, ALU.add))
                v.tensor_copy(pad[:, :], padf[:, :]).then_inc(s["pads"], 1)
                then(v.tensor_scalar(cnt1[:, :], base_cnt[:, :], float(P - 1), None, ALU.add))
                then(v.tensor_copy(cnti[:, :], cnt1[:, :]))
                then(v.tensor_scalar(cnti[:, :], cnti[:, :], P.bit_length() - 1, None, ALU.logical_shift_right))
                then(v.tensor_scalar(tiles[:, :], cnti[:, :], 1, None, ALU.max))
                then(v.scalar_tensor_tensor(key[:, :], tiles[:, :], float(E), expert_no[:, :], ALU.mult, ALU.subtract))
                by_expert = [P, E, E]
                then(v.tensor_tensor(ahead_of[:, :, :], key[:, :].unsqueeze(1).to_broadcast(by_expert), key[:, :].unsqueeze(2).to_broadcast(by_expert), ALU.is_gt))
                then(v.tensor_reduce(rank_e[:, :], ahead_of[:, :, :], AX_X, ALU.add))
                then(v.tensor_tensor(at_rank[:, :, :], expert_no[:, :].unsqueeze(2).to_broadcast(by_expert), rank_e[:, :].unsqueeze(1).to_broadcast(by_expert), ALU.is_equal))
                then(v.tensor_tensor(at_rank[:, :, :], at_rank[:, :, :], expert_no[:, :].unsqueeze(1).to_broadcast(by_expert), ALU.mult))
                then(v.tensor_reduce(order_f[:, :], at_rank[:, :, :], AX_X, ALU.add))
                v.tensor_copy(order[:, :], order_f[:, :]).then_inc(s["order"], 1)
                then(v.tensor_tensor(ahead_of[:, :, :], ahead_of[:, :, :], tiles[:, :].unsqueeze(1).to_broadcast(by_expert), ALU.mult))
                then(v.tensor_reduce(start[:, :], ahead_of[:, :, :], AX_X, ALU.add))
                then(v.tensor_tensor(end[:, :], start[:, :], tiles[:, :], ALU.add))
                by_slot = [P, MT, E]
                slots = slot_no[:, :].unsqueeze(2).to_broadcast(by_slot)
                v.tensor_tensor(past[:, :, :], slots, end[:, :].unsqueeze(1).to_broadcast(by_slot), ALU.is_ge)
                then(v.tensor_tensor(within[:, :, :], slots, start[:, :].unsqueeze(1).to_broadcast(by_slot), ALU.is_ge))
                v.tensor_reduce(rank_j[:, :], past[:, :, :], AX_X, ALU.add)
                then(v.tensor_tensor(within[:, :, :], within[:, :, :], past[:, :, :], ALU.subtract))
                then(v.scalar_tensor_tensor(start[:, :], expert_no[:, :], -float(REG // P), start[:, :], ALU.mult, ALU.add))
                then(v.tensor_tensor(past[:, :, :], slots, start[:, :].unsqueeze(1).to_broadcast(by_slot), ALU.subtract))
                then(v.tensor_tensor(past[:, :, :], past[:, :, :], within[:, :, :], ALU.mult))
                then(v.tensor_reduce(row_j[:, :], past[:, :, :], AX_X, ALU.add))
                then(v.tensor_scalar(none_left[:, :], rank_j[:, :], float(E), float(DUMMY // P), ALU.is_ge, ALU.mult))
                then(v.tensor_tensor(row_j[:, :], row_j[:, :], none_left[:, :], ALU.add))
                then(v.tensor_scalar(rank_j[:, :], rank_j[:, :], float(E - 1), None, ALU.min))
                v.tensor_copy(table[:, 0, :], rank_j[:, :])
                v.tensor_copy(table[:, 1, :], row_j[:, :])
                for n in range(len(CHUNKS)):
                    split_low(dve, 0, n)

        block = ctx.enter_context(nc.Block())

        @block.sync
        def _(sp):
            def load(i, p, free=True):
                j = RT * i + p
                r = sp.value_load(table[0:1, 1, bass.ds(j, 1)] if not isinstance(j, int) else table[0:1, 1, j:j + 1], min_val=0, max_val=DUMMY // P)
                if free:
                    sp.wait_ge(s["eT_ps"], j - 1)
                    sp.wait_ge(s["e_tok"], j - 1)
                sp.dma_start(xq[p % 2][:, :], queue[bass.ds(r * P, P), :]).then_inc(s["xq_in"][p % 2], 16)

            def slot(i, p):
                load(i + (p + 2) // RT, (p + 2) % RT)
                if p == 1:
                    sp.wait_ge(s["w_in"], 32 * (i + 2))
                    load_weights(sp, i + 2)

            load(0, 0, False)
            load(0, 1, False)
            for p in range(RT):
                slot(0, p)
            with sp.Fori(1, E - 2) as i:
                for p in range(RT):
                    slot(i, p)
            with sp.Fori(E - 2, LOOPS) as i:
                for p in range(RT):
                    load(i + (p + 2) // RT, (p + 2) % RT)
            for j in range(RT * LOOPS + 2, MT):
                load(*divmod(j, RT))

        @block.gpsimd
        def _(pool):
            def tokens(i, p):
                j = RT * i + p
                pool.wait_ge(s["xq_in"][p % 2], 16 * ((RT // 2) * i + p // 2 + 1))
                at_least(pool, s["e_idx"], j - 1)
                nc.gpsimd.tensor_tensor(tok[p % 2][:, :], xq[p % 2][:, D:RW].bitcast(U32), no_offset[:, :], ALU.add).then_inc(s["e_tok"], 1)

            def scatter_add(i, p):
                j = RT * i + p
                pool.wait_ge(s["e_ysb"], j + 1)
                pool.wait_ge(s["e_tok"], j + 1)
                at_least(pool, s["e_add"], 16 * j)
                nc.gpsimd.tensor_tensor(to_row[:, :], tok[p % 2][:, :], no_offset[:, :], ALU.add).then_inc(s["e_idx"], 1)
                nc.gpsimd.drain()
                nc.gpsimd.indirect_dma_start(out[:, :], bass.IndirectOffsetOnAxis(to_row[:, 0:1], 0), yq[p % 2][:, :], None,
                                             compute_op=ALU.add).then_inc(s["e_add"], 16)

            def slot(i, p):
                if not (isinstance(i, int) and RT * i + p + 1 >= MT):
                    tokens(i + (p + 1) // RT, (p + 1) % RT)
                scatter_add(i, p)

            nc.gpsimd.memset(no_offset[:, :], 0)
            nc.gpsimd.drain()
            tokens(0, 0)
            for p in range(RT):
                slot(0, p)
            with pool.Fori(1, LOOPS) as i:
                for p in range(RT):
                    slot(i, p)
            for j in range(RT * LOOPS, MT):
                slot(*divmod(j, RT))
            pool.wait_ge(s["e_add"], 16 * MT)

        @block.tensor
        def _(pe):
            def transpose_rows(i, p):
                j = RT * i + p
                pe.wait_ge(s["xq_in"][p % 2], 16 * ((RT // 2) * i + p // 2 + 1))
                at_least(pe, s["eT_lo"], j)
                for c in range(KD):
                    last = nc.tensor.transpose(XT_BANK[:, c * P:(c + 1) * P], xq[p % 2][:, c * P:(c + 1) * P], ident[:, :])
                last.then_inc(s["eT_ps"], 1)

            def rank_of(i, p):
                j = RT * i + p
                return pe.value_load(table[0:1, 0, bass.ds(j, 1)] if not isinstance(j, int) else table[0:1, 0, j:j + 1], min_val=0, max_val=E - 1)

            def weights(part, rank, col, n):
                return part[:, bass.ds(rank, 1), col:col + n].rearrange("p a f -> p (a f)")

            def up(i, p, rank, half, at, done, free):
                j = RT * i + p
                pe.wait_ge(s["eT_lo"], j + 1)
                at_least(pe, s[free], j - 1)
                n = 0
                for c in range(KD):
                    for rows, w in ((xqT_hi, gu_hi), (xqT_lo, gu_hi), (xqT_hi, gu_lo)):
                        last = nc.tensor.matmul(at[p % 2][:, :], rows[:, c, :], weights(w, rank, c * FF2 + half * FF, FF),
                                                start=(n == 0), stop=(n == 3 * KD - 1))
                        n += 1
                last.then_inc(s[done], 1)

            def transpose_hidden(i, p):
                j = RT * i + p
                pe.wait_ge(s["e_hid"], j + 1)
                at_least(pe, s["e_hT_lo"], j)
                for c in range(KF):
                    last = nc.tensor.transpose(HT_BANK[:, c * P:(c + 1) * P], hid[p % 2][:, c * P:(c + 1) * P], ident[:, :])
                last.then_inc(s["e_hT_ps"], 1)

            def down(i, p, rank):
                j = RT * i + p
                pe.wait_ge(s["e_hT_lo"], j + 1)
                at_least(pe, s["e_ysb"], j - 1)
                n = 0
                for c in range(KF):
                    for h, w in ((hidT_hi, dn_hi), (hidT_lo, dn_hi), (hidT_hi, dn_lo)):
                        last = nc.tensor.matmul(Y_BANK[p % 2][:, 0:D], h[:, c, :], weights(w, rank, c * D, D),
                                                start=(n == 0), stop=(n == 3 * KF - 1))
                        n += 1
                last.then_inc(s["e_y"], 1)

            def slot(i, p, behind=True, more=True, new_rank=True):
                rank = rank_of(i, p)
                tile_before = (i - 1, RT - 1) if p == 0 else (i, p - 1)
                if p == 0 and new_rank:
                    pe.wait_ge(s["w_lo"], len(CHUNKS) * (i + 1))
                if more:
                    transpose_rows(i + (p + 1) // RT, (p + 1) % RT)
                if behind:
                    transpose_hidden(*tile_before)
                up(i, p, rank, 0, G_BANK, "e_gate", "e_silu")
                up(i, p, rank, 1, U_BANK, "e_up", "e_hid")
                if behind:
                    down(*tile_before, rank_of(*tile_before))

            transpose_rows(0, 0)
            for p in range(RT):
                slot(0, p, behind=(p > 0))
            with pe.Fori(1, E) as i:
                for p in range(RT):
                    slot(i, p)
            with pe.Fori(E, LOOPS) as i:
                for p in range(RT):
                    slot(i, p, new_rank=False)
            for j in range(RT * LOOPS, MT):
                slot(*divmod(j, RT), new_rank=False, more=(j < MT - 1))
            last_tile = divmod(MT - 1, RT)
            transpose_hidden(*last_tile)
            down(*last_tile, rank_of(*last_tile))

        @block.scalar
        def _(act):
            def rows_T(i, p):
                j = RT * i + p
                act.wait_ge(s["eT_ps"], j + 1)
                at_least(act, s["e_up"], j)
                nc.scalar.copy(xqT_hi[:, :, :].rearrange("p c t -> p (c t)"), XT_BANK[:, 0:KD * P]).then_inc(s["eT_hi"], 1)

            def silu(i, p):
                j = RT * i + p
                act.wait_ge(s["e_gate"], j + 1)
                at_least(act, s["e_hT_ps"], j - 1)
                nc.scalar.activation(hid[p % 2][:, :], G_BANK[p % 2][:, :], ACT.Silu).then_inc(s["e_silu"], 1)

            def hidden_T(i, p):
                j = RT * i + p
                act.wait_ge(s["e_hT_ps"], j + 1)
                at_least(act, s["e_y"], j)
                nc.scalar.copy(hidT_hi[:, :, :].rearrange("p c t -> p (c t)"), HT_BANK[:, :]).then_inc(s["e_hT_hi"], 1)

            def scaled(i, p):
                j = RT * i + p
                act.wait_ge(s["e_y"], j + 1)
                at_least(act, s["e_add"], 16 * (j - 1))
                nc.scalar.activation(yq[p % 2][:, :], Y_BANK[p % 2][:, 0:D], ACT.Copy, scale=tgf[:, 0:1]).then_inc(s["e_ysb"], 1)

            def slot(i, p, chunks=(), behind=True, more=True):
                tile_before = (i - 1, RT - 1) if p == 0 else (i, p - 1)
                if behind:
                    hidden_T(*tile_before)
                for n in chunks:
                    split_high(act, i + 1, n)
                silu(i, p)
                if more:
                    rows_T(i + (p + 1) // RT, (p + 1) % RT)
                if behind:
                    scaled(*tile_before)

            rows_T(0, 0)
            for p in range(RT):
                slot(0, p, FIRST_CHUNKS[p], behind=(p > 0))
            with act.Fori(1, E - 1) as i:
                for p in range(RT):
                    slot(i, p, (p,) if p < len(CHUNKS) else ())
            with act.Fori(E - 1, LOOPS) as i:
                for p in range(RT):
                    slot(i, p)
            for j in range(RT * LOOPS, MT):
                slot(*divmod(j, RT), more=(j < MT - 1))
            hidden_T(*divmod(MT - 1, RT))
            scaled(*divmod(MT - 1, RT))

        @block.vector
        def _(dve):
            def rows_T(i, p):
                j = RT * i + p
                dve.wait_ge(s["eT_hi"], j + 1)
                nc.vector.tensor_tensor(xqT_lo[:, :, :].rearrange("p c t -> p (c t)"), XT_BANK[:, 0:KD * P],
                                        xqT_hi[:, :, :].rearrange("p c t -> p (c t)").bitcast(F32), ALU.subtract).then_inc(s["eT_lo"], 1)

            def gated(i, p):
                j = RT * i + p
                dve.wait_ge(s["e_silu"], j + 1)
                dve.wait_ge(s["e_up"], j + 1)
                nc.vector.tensor_tensor(hid[p % 2][:, :], hid[p % 2][:, :], U_BANK[p % 2][:, :], ALU.mult).then_inc(s["e_hid"], 1)

            def hidden_T(i, p):
                j = RT * i + p
                dve.wait_ge(s["e_hT_hi"], j + 1)
                nc.vector.tensor_tensor(hidT_lo[:, :, :].rearrange("p c t -> p (c t)"), HT_BANK[:, :],
                                        hidT_hi[:, :, :].rearrange("p c t -> p (c t)").bitcast(F32), ALU.subtract).then_inc(s["e_hT_lo"], 1)

            def slot(i, p, chunks=(), behind=True, more=True):
                if behind:
                    hidden_T(*((i - 1, RT - 1) if p == 0 else (i, p - 1)))
                for n in chunks:
                    split_low(dve, i + 1, n)
                gated(i, p)
                if more:
                    rows_T(i + (p + 1) // RT, (p + 1) % RT)

            rows_T(0, 0)
            for p in range(RT):
                slot(0, p, FIRST_CHUNKS[p], behind=(p > 0))
            with dve.Fori(1, E - 1) as i:
                for p in range(RT):
                    slot(i, p, (p,) if p < len(CHUNKS) else ())
            with dve.Fori(E - 1, LOOPS) as i:
                for p in range(RT):
                    slot(i, p)
            for j in range(RT * LOOPS, MT):
                slot(*divmod(j, RT), more=(j < MT - 1))
            hidden_T(*divmod(MT - 1, RT))


_INS = ['x', 'ctxT', 'g_xattn', 'g_ffn', 'L0_xattn_Wq', 'L0_xattn_Wk', 'L0_xattn_Wv', 'L0_xattn_Wo', 'L0_xattn_bo',
        'L0_ffn_ln_gamma', 'L0_ffn_ln_beta', 'router_wT', 'gate_up_wT', 'down_wT']


def kernel(**inputs):
    import numpy as _np
    import concourse.bacc as _bacc
    from concourse import mybir as _mybir
    from concourse.bass_utils import run_bass_kernel_spmd as _run

    laid = {k: _np.asarray(v) for k, v in inputs.items()}
    laid['ctxT'] = laid['ctx_768'].transpose(0, 2, 1)
    laid['router_wT'] = laid['L0_ffn_router_w'].transpose(1, 0)
    laid['gate_up_wT'] = laid['L0_ffn_gate_up_w'].transpose(0, 2, 1)
    laid['down_wT'] = laid['L0_ffn_down_w'].transpose(0, 2, 1)
    B, SEQ, D = laid['x'].shape
    nc = _bacc.Bacc("TRN2", target_bir_lowering=False, num_devices=1)
    arrays, args = {}, []
    for name in _INS:
        a = _np.ascontiguousarray(laid[name])
        arrays[f"in_{name}_dram"] = a
        args.append(nc.dram_tensor(f"in_{name}_dram", a.shape, _mybir.dt.from_np(a.dtype), kind="ExternalInput").ap())
    out = nc.dram_tensor("out_dram", (B * SEQ + 128, D), _mybir.dt.float32, kind="ExternalOutput").ap()
    gated_xattn_moe(nc, *args, out)
    r = _run(nc, [arrays], core_ids=[0])
    return r.results[0]["out_dram"][:B * SEQ].reshape(B, SEQ, D)
```

```python
from contextlib import ExitStack

import concourse.bass as bass
from concourse import mybir

ALU = mybir.AluOpType
ACT = mybir.ActivationFunctionType
F32 = mybir.dt.float32
F32R = mybir.dt.float32r
BF16 = mybir.dt.bfloat16
I32 = mybir.dt.int32
U32 = mybir.dt.uint32
U16 = mybir.dt.uint16
AX_X = mybir.AxisListType.X

P = 128
LN_EPS = 1e-5
ROUTER_EPS = 1e-8
CLAMP = 10000.0


def at_least(eng, sem, value):
    if not isinstance(value, int) or value > 0:
        eng.wait_ge(sem, value)


def pick(buf, t):
    if isinstance(t, int):
        return buf[:, t, :]
    return buf[:, bass.ds(t, 1), :].rearrange("p a d -> p (a d)")


def pick_cols(buf, t, col, n):
    if isinstance(t, int):
        return buf[:, t, col:col + n]
    return buf[:, bass.ds(t, 1), col:col + n].rearrange("p a d -> p (a d)")


def gated_xattn_moe(nc, x, ctxT, g_x, g_f, Wq, Wk, Wv, Wo, bo, gamma, beta, rwT, guT, dnT, out):
    B, SEQ, D = x.shape
    CD, NKB = ctxT.shape[1], ctxT.shape[2]
    INNER = Wq.shape[1]
    DH = 64
    H = INNER // DH
    E = rwT.shape[1]
    FF2 = guT.shape[2]
    FF = FF2 // 2
    N = B * SEQ
    NT = N // P
    CK = CD // 2
    KD = D // P
    KF = FF // P
    HQ = 4
    UPT = H // HQ
    TPI, GPI = 4, 2
    UPI = UPT * TPI
    NI = NT // TPI
    GT = 2 * P
    SCALE = float(DH) ** -0.5
    PW = HQ * NKB
    NBLK = -(-PW // P)
    LASTB = PW - (NBLK - 1) * P

    pieces = [(b, j) for b in range(NBLK) for j in range(HQ) if j * NKB < min((b + 1) * P, PW) and (j + 1) * NKB > b * P]
    blk_cols = [[k for k, pc in enumerate(pieces) if pc[0] == b] for b in range(NBLK)]
    VC = len(pieces) * DH

    REG = N + P
    MT = (2 * N - E) // P + E
    DUMMY = E * REG
    RW = D + 1

    RT = 2 * N // P // E
    LOOPS = MT // RT
    CHUNK = KF * D
    FIRST_CHUNKS = [(), (0,), (1, 2), ()]

    with ExitStack() as ctx:
        def sb(name, shape, dt=F32):
            return ctx.enter_context(nc.sbuf_tensor(name, shape, dt))

        def sem(name):
            return ctx.enter_context(nc.semaphore(name))

        bank = [ctx.enter_context(nc.psum_tensor(f"bank{n}", [P, 512], F32)) for n in range(8)]
        S_BANK, TA, TB, O_BANK, M_BANK = bank[0:2], bank[2], bank[3], bank[4:6], bank[6:8]
        V_BANK = [bank[4], bank[5], bank[2], bank[3]]

        queue = nc.dram_tensor("expert_queue", [E * REG + P, RW], F32)

        s = {}
        for name in ("ones const ctx_in wv_in wq_in wo_in small_in tanh wq_hi wq_lo kp k_hi k_lo vp vdone "
                     "out0 out0_q xf xfT_ps logits lg_read lsh ex chosen pos_ps pos_read row_sb rows_q gated pads_q "
                     "k_zero zero pads order table rows_made zero_q wo_split "
                     "ptA ptB ptA_sb ptB_sb pv y y_sb "
                     "xstat xrstd xn xres "
                     "w_in w_hi w_lo eT_ps eT_hi eT_lo e_gate e_silu e_up e_hid e_hT_ps e_hT_hi e_hT_lo e_y e_ysb e_tok e_idx e_add").split():
            s[name] = sem("s_" + name)
        for name, n in dict(x_in=4, wk_in=2, scores=2, smax=2, exp=2, o_sb=2, ot_ps=2, ot_hi=2, ot_sb=2, proj=5, proj_hi=5, proj_sb=5,
                            stat1=2, stat2=2, var=4, rstd=4, xin=2, xfT_sb=2, xq_in=2).items():
            s[name] = [sem(f"s_{name}{k}") for k in range(n)]

        ident = sb("ident", [P, P])
        gx = sb("gx", [P, 1]); gf = sb("gf", [P, 1])
        tgx = sb("tgx", [P, 1]); tgf = sb("tgf", [P, 1])
        table = sb("table", [P, 2, MT], U16)
        order = sb("order", [P, E], U16)

        with ExitStack() as fctx:
            def fsb(name, shape, dt=F32):
                return fctx.enter_context(nc.sbuf_tensor(name, shape, dt))

            with ExitStack() as early:
                gu_raw = early.enter_context(nc.sbuf_tensor("gu_raw", [P, E, KD * FF2], F32))
                dn_raw = early.enter_context(nc.sbuf_tensor("dn_raw", [P, E, KF * D], F32))
            gu_lo = fsb("gu_lo", [P, E, KD * FF2], F32R)
            dn_lo = fsb("dn_lo", [P, E, KF * D], F32R)
            gu_hi = fsb("gu_hi", [P, E, KD * FF2], F32R)
            dn_hi = fsb("dn_hi", [P, E, KF * D], F32R)
            xq = [fsb(f"xq{n}", [P, RW]) for n in range(2)]
            tok = [fsb(f"tok{n}", [P, 1], U32) for n in range(RT)]
            to_row = fsb("to_row", [P, 1], U32); no_offset = fsb("no_offset", [P, 1], U32)
            xqT_hi = fsb("xqT_hi", [P, KD, P], F32R)
            xqT_lo = fsb("xqT_lo", [P, KD, P], F32R)
            hid = [fsb(f"hid{n}", [P, FF]) for n in range(2)]
            hidT_hi = fsb("hidT_hi", [P, KF, P], F32R)
            hidT_lo = fsb("hidT_lo", [P, KF, P], F32R)
            yq = [fsb(f"yq{n}", [P, D]) for n in range(2)]
        G_BANK, U_BANK, XT_BANK, HT_BANK, Y_BANK = bank[0:2], bank[2:4], bank[4], bank[5], bank[6:8]

        def load_weights(sp, rank):
            e = sp.value_load(order[0:1, rank:rank + 1] if isinstance(rank, int) else order[0:1, bass.ds(rank, 1)], min_val=0, max_val=E - 1)
            for src, raw in ((guT, gu_raw), (dnT, dn_raw)):
                w = src[bass.ds(e, 1)].rearrange("a (c p) f -> p (a c) f", p=P)
                sp.dma_start(pick(raw, rank).rearrange("p (c f) -> p c f", f=src.shape[2]), w).then_inc(s["w_in"], 16)

        def load_rows(sp, i, p, free=True):
            j = RT * i + p
            r = sp.value_load(table[0:1, 1, bass.ds(j, 1)] if not isinstance(j, int) else table[0:1, 1, j:j + 1], min_val=0, max_val=DUMMY // P)
            if free:
                sp.wait_ge(s["eT_ps"], j - 1)
                sp.wait_ge(s["e_tok"], j - 1)
            sp.dma_start(xq[p % 2][:, :], queue[bass.ds(r * P, P), :]).then_inc(s["xq_in"][p % 2], 16)

        CHUNKS = [(gu_raw, gu_hi, gu_lo, 0), (gu_raw, gu_hi, gu_lo, CHUNK), (dn_raw, dn_hi, dn_lo, 0)]

        def split_high(act, rank, n):
            raw, hi, _, col = CHUNKS[n]
            act.wait_ge(s["w_in"], 32 * (rank + 1))
            nc.scalar.copy(pick_cols(hi, rank, col, CHUNK), pick_cols(raw, rank, col, CHUNK)).then_inc(s["w_hi"], 1)

        def split_low(dve, rank, n):
            raw, hi, lo, col = CHUNKS[n]
            dve.wait_ge(s["w_hi"], len(CHUNKS) * rank + n + 1)
            nc.vector.tensor_tensor(pick_cols(lo, rank, col, CHUNK), pick_cols(raw, rank, col, CHUNK),
                                    pick_cols(hi, rank, col, CHUNK).bitcast(F32), ALU.subtract).then_inc(s["w_lo"], 1)

        with ExitStack() as actx:
            def asb(name, shape, dt=F32):
                return actx.enter_context(nc.sbuf_tensor(name, shape, dt))

            wq_hi = asb("wq_hi", [P, KD, INNER], F32R)
            wq_lo = asb("wq_lo", [P, KD, INNER], F32R)
            wo_hi = asb("wo_hi", [P, INNER // P, D], F32R)
            wo_lo = asb("wo_lo", [P, INNER // P, D], F32R)
            k_hi = asb("k_hi", [P, H // 2, B, 2 * NKB], F32R)
            k_lo = asb("k_lo", [P, H // 2, B, 2 * NKB], F32R)
            vdiag = asb("vdiag", [P, B, H // HQ, VC])
            mv = asb("mv", [P, 2, 2, 2]); stat6 = asb("stat6", [P, 2, 2, 6])
            rstd = asb("rstd", [P, 2, 2]); vare = asb("vare", [P, 2, 2])
            xn = asb("xn", [P, 2, 2, D])
            xT_hi = asb("xT_hi", [P, KD, GT], F32R)
            xT_lo = asb("xT_lo", [P, KD, GT], F32R)
            with ExitStack() as early:
                wk = early.enter_context(nc.sbuf_tensor("wk", [CK, 2, INNER], F32))
                wq_raw = early.enter_context(nc.sbuf_tensor("wq_raw", [P, KD, INNER], F32))
            q_hi, q_lo = [None, None], [None, None]
            for n in (1, 0):
                q_hi[n] = asb(f"q_hi{n}", [P, H // 2, GT], F32R)
                q_lo[n] = asb(f"q_lo{n}", [P, H // 2, GT], F32R)
            before = asb("before", [P, P], BF16)
            ones = asb("ones", [P, P], BF16)
            neg_half = asb("neg_half", [P, 8])
            eps = asb("eps", [P, 8])
            tie_rank = asb("tie_rank", [P, TPI, E])
            region0 = asb("region0", [P, TPI, E])
            token_no = asb("token_no", [P, NT], I32)
            bo_b = asb("bo_b", [P, D]); gamma_b = asb("gamma_b", [P, D]); beta_b = asb("beta_b", [P, D])
            rw = asb("rw", [P, KD, E])
            x1 = asb("x1", [P, NT, D])
            base_cnt = asb("base_cnt", [P, E])
            nmax = asb("nmax", [P, 4, HQ])
            probs = [asb(f"probs{n}", [P, PW]) for n in range(4)]
            psum_row = asb("psum_row", [P, 2, H])
            rsum = asb("rsum", [P, H // 2])
            pT = [asb(f"pT{n}", [P, NBLK, P]) for n in range(2)]
            o_sb = asb("o_sb", [P, INNER])
            oT_hi = asb("oT_hi", [P, INNER // P, P], F32R)
            oT_lo = asb("oT_lo", [P, INNER // P, P], F32R)
            with ExitStack() as early:
                ctx_pad = early.enter_context(nc.sbuf_tensor("ctx_pad", [CK, B, 2, P + NKB + P], F32))
                wv = early.enter_context(nc.sbuf_tensor("wv", [CK, 2, INNER], F32))
                wo_raw = early.enter_context(nc.sbuf_tensor("wo_raw", [P, INNER // P, D], F32))
            stat_b = asb("stat_b", [P, 2, TPI, 6]); mv_b = asb("mv_b", [P, 2, TPI, 2])
            vare_b = asb("vare_b", [P, 2, TPI]); rstd_b = asb("rstd_b", [P, 2, TPI])
            xin = asb("xin", [P, TPI, D]); out0 = asb("out0", [P, TPI, D]); xf = asb("xf", [P, TPI, D])
            xfT = asb("xfT", [P, TPI * KD, P])
            lg = asb("lg", [P, TPI, E]); lmax = asb("lmax", [P, TPI]); lsh = asb("lsh", [P, TPI, E]); ex = asb("ex", [P, TPI, E])
            esum = asb("esum", [P, TPI]); erec = asb("erec", [P, TPI]); pr = [asb(f"pr{n}", [P, TPI, E]) for n in range(2)]
            gate = asb("gate", [P, 2, TPI]); pick1 = asb("pick1", [P, 2, TPI, E]); top = asb("top", [P, TPI, E]); topm = asb("topm", [P, TPI])
            chosen = asb("chosen", [P, TPI, E], BF16)
            pos = asb("pos", [P, TPI, E]); posm = asb("posm", [P, 2, TPI, E]); rowf = asb("rowf", [P, 2, TPI]); row = asb("row", [P, 2, TPI], U32)
            row_at = asb("row_at", [P, 2, TPI], U32); no_shift = asb("no_shift", [P, 2], U32)
            rows = asb("rows", [P, 2, TPI, RW])
            padf = asb("padf", [P, E]); pad = asb("pad", [P, E], U16); zrow = asb("zrow", [P, RW])
            cnt1 = asb("cnt1", [P, E]); cnti = asb("cnti", [P, E], I32); tiles = asb("tiles", [P, E]); key = asb("key", [P, E])
            rank_e = asb("rank_e", [P, E]); order_f = asb("order_f", [P, E]); start = asb("start", [P, E]); end = asb("end", [P, E])
            expert_no = asb("expert_no", [P, E]); ahead_of = asb("ahead_of", [P, E, E]); at_rank = asb("at_rank", [P, E, E])
            slot_no = asb("slot_no", [P, MT]); past = asb("past", [P, MT, E]); within = asb("within", [P, MT, E])
            rank_j = asb("rank_j", [P, MT]); row_j = asb("row_j", [P, MT]); none_left = asb("none_left", [P, MT])

            block = actx.enter_context(nc.Block())

            WARMING = 34
            JOB_SLOT = {0: 0, 1: 1, 2: 2, 4: 3, 5: 4}
            JOB_BANK = [0, 1, 0, 0, 1]
            FIRST_BANK = [0, 1, 0, 1, 0]

            TURN, LOGIT, COUNT = 9, 10, 14
            LG0 = 2 * P

            def tile_at(i, n):
                k, r = divmod(n, TPI)
                return (r // 2) * (SEQ // P) + 2 * (i + k) + r % 2

            def two_tiles(i, b):
                first = b * (SEQ // P) + 2 * (i - 1)
                return x1[:, first:first + 2, :] if isinstance(i, int) else x1[:, bass.ds(first, 2), :]

            zero_keys = ((slice(DH, P), slice(0, NKB)), (slice(0, DH), slice(NKB, 2 * NKB)))

            @block.sync
            def _(sp):
                for b in range(B):
                    sp.dma_start(ctx_pad[:, b, :, P:P + NKB], ctxT[b].rearrange("(c p) k -> p c k", p=CK)).then_inc(s["ctx_in"], 16)
                for m in range(2):
                    half = slice(m * INNER // 2, (m + 1) * INNER // 2)
                    sp.dma_start(wk[:, :, half], Wk.rearrange("(c p) n -> p c n", p=CK)[:, :, half]).then_inc(s["wk_in"][m], 16)
                for n in (0, 2, 1, 3):
                    sp.dma_start(x1[:, 4 * n:4 * n + 4, :], x.rearrange("b (t p) d -> p (b t) d", p=P)[:, 4 * n:4 * n + 4, :]).then_inc(s["x_in"][n], 16)
                    if n == 0:
                        sp.dma_start(wv[:, :, :], Wv.rearrange("(c p) n -> p c n", p=CK)).then_inc(s["wv_in"], 16)
                        sp.dma_start(wq_raw[:, :, :], Wq.rearrange("(c p) n -> p c n", p=P)).then_inc(s["wq_in"], 16)
                for dst, src in ((gx, g_x), (gf, g_f), (bo_b, bo), (gamma_b, gamma), (beta_b, beta)):
                    sp.dma_start(dst[:, :], src.partition_broadcast(P)).then_inc(s["small_in"], 16)
                sp.dma_start(rw[:, :, :], rwT.rearrange("(c p) e -> p c e", p=P)).then_inc(s["small_in"], 16)
                sp.dma_start(wo_raw[:, :, :], Wo.rearrange("(c p) n -> p c n", p=P)).then_inc(s["wo_in"], 16)
                sp.wait_ge(s["zero"], 1)
                sp.dma_start(queue[DUMMY:DUMMY + P, :], zrow[:, :]).then_inc(s["zero_q"], 16)
                sp.dma_start(out[N:N + P, :], zrow[:, 0:D]).then_inc(s["zero_q"], 16)

                def send_output(i):
                    sp.wait_ge(s["out0"], 2 * (i + 1))
                    for b in range(B):
                        dst = out[bass.ds((b * (SEQ // P) + 2 * i) * P, 2 * P), :].rearrange("(t p) d -> p t d", p=P)
                        sp.dma_start(dst, out0[:, 2 * b:2 * b + 2, :]).then_inc(s["out0_q"], 16)

                with sp.Fori(0, NI - 1) as i:
                    send_output(i)
                sp.wait_ge(s["pads"], 1)
                for e in range(E):
                    first = sp.value_load(pad[0:1, e:e + 1], min_val=0, max_val=DUMMY - (TPI + 1) * P)
                    sp.dma_start(queue[bass.ds(first, (TPI + 1) * P), :].rearrange("(a p) d -> p a d", p=P),
                                 zrow[:, :].unsqueeze(1).to_broadcast([P, TPI + 1, RW])).then_inc(s["pads_q"], 16)
                send_output(NI - 1)
                sp.wait_ge(s["out0_q"], 32 * NI)
                sp.wait_ge(s["zero_q"], 32)
                sp.wait_ge(s["order"], 1)
                sp.wait_ge(s["pos_ps"], NI)
                load_weights(sp, 0)
                sp.wait_ge(s["rows_q"], 16 * 2 * NT)
                sp.wait_ge(s["table"], 1)
                load_rows(sp, 0, 0, False)
                load_rows(sp, 0, 1, False)

            @block.gpsimd
            def _(pool):
                nc.gpsimd.memset(ones[:, :], 1.0).then_inc(s["ones"], 1)
                nc.gpsimd.memset(ctx_pad[:, :, :, 0:P], 0.0)
                nc.gpsimd.memset(ctx_pad[:, :, :, P + NKB:], 0.0).then_inc(s["const"], 1)
                nc.gpsimd.memset(ident[:, :], 0.0)
                nc.gpsimd.memset(before[:, :], 1.0)
                nc.gpsimd.memset(neg_half[:, :], -0.5)
                nc.gpsimd.memset(eps[:, :], LN_EPS)
                nc.gpsimd.memset(base_cnt[:, :], 0.0)
                nc.gpsimd.iota(token_no[:, :], [[P, NT]], base=0, channel_multiplier=1)
                nc.gpsimd.iota(tie_rank[:, :, :], [[0, TPI], [-1, E]], base=E, channel_multiplier=0, allow_small_or_imprecise_dtypes=True)
                nc.gpsimd.iota(region0[:, :, :], [[0, TPI], [REG, E]], base=0, channel_multiplier=0, allow_small_or_imprecise_dtypes=True)
                nc.gpsimd.drain()
                nc.gpsimd.affine_select(out=ident[:, :], in_=ident[:, :], compare_op=ALU.not_equal, fill=1.0,
                                        base=0, pattern=[[-1, P]], channel_multiplier=1)
                nc.gpsimd.affine_select(out=before[:, :], in_=before[:, :], compare_op=ALU.is_gt, fill=0.0,
                                        base=0, pattern=[[1, P]], channel_multiplier=-1).then_inc(s["const"], 1)

                nc.gpsimd.iota(slot_no[:, :], [[1, MT]], base=0, channel_multiplier=0, allow_small_or_imprecise_dtypes=True)
                nc.gpsimd.iota(expert_no[:, :], [[1, E]], base=0, channel_multiplier=0, allow_small_or_imprecise_dtypes=True)

                def rstd_step(i, par):
                    g = GPI * i + par
                    pool.wait_ge(s["xstat"], g + 1)
                    nc.gpsimd.tensor_tensor(vare[:, par, :], mv[:, par, :, 1], eps[:, 0:2], ALU.add)
                    nc.gpsimd.drain()
                    nc.gpsimd.tensor_tensor(rstd[:, par, :], vare[:, par, :], neg_half[:, 0:2], ALU.pow).then_inc(s["xrstd"], 1)

                nc.gpsimd.drain()
                for half, keys in zero_keys:
                    nc.gpsimd.memset(k_lo[half, :, :, keys].bitcast(F32), 0.0).then_inc(s["k_zero"], 1)
                    nc.gpsimd.drain()
                rstd_step(0, 0)
                rstd_step(0, 1)
                pool.wait_ge(s["tanh"], 1)
                nc.gpsimd.tensor_scalar(bo_b[:, :], bo_b[:, :], tgx[:, 0:1], None, ALU.mult)
                nc.gpsimd.drain()

                def add_bias(i, gl):
                    pool.wait_ge(s["xn"], GPI * i + gl + 1)
                    for j in range(2):
                        tile = pick(x1, tile_at(i, 2 * gl + j))
                        last = nc.gpsimd.tensor_tensor(tile, tile, bo_b[:, :], ALU.add)
                    last.then_inc(s["xres"], 1)

                add_bias(0, 0)
                add_bias(0, 1)
                pool.wait_ge(s["wo_in"], 16)
                for c in range(4):
                    part = slice(2 * c, 2 * c + 2)
                    nc.gpsimd.tensor_copy(wo_hi[:, part, :], wo_raw[:, part, :]).then_inc(s["wo_split"], 1)
                    pool.wait_ge(s["wo_split"], 2 * c + 1)
                    nc.gpsimd.tensor_tensor(wo_lo[:, part, :], wo_raw[:, part, :], wo_hi[:, part, :].bitcast(F32), ALU.subtract).then_inc(s["wo_split"], 1)

                def route_rstd(i, k, b):
                    two = slice(2 * b, 2 * b + 2)
                    pool.wait_ge(s[("stat1", "stat2")[k]][b], i)
                    nc.gpsimd.tensor_tensor(vare_b[:, k, two], mv_b[:, k, two, 1], eps[:, 0:2], ALU.add).then_inc(s["var"][2 * k + b], 1)
                    pool.wait_ge(s["var"][2 * k + b], i)
                    nc.gpsimd.tensor_tensor(rstd_b[:, k, two], vare_b[:, k, two], neg_half[:, 0:2], ALU.pow).then_inc(s["rstd"][2 * k + b], 1)

                def first_norm(i, b):
                    route_rstd(i, 0, b)
                    nc.gpsimd.drain()
                    two, shape = slice(2 * b, 2 * b + 2), [P, 2, D]
                    nc.gpsimd.tensor_tensor(xin[:, two, :], two_tiles(i, b), mv_b[:, 0, two, 0:1].to_broadcast(shape), ALU.subtract)
                    nc.gpsimd.drain()
                    nc.gpsimd.tensor_tensor(xin[:, two, :], xin[:, two, :], rstd_b[:, 0, two].unsqueeze(2).to_broadcast(shape), ALU.mult).then_inc(s["xin"][b], 1)

                def second_norm(i, b):
                    route_rstd(i, 1, b)
                    nc.gpsimd.drain()
                    for j in (2 * b, 2 * b + 1):
                        nc.gpsimd.tensor_scalar(xf[:, j, :], xin[:, j, :], mv_b[:, 1, j, 0:1], rstd_b[:, 1, j:j + 1], ALU.subtract, ALU.mult)
                    nc.gpsimd.drain()
                    two, shape = slice(2 * b, 2 * b + 2), [P, 2, D]
                    nc.gpsimd.tensor_tensor(xf[:, two, :], xf[:, two, :], gamma_b[:, :].unsqueeze(1).to_broadcast(shape), ALU.mult)
                    nc.gpsimd.drain()
                    nc.gpsimd.tensor_tensor(xf[:, two, :], xf[:, two, :], beta_b[:, :].unsqueeze(1).to_broadcast(shape), ALU.add).then_inc(s["xf"], 1)

                def number_tokens(i):
                    of_batch = token_no[:, :].rearrange("p (b t) -> p b t", b=B)
                    first = 2 * (i - 1)
                    of_batch = of_batch[:, :, first:first + 2] if isinstance(i, int) else of_batch[:, :, bass.ds(first, 2)]
                    for k in range(2):
                        last = nc.gpsimd.tensor_copy(rows[:, k, :, D:RW].bitcast(I32).rearrange("p (b t) o -> p b (t o)", b=B), of_batch)
                    last.then_inc(s["rows_made"], 1)

                def gated_rows(i):
                    pool.wait_ge(s["chosen"], i)
                    at_least(pool, s["rows_q"], 16 * 2 * TPI * (i - 1))
                    for k in range(2):
                        for j in range(TPI):
                            if k == 0 and j == 0:
                                nc.gpsimd.tensor_tensor(rows[:, 0, 0, 0:D], xf[:, 0, :], gate[:, 0, 0:1].to_broadcast([P, D]), ALU.mult)
                                continue
                            nc.gpsimd.tensor_scalar(rows[:, k, j, 0:D], xf[:, j, :], gate[:, k, j:j + 1], None, ALU.mult)
                    number_tokens(i)
                    nc.gpsimd.drain()

                def send_rows(i, k):
                    if k == 0:
                        pool.wait_ge(s["row_sb"], i)
                        nc.gpsimd.tensor_tensor(row_at[:, :, :], row[:, :, :], no_shift[:, :].unsqueeze(2).to_broadcast([P, 2, TPI]), ALU.add)
                        nc.gpsimd.drain()
                    for j in range(TPI):
                        nc.gpsimd.indirect_dma_start(queue[:, :], bass.IndirectOffsetOnAxis(row_at[:, k, j:j + 1], 0),
                                                     rows[:, k, j, :], None).then_inc(s["rows_q"], 16)

                def body(i, more=True):
                    behind = not (isinstance(i, int) and i == 0)
                    if behind:
                        first_norm(i, 0)
                    if more:
                        rstd_step(i + 1, 0)
                    if behind:
                        first_norm(i, 1)
                        second_norm(i, 0)
                        second_norm(i, 1)
                    if more:
                        add_bias(i + 1, 0)
                        rstd_step(i + 1, 1)
                        add_bias(i + 1, 1)
                    if behind:
                        gated_rows(i)

                body(0)
                pool.wait_ge(s["vdone"], B * len(pieces) // 2)
                nc.gpsimd.drain()
                nc.gpsimd.memset(zrow[:, 0:D], 0.0)
                nc.gpsimd.memset(no_shift[:, :], 0)
                nc.gpsimd.iota(zrow[:, D:RW].bitcast(I32), [[0, 1]], base=N, channel_multiplier=1).then_inc(s["zero"], 1)
                with pool.Fori(1, NI - 1) as i:
                    body(i)
                    for k in range(2):
                        send_rows(i, k)
                body(NI - 1, more=False)
                route_rstd(NI, 0, 0)
                send_rows(NI - 1, 0)
                route_rstd(NI, 1, 0)
                for k in range(2):
                    route_rstd(NI, k, 1)
                send_rows(NI - 1, 1)
                pool.wait_ge(s["rows_q"], 16 * 2 * (NT - TPI))
                number_tokens(NI)
                nc.gpsimd.drain()
                pool.wait_ge(s["gated"], 1)
                pool.wait_ge(s["pads_q"], 16 * E)
                for k in range(2):
                    send_rows(NI, k)
                pool.wait_ge(s["rows_q"], 16 * 2 * NT)

            @block.tensor
            def _(pe):
                pe.wait_ge(s["ones"], 1)
                for _ in range(WARMING):
                    nc.tensor.matmul(M_BANK[1][:, 0:P], ones[:, :], ones[:, :], start=True, stop=True)
                pe.wait_ge(s["ctx_in"], 32)
                for m in range(H // 2):
                    if m % 4 == 0:
                        pe.wait_ge(s["wk_in"][m // 4], 16)
                    if m >= 4:
                        pe.wait_ge(s["k_lo"], m - 3)
                    for c in range(2):
                        last = nc.tensor.matmul(bank[m % 4][:, 0:B * NKB].rearrange("p (b k) -> p b k", b=B),
                                                wk[:, c, m * P:(m + 1) * P], ctx_pad[:, :, c, P:P + NKB],
                                                start=(c == 0), stop=(c == 1))
                    last.then_inc(s["kp"], 1)

                def group_job(g, par, k, banks, free):
                    at = M_BANK[banks[k]]
                    free()
                    if k == 0:
                        pe.wait_ge(s["xn"], g + 1)
                        if isinstance(g, int) and g == 0:
                            pe.wait_ge(s["const"], 2)
                        for j in range(2):
                            for c in range(KD):
                                last = nc.tensor.transpose(at[:, (2 * j + c) * P:(2 * j + c + 1) * P],
                                                           xn[:, par, j, c * P:(c + 1) * P], ident[:, :])
                    else:
                        if k == 1:
                            pe.wait_ge(s["proj_sb"][0], g + 1)
                        for m in range(2):
                            pair = 2 * (k - 1) + m
                            cols = slice(pair * P, (pair + 1) * P)
                            n = 0
                            for c in range(KD):
                                for w, v in ((wq_hi, xT_hi), (wq_lo, xT_hi), (wq_hi, xT_lo)):
                                    last = nc.tensor.matmul(at[:, m * GT:(m + 1) * GT], w[:, c, cols], v[:, c, :],
                                                            start=(n == 0), stop=(n == 5))
                                    n += 1
                    last.then_inc(s["proj"][k], 1)

                def scores(i, u):
                    par, w = (u // 8) % 2, u % 8
                    for hf in range(2):
                        at_least(pe, s["exp"][hf], UPI * i + u)
                        if w < UPT and hf == 0:
                            pe.wait_ge(s["proj_sb"][w + 1], GPI * i + u // 8 + 1)
                        pair = (u % UPT) * 2 + hf
                        tok = ((u // UPT) % 2) * P
                        n = 0
                        for q, k in ((q_hi, k_hi), (q_hi, k_lo), (q_lo, k_hi)):
                            last = nc.tensor.matmul(S_BANK[hf][:, 0:2 * NKB], q[par][:, pair, tok:tok + P], k[:, pair, par, :],
                                                    start=(n == 0), stop=(n == 2))
                            n += 1
                        last.then_inc(s["scores"][hf], 1)
                        yield

                def transpose_probs(i, u):
                    U = UPI * i + u
                    pe.wait_ge(s["exp"][1], U + 1)
                    at_least(pe, s["ptA_sb"], U)
                    at_least(pe, s["ptB_sb"], U)
                    for b in range(NBLK):
                        rows = P if b < NBLK - 1 else LASTB
                        dst = (TA if b < 3 else TB)[0:rows, (b % 3) * P:(b % 3 + 1) * P]
                        last = nc.tensor.transpose(dst, probs[u % 4][:, b * P:b * P + rows], ident[:, :])
                        if b == 2:
                            last.then_inc(s["ptA"], 1)
                    last.then_inc(s["ptB"], 1)

                def attend(i, u, waits=False):
                    U = UPI * i + u
                    batch = (u // 8) % 2
                    if waits:
                        pe.wait_ge(s["ptA_sb"], U + 1)
                        pe.wait_ge(s["ptB_sb"], U + 1)
                    if u % 2 == 0:
                        at_least(pe, s["ot_sb"][(u % UPT) // 2], TPI * i + u // UPT)
                    at = O_BANK[(u % UPT) // 2]
                    col0 = (u % 2) * HQ * DH
                    g = u % UPT
                    for b in range(NBLK):
                        rows = P if b < NBLK - 1 else LASTB
                        ks = blk_cols[b]
                        j0 = pieces[ks[0]][1]
                        n = len(ks) * DH
                        v = vdiag[0:rows, batch, g, ks[0] * DH:ks[0] * DH + n]
                        last = nc.tensor.matmul(at[:, col0 + j0 * DH:col0 + j0 * DH + n], pT[u % 2][0:rows, b, :],
                                                v, start=(b == 0), stop=(b == NBLK - 1), skip_group_check=True)
                    last.then_inc(s["pv"], 1)

                def transpose_out(i, u):
                    half = (u % UPT) // 2
                    pe.wait_ge(s["o_sb"][half], TPI * i + u // UPT)
                    for c in range(4):
                        last = nc.tensor.transpose(O_BANK[half][:, c * P:(c + 1) * P],
                                                   o_sb[:, (4 * half + c) * P:(4 * half + c + 1) * P], ident[:, :])
                    last.then_inc(s["ot_ps"][half], 1)

                def project_out(i, u):
                    for half in range(2):
                        pe.wait_ge(s["ot_sb"][half], TPI * i + u // UPT)
                    if isinstance(i, int) and TPI * i + u // UPT == 1:
                        pe.wait_ge(s["wo_split"], 8)
                    n, most = 0, 3 * INNER // P
                    for c in range(INNER // P):
                        for o, w in ((oT_hi, wo_hi), (oT_lo, wo_hi), (oT_hi, wo_lo)):
                            last = nc.tensor.matmul(M_BANK[1][:, 0:D], o[:, c, :], w[:, c, :], start=(n == 0), stop=(n == most - 1))
                            n += 1
                    last.then_inc(s["y"], 1)

                def turn_features(i, b):
                    pe.wait_ge(s["xf"], 2 * i - 1 + b)
                    for a in range(2 * KD):
                        last = nc.tensor.transpose((TA, TB)[b][:, a * P:(a + 1) * P],
                                                   xf[:, 2 * b + a // KD, (a % KD) * P:(a % KD + 1) * P], ident[:, :])
                    last.then_inc(s["xfT_ps"], 1)

                def router_logits(i, b, at):
                    pe.wait_ge(s["xfT_sb"][b], i)
                    for j in (2 * b, 2 * b + 1):
                        for c in range(KD):
                            last = nc.tensor.matmul(at[:, LG0 + j * E:LG0 + (j + 1) * E], xfT[:, j * KD + c, :], rw[:, c, :],
                                                    start=(c == 0), stop=(c == KD - 1))
                    last.then_inc(s["logits"], 1)

                def rows_before(i):
                    pe.wait_ge(s["chosen"], i)
                    flat = chosen[:, :, :].rearrange("p t e -> p (t e)")
                    nc.tensor.matmul(TB[:, LG0:LG0 + TPI * E], before[:, :], flat, start=True, stop=False, skip_group_check=True)
                    for j in range(TPI - 1):
                        for jj in range(j + 1, TPI):
                            nc.tensor.matmul(TB[:, LG0 + jj * E:LG0 + (jj + 1) * E], ones[:, :], chosen[:, j, :],
                                             start=False, stop=(jj == j + 1), skip_group_check=True)
                    for j in range(TPI):
                        last = nc.tensor.matmul(TB[:, LG0 + TPI * E:LG0 + (TPI + 1) * E], ones[:, :], chosen[:, j, :],
                                                start=False, stop=(j == TPI - 1), skip_group_check=True)
                    last.then_inc(s["pos_ps"], 1)

                def route_step(i, u):
                    if u in (TURN, LOGIT, COUNT):
                        pe.wait_ge(s["ptB_sb"], UPI * i + u + 1)
                    if u == TURN:
                        pe.wait_ge(s["ptA_sb"], UPI * i + u + 1)
                        for b in range(B):
                            turn_features(i, b)
                    if u == LOGIT:
                        for b in range(B):
                            router_logits(i, b, TB)
                    if u == COUNT:
                        rows_before(i)

                def slot(i, u):
                    first = isinstance(i, int) and i == 0
                    last = isinstance(i, int) and i == NI - 1
                    ahead = scores(i, u + 2) if not (last and u + 2 >= UPI) else iter(())
                    next(ahead, None)
                    if first and u == 0:
                        pe.wait_ge(s["vdone"], B * len(pieces) // 2 + 1)
                    if not first and u == TURN + 1:
                        for m in range(2):
                            pe.wait_ge(s["xfT_sb"][m], i)
                    if not first and u == LOGIT + 1:
                        pe.wait_ge(s["lg_read"], i)
                    if not first and u == COUNT + 1:
                        pe.wait_ge(s["pos_read"], i)
                    transpose_probs(i, u)
                    if u % 2 == 0 and not (first and u < UPT):
                        transpose_out(i, u)
                    next(ahead, None)
                    if not (first and u == 0):
                        attend(i, u - 1)
                    w, g = u % 8, GPI * i + u // 8 + 1
                    par = (u // 8 + 1) % 2
                    if w in JOB_SLOT and not (last and u >= 8):
                        k = JOB_SLOT[w]

                        def free():
                            if k == 0:
                                pe.wait_ge(s["proj_sb"][3], g)
                            elif k in (1, 4):
                                at_least(pe, s["y_sb"], TPI * i + u // UPT - 1)
                            else:
                                pe.wait_ge(s["proj_sb"][k - 1 if k == 3 else 0], g + 1)
                        group_job(g, par, k, JOB_BANK, free)
                    if w % UPT == UPT - 1 and not (first and u < UPT):
                        if not (last and u >= 8):
                            pe.wait_ge(s["proj_sb"][1 if w == 3 else 4], g + 1)
                        at_least(pe, s["y_sb"], TPI * i + u // UPT - 1)
                        project_out(i, u)
                    if not first:
                        route_step(i, u)

                def values(b, ms):
                    for m in ms:
                        n = b * (len(pieces) // 2) + m
                        at = V_BANK[n % 4]
                        if n == 2:
                            pe.wait_ge(s["k_lo"], H // 2)
                        if n >= 4:
                            pe.wait_ge(s["vdone"], n - 3)
                        for a in range(2):
                            blk, j = pieces[2 * m + a]
                            lo = P + blk * P - j * NKB
                            for c in range(2):
                                last = nc.tensor.matmul(at[:, :].rearrange("p (g a d) -> p g a d", g=H // HQ, a=2)[:, :, a, :],
                                                        ctx_pad[:, b, c, lo:lo + P],
                                                        wv[:, c, :].rearrange("p (g j d) -> p g j d", j=HQ, d=DH)[:, :, j, :],
                                                        start=(c == 0 and a == 0), stop=(c == 1), skip_group_check=True)
                        last.then_inc(s["vp"], 1)

                def first_job(k):
                    group_job(0, 0, k, FIRST_BANK, lambda: k >= 2 and pe.wait_ge(s["proj_sb"][k - 2], 1))

                first_job(0)
                pe.wait_ge(s["const"], 1)
                pe.wait_ge(s["wv_in"], 16)
                values(0, range(len(pieces) // 2))
                pe.wait_ge(s["wq_lo"], KD)
                for k in range(1, 5):
                    first_job(k)
                pe.wait_ge(s["k_zero"], 3)
                for u in range(2):
                    for _ in scores(0, u):
                        pass
                    values(1, (2 * u, 2 * u + 1))
                for u in range(UPI):
                    slot(0, u)
                with pe.Fori(1, NI - 1) as i:
                    for u in range(UPI):
                        slot(i, u)
                for u in range(UPI):
                    slot(NI - 1, u)
                attend(NI, -1, waits=True)
                transpose_out(NI, 0)
                transpose_out(NI, 2)
                at_least(pe, s["y_sb"], NT - 1)
                project_out(NI, 3)
                for b in range(B):
                    turn_features(NI, b)
                    router_logits(NI, b, S_BANK[0])
                rows_before(NI)

            @block.scalar
            def _(act):
                for m in range(H // 2):
                    act.wait_ge(s["kp"], m + 1)
                    for a in range(2):
                        half = slice(a * DH, (a + 1) * DH)
                        last = nc.scalar.activation(k_hi[half, m, :, a * NKB:(a + 1) * NKB],
                                                    bank[m % 4][half, 0:B * NKB].rearrange("p (b k) -> p b k", b=B), ACT.Copy, scale=SCALE)
                    last.then_inc(s["k_hi"], 1)

                def high_part(g, k, banks, par):
                    act.wait_ge(s["proj"][k], g + 1)
                    at = M_BANK[banks[k]]
                    if k == 0:
                        last = nc.scalar.copy(xT_hi[:, :, :].rearrange("p c (j t) -> p j c t", j=2),
                                              at[:, :].rearrange("p (j c t) -> p j c t", j=2, c=KD))
                    else:
                        last = nc.scalar.copy(q_hi[par][:, 2 * k - 2:2 * k, :].rearrange("p m t -> p (m t)"), at[:, :])
                    last.then_inc(s["proj_hi"][k], 1)

                def exps(i, u):
                    for hf in range(2):
                        act.wait_ge(s["smax"][hf], UPI * i + u + 1)
                        for m in range(2):
                            j = 2 * hf + m
                            h = (u % UPT) * HQ + j
                            last = nc.scalar.activation(probs[u % 4][:, j * NKB:(j + 1) * NKB], S_BANK[hf][:, m * NKB:(m + 1) * NKB],
                                                        ACT.Exp, bias=nmax[:, u % 4, j:j + 1], scale=1.0,
                                                        accum_out=psum_row[:, (u // UPT) % 2, h:h + 1])
                        last.then_inc(s["exp"][hf], 1)
                        yield

                def transposed_out(i, u):
                    half = (u % UPT) // 2
                    act.wait_ge(s["ot_ps"][half], TPI * i + u // UPT)
                    nc.scalar.copy(oT_hi[:, 4 * half:4 * half + 4, :].rearrange("p c t -> p (c t)"), O_BANK[half][:, :]).then_inc(s["ot_hi"][half], 1)

                def turned_features(i):
                    act.wait_ge(s["xfT_ps"], 2 * i - 1)
                    nc.scalar.copy(xfT[:, 0:4, :].rearrange("p c t -> p (c t)"), TA[:, :]).then_inc(s["xfT_sb"][0], 1)

                def router_exp(i):
                    act.wait_ge(s["lsh"], i)
                    nc.scalar.activation(ex[:, :, :], lsh[:, :, :], ACT.Exp).then_inc(s["ex"], 1)

                def slot(i, u):
                    first = isinstance(i, int) and i == 0
                    last = isinstance(i, int) and i == NI - 1
                    if not first and u == TURN + 1:
                        turned_features(i)
                    ahead = exps(i, u + 2) if not (last and u + 2 >= UPI) else iter(())
                    next(ahead, None)
                    act.wait_ge(s["ptA"], UPI * i + u + 1)
                    nc.scalar.copy(pT[u % 2][:, 0:3, :].rearrange("p b t -> p (b t)"), TA[:, 0:3 * P]).then_inc(s["ptA_sb"], 1)
                    next(ahead, None)
                    if u % 2 == 0 and not (first and u < UPT):
                        transposed_out(i, u)
                    w, g = u % 8, GPI * i + u // 8 + 1
                    if w in JOB_SLOT and not (last and u >= 8):
                        high_part(g, JOB_SLOT[w], JOB_BANK, (u // 8 + 1) % 2)
                    if not first and u == LOGIT + 1:
                        router_exp(i)

                high_part(0, 0, FIRST_BANK, 0)
                act.wait_ge(s["wq_in"], 16)
                for c in range(KD):
                    nc.scalar.copy(wq_hi[:, c, :], wq_raw[:, c, :]).then_inc(s["wq_hi"], 1)
                act.wait_ge(s["small_in"], 96)
                nc.scalar.activation(tgx[:, :], gx[:, :], ACT.Tanh)
                nc.scalar.activation(tgf[:, :], gf[:, :], ACT.Tanh).then_inc(s["tanh"], 1)
                for k in range(1, 5):
                    high_part(0, k, FIRST_BANK, 0)
                for u in range(2):
                    for _ in exps(0, u):
                        pass
                for u in range(UPI):
                    slot(0, u)
                with act.Fori(1, NI - 1) as i:
                    for u in range(UPI):
                        slot(i, u)
                for u in range(UPI):
                    slot(NI - 1, u)
                transposed_out(NI, 0)
                transposed_out(NI, 2)
                turned_features(NI)
                router_exp(NI)
                act.wait_ge(s["chosen"], NI)
                act.wait_ge(s["rows_q"], 16 * 2 * (NT - TPI))
                for k in range(2):
                    for j in range(TPI):
                        last = nc.scalar.activation(rows[:, k, j, 0:D], xf[:, j, :], ACT.Copy, scale=gate[:, k, j:j + 1])
                last.then_inc(s["gated"], 1)
                for n in range(2):
                    split_high(act, 0, n)

            @block.vector
            def _(dve):
                v = nc.vector

                def then(ins):
                    v.drain()
                    return ins

                for half, keys in zero_keys:
                    last = nc.vector.memset(k_hi[half, :, :, keys].bitcast(F32), 0.0)
                last.then_inc(s["k_zero"], 1)

                def token_stats(i, gl):
                    par = gl % 2
                    for j in range(2):
                        nc.vector.bn_stats(stat6[:, par, j, :], pick(x1, tile_at(i, 2 * gl + j)))
                    nc.vector.drain()
                    for j in range(2):
                        last = nc.vector.bn_aggr(mv[:, par, j, :], stat6[:, par, j, :])
                    last.then_inc(s["xstat"], 1)

                def normalise(i, gl):
                    par = gl % 2
                    dve.wait_ge(s["xrstd"], GPI * i + gl + 1)
                    for j in range(2):
                        last = nc.vector.tensor_scalar(xn[:, par, j, :], pick(x1, tile_at(i, 2 * gl + j)), mv[:, par, j, 0:1], rstd[:, par, j:j + 1],
                                                       ALU.subtract, ALU.mult)
                    last.then_inc(s["xn"], 1)

                def low_part(g, k, banks, par):
                    dve.wait_ge(s["proj_hi"][k], g + 1)
                    at = M_BANK[banks[k]]
                    if k == 0:
                        last = nc.vector.tensor_tensor(xT_lo[:, :, :].rearrange("p c (j t) -> p j c t", j=2),
                                                       at[:, :].rearrange("p (j c t) -> p j c t", j=2, c=KD),
                                                       xT_hi[:, :, :].rearrange("p c (j t) -> p j c t", j=2).bitcast(F32), ALU.subtract)
                    else:
                        queries = slice(2 * k - 2, 2 * k)
                        last = nc.vector.tensor_tensor(q_lo[par][:, queries, :].rearrange("p m t -> p (m t)"), at[:, :],
                                                       q_hi[par][:, queries, :].rearrange("p m t -> p (m t)").bitcast(F32), ALU.subtract)
                    last.then_inc(s["proj_sb"][k], 1)

                def maxima(i, u):
                    for hf in range(2):
                        dve.wait_ge(s["scores"][hf], UPI * i + u + 1)
                        nc.vector.tensor_reduce(nmax[:, u % 4, 2 * hf:2 * hf + 2], S_BANK[hf][:, 0:2 * NKB].rearrange("p (m k) -> p m k", m=2),
                                                AX_X, ALU.max, negate=True).then_inc(s["smax"][hf], 1)
                        yield

                def scale_out(i, u):
                    half = (u % UPT) // 2
                    U = UPI * i + u
                    dve.wait_ge(s["pv"], U + 1)
                    nc.vector.reciprocal(rsum[:, :], psum_row[:, (u // UPT) % 2, 8 * half:8 * half + 8])
                    nc.vector.drain()
                    nc.vector.tensor_tensor(o_sb[:, half * 512:(half + 1) * 512].rearrange("p (h d) -> p h d", h=8),
                                            O_BANK[half][:, :].rearrange("p (h d) -> p h d", h=8),
                                            rsum[:, :].unsqueeze(2).to_broadcast([P, 8, DH]), ALU.mult).then_inc(s["o_sb"][half], 1)

                def residual_group(i, u):
                    return GPI * i + (u // UPT - 1) // 2

                def transposed_out(i, u):
                    half = (u % UPT) // 2
                    part = slice(4 * half, 4 * half + 4)
                    dve.wait_ge(s["ot_hi"][half], TPI * i + u // UPT)
                    nc.vector.tensor_tensor(oT_lo[:, part, :].rearrange("p c t -> p (c t)"), O_BANK[half][:, :],
                                            oT_hi[:, part, :].rearrange("p c t -> p (c t)").bitcast(F32), ALU.subtract).then_inc(s["ot_sb"][half], 1)

                def add_residual(i, u):
                    dve.wait_ge(s["y"], TPI * i + u // UPT)
                    dve.wait_ge(s["xres"], residual_group(i, u) + 1)
                    tile = pick(x1, tile_at(i, u // UPT - 1))
                    nc.vector.scalar_tensor_tensor(tile, M_BANK[1][:, 0:D], tgx[:, 0:1], tile, ALU.mult, ALU.add).then_inc(s["y_sb"], 1)

                def over_experts(ap):
                    return ap.unsqueeze(2).to_broadcast([P, TPI, E])

                def block_stats(i, j):
                    v.drain()
                    v.bn_stats(stat_b[:, 0, j, :], pick(x1, tile_at(i, j - TPI)))
                    v.drain()
                    last = v.bn_aggr(mv_b[:, 0, j, :], stat_b[:, 0, j, :])
                    if j % 2 == 1:
                        last.then_inc(s["stat1"][j // 2], 1)

                def norm_stats(i, b):
                    dve.wait_ge(s["xin"][b], i)
                    for j in (2 * b, 2 * b + 1):
                        v.bn_stats(stat_b[:, 1, j, :], xin[:, j, :])
                    v.drain()
                    for j in (2 * b, 2 * b + 1):
                        last = v.bn_aggr(mv_b[:, 1, j, :], stat_b[:, 1, j, :])
                    last.then_inc(s["stat2"][b], 1)

                def first_norm(b):
                    dve.wait_ge(s["rstd"][b], NI)
                    for j in (2 * b, 2 * b + 1):
                        last = v.tensor_scalar(xin[:, j, :], pick(x1, tile_at(NI, j - TPI)), mv_b[:, 0, j, 0:1], rstd_b[:, 0, j:j + 1], ALU.subtract, ALU.mult)
                    last.then_inc(s["xin"][b], 1)
                    v.drain()

                def second_norm(b):
                    dve.wait_ge(s["rstd"][2 + b], NI)
                    dve.wait_ge(s["rows_made"], NI - 1)
                    for j in (2 * b, 2 * b + 1):
                        v.scalar_tensor_tensor(xf[:, j, :], xin[:, j, :], mv_b[:, 1, j, 0:1], gamma_b[:, :], ALU.subtract, ALU.mult)
                    v.drain()
                    for j in (2 * b, 2 * b + 1):
                        last = v.scalar_tensor_tensor(xf[:, j, :], xf[:, j, :], rstd_b[:, 1, j:j + 1], beta_b[:, :], ALU.mult, ALU.add)
                    last.then_inc(s["xf"], 1)

                def start_output(i, b):
                    two = slice(2 * b, 2 * b + 2)
                    at_least(dve, s["out0_q"], 32 * (i - 1))
                    v.scalar_tensor_tensor(out0[:, two, :], xin[:, two, :], tgf[:, 0:1], two_tiles(i, b), ALU.mult, ALU.add).then_inc(s["out0"], 1)

                def turned_features(i):
                    dve.wait_ge(s["xfT_ps"], 2 * i)
                    v.tensor_copy(xfT[:, 4:8, :].rearrange("p c t -> p (c t)"), TB[:, :]).then_inc(s["xfT_sb"][1], 1)

                def clamped_logits(i, at):
                    dve.wait_ge(s["logits"], 2 * i)
                    v.tensor_scalar(lg[:, :, :], at[:, LG0:LG0 + TPI * E].rearrange("p (t e) -> p t e", t=TPI),
                                    CLAMP, -CLAMP, ALU.min, ALU.max).then_inc(s["lg_read"], 1)

                def shifted_logits(i):
                    v.drain()
                    then(v.tensor_reduce(lmax[:, :], lg[:, :, :], AX_X, ALU.max))
                    v.tensor_tensor(lsh[:, :, :], lg[:, :, :], over_experts(lmax[:, :]), ALU.subtract).then_inc(s["lsh"], 1)

                def router_probs(i):
                    dve.wait_ge(s["ex"], i)
                    then(v.tensor_reduce(esum[:, :], ex[:, :, :], AX_X, ALU.add))
                    then(v.tensor_scalar(esum[:, :], esum[:, :], ROUTER_EPS, None, ALU.add))
                    then(v.reciprocal(erec[:, :], esum[:, :]))
                    then(v.tensor_tensor(pr[0][:, :, :], ex[:, :, :], over_experts(erec[:, :]), ALU.mult))
                    then(v.tensor_scalar(pr[0][:, :, :], pr[0][:, :, :], ROUTER_EPS, 1.0, ALU.max, ALU.min))

                def choose(i, k):
                    then(v.tensor_reduce(gate[:, k, :], pr[k][:, :, :], AX_X, ALU.max))
                    then(v.tensor_tensor(top[:, :, :], pr[k][:, :, :], over_experts(gate[:, k, :]), ALU.is_ge))
                    then(v.tensor_tensor(top[:, :, :], top[:, :, :], tie_rank[:, :, :], ALU.mult))
                    then(v.tensor_reduce(topm[:, :], top[:, :, :], AX_X, ALU.max))
                    then(v.tensor_tensor(pick1[:, k, :, :], top[:, :, :], over_experts(topm[:, :]), ALU.is_equal))
                    if k == 0:
                        then(v.scalar_tensor_tensor(pr[1][:, :, :], pick1[:, 0, :, :], -4.0, pr[0][:, :, :], ALU.mult, ALU.add))
                    else:
                        v.tensor_tensor(chosen[:, :, :], pick1[:, 0, :, :], pick1[:, 1, :, :], ALU.add).then_inc(s["chosen"], 1)

                def count_rows(i):
                    dve.wait_ge(s["pos_ps"], i)
                    v.tensor_tensor(pos[:, :, :], TB[:, LG0:LG0 + TPI * E].rearrange("p (t e) -> p t e", t=TPI),
                                    base_cnt[:, :].unsqueeze(1).to_broadcast([P, TPI, E]), ALU.add)
                    v.drain()
                    v.tensor_tensor(base_cnt[:, :], base_cnt[:, :], TB[:, LG0 + TPI * E:LG0 + (TPI + 1) * E], ALU.add).then_inc(s["pos_read"], 1)

                def number_rows(i):
                    then(v.tensor_tensor(pos[:, :, :], pos[:, :, :], region0[:, :, :], ALU.add))
                    then(v.tensor_tensor(posm[:, :, :, :], pick1[:, :, :, :], pos[:, :, :].unsqueeze(1).to_broadcast([P, 2, TPI, E]), ALU.mult))
                    then(v.tensor_reduce(rowf[:, :, :], posm[:, :, :, :], AX_X, ALU.add))
                    v.tensor_copy(row[:, :, :], rowf[:, :, :]).then_inc(s["row_sb"], 1)

                def route_step_early(i, u):
                    if u == TURN + 1:
                        turned_features(i)
                    if u == LOGIT + 1:
                        clamped_logits(i, TB)

                def route_step(i, u):
                    if u in (5, 6):
                        norm_stats(i, u - 5)
                    if u in (7, 8):
                        start_output(i, u - 7)
                    if u == LOGIT + 2:
                        choose(i, 0)
                    if u == LOGIT + 3:
                        choose(i, 1)
                    if u == COUNT + 1:
                        number_rows(i)

                def slot(i, u):
                    first = isinstance(i, int) and i == 0
                    last = isinstance(i, int) and i == NI - 1
                    w, g = u % 8, GPI * i + u // 8 + 1
                    if not first:
                        route_step_early(i, u)
                    ahead = maxima(i, u + 2) if not (last and u + 2 >= UPI) else iter(())
                    next(ahead, None)
                    if not first and u == LOGIT + 1:
                        shifted_logits(i)
                    if not first and u == LOGIT + 2:
                        router_probs(i)
                    if u % 2 == 1 and not (first and u < 2):
                        scale_out(i, u - 2)
                    dve.wait_ge(s["ptB"], UPI * i + u + 1)
                    nc.vector.tensor_copy(pT[u % 2][:, 3:5, :].rearrange("p b t -> p (b t)"), TB[:, 0:2 * P]).then_inc(s["ptB_sb"], 1)
                    next(ahead, None)
                    if u % UPT == 0 and u // UPT >= 2:
                        block_stats(i + 1, u // UPT - 2)
                    elif u % UPT == 0 and not first:
                        block_stats(i, u // UPT + 2)
                    if w == 2 and not last:
                        token_stats(i + 1, u // 8)
                    if w == 7 and not last:
                        normalise(i + 1, u // 8)
                    if not first:
                        route_step(i, u)
                        if u == COUNT:
                            count_rows(i)
                    if u % 2 == 0 and not (first and u < UPT):
                        transposed_out(i, u)
                    if w in JOB_SLOT and not (last and u >= 8):
                        low_part(g, JOB_SLOT[w], JOB_BANK, (u // 8 + 1) % 2)
                    if w % UPT == UPT - 1 and not (first and u < UPT):
                        add_residual(i, u)

                for m in range(H // 2):
                    if m == 2:
                        dve.wait_ge(s["x_in"][0], 16)
                        token_stats(0, 0)
                    if m == 6:
                        normalise(0, 0)
                    dve.wait_ge(s["k_hi"], m + 1)
                    for a in range(2):
                        half, keys = slice(a * DH, (a + 1) * DH), slice(a * NKB, (a + 1) * NKB)
                        last = nc.vector.scalar_tensor_tensor(k_lo[half, m, :, keys], bank[m % 4][half, 0:B * NKB].rearrange("p (b k) -> p b k", b=B),
                                                              SCALE, k_hi[half, m, :, keys].bitcast(F32), ALU.mult, ALU.subtract)
                    last.then_inc(s["k_lo"], 1)

                def value(b, m):
                    n = b * (len(pieces) // 2) + m
                    dve.wait_ge(s["vp"], n + 1)
                    nc.vector.tensor_copy(vdiag[:, b, :, 2 * m * DH:(2 * m + 2) * DH],
                                          V_BANK[n % 4][:, :].rearrange("p (g c) -> p g c", g=H // HQ)).then_inc(s["vdone"], 1)

                low_part(0, 0, FIRST_BANK, 0)
                for m in range(len(pieces) // 2):
                    value(0, m)
                    if 0 < m <= KD:
                        dve.wait_ge(s["wq_hi"], m)
                        nc.vector.tensor_tensor(wq_lo[:, m - 1, :], wq_raw[:, m - 1, :], wq_hi[:, m - 1, :].bitcast(F32), ALU.subtract).then_inc(s["wq_lo"], 1)
                dve.wait_ge(s["x_in"][2], 16)
                token_stats(0, 1)
                for k in range(1, 5):
                    low_part(0, k, FIRST_BANK, 0)
                for u in range(2):
                    for _ in maxima(0, u):
                        pass
                    if u == 0:
                        normalise(0, 1)
                    for m in (2 * u, 2 * u + 1):
                        value(1, m)
                nc.vector.drain()
                nc.vector.memset(TB[96:P, P:2 * P], 0.0).then_inc(s["vdone"], 1)
                for n in range(4):
                    dve.wait_ge(s["x_in"][n], 16)
                for u in range(UPI):
                    slot(0, u)
                with dve.Fori(1, NI - 1) as i:
                    for u in range(UPI):
                        slot(i, u)
                for u in range(UPI):
                    slot(NI - 1, u)
                dve.wait_ge(s["zero"], 1)
                then(v.tensor_tensor(padf[:, :], base_cnt[:, :], region0[:, 0, :], ALU.add))
                v.tensor_copy(pad[:, :], padf[:, :]).then_inc(s["pads"], 1)
                scale_out(NI, -1)
                block_stats(NI, 2)
                for u in (0, 2):
                    transposed_out(NI, u)
                first_norm(0)
                norm_stats(NI, 0)
                add_residual(NI, 3)
                block_stats(NI, 3)
                second_norm(0)
                first_norm(1)
                norm_stats(NI, 1)
                start_output(NI, 0)
                second_norm(1)
                start_output(NI, 1)
                turned_features(NI)
                clamped_logits(NI, S_BANK[0])
                shifted_logits(NI)
                router_probs(NI)
                choose(NI, 0)
                choose(NI, 1)
                count_rows(NI)
                number_rows(NI)
                then(v.tensor_scalar(cnt1[:, :], base_cnt[:, :], float(P - 1), None, ALU.add))
                then(v.tensor_copy(cnti[:, :], cnt1[:, :]))
                then(v.tensor_scalar(cnti[:, :], cnti[:, :], P.bit_length() - 1, None, ALU.logical_shift_right))
                then(v.tensor_scalar(tiles[:, :], cnti[:, :], 1, None, ALU.max))
                then(v.scalar_tensor_tensor(key[:, :], tiles[:, :], float(E), expert_no[:, :], ALU.mult, ALU.subtract))
                by_expert = [P, E, E]
                then(v.tensor_tensor(ahead_of[:, :, :], key[:, :].unsqueeze(1).to_broadcast(by_expert), key[:, :].unsqueeze(2).to_broadcast(by_expert), ALU.is_gt))
                then(v.tensor_reduce(rank_e[:, :], ahead_of[:, :, :], AX_X, ALU.add))
                then(v.tensor_tensor(at_rank[:, :, :], expert_no[:, :].unsqueeze(2).to_broadcast(by_expert), rank_e[:, :].unsqueeze(1).to_broadcast(by_expert), ALU.is_equal))
                then(v.tensor_tensor(at_rank[:, :, :], at_rank[:, :, :], expert_no[:, :].unsqueeze(1).to_broadcast(by_expert), ALU.mult))
                then(v.tensor_reduce(order_f[:, :], at_rank[:, :, :], AX_X, ALU.add))
                v.tensor_copy(order[:, :], order_f[:, :]).then_inc(s["order"], 1)
                then(v.tensor_tensor(ahead_of[:, :, :], ahead_of[:, :, :], tiles[:, :].unsqueeze(1).to_broadcast(by_expert), ALU.mult))
                then(v.tensor_reduce(start[:, :], ahead_of[:, :, :], AX_X, ALU.add))
                then(v.tensor_tensor(end[:, :], start[:, :], tiles[:, :], ALU.add))
                by_slot = [P, MT, E]
                slots = slot_no[:, :].unsqueeze(2).to_broadcast(by_slot)
                v.tensor_tensor(past[:, :, :], slots, end[:, :].unsqueeze(1).to_broadcast(by_slot), ALU.is_ge)
                then(v.tensor_tensor(within[:, :, :], slots, start[:, :].unsqueeze(1).to_broadcast(by_slot), ALU.is_ge))
                v.tensor_reduce(rank_j[:, :], past[:, :, :], AX_X, ALU.add)
                then(v.tensor_tensor(within[:, :, :], within[:, :, :], past[:, :, :], ALU.subtract))
                then(v.scalar_tensor_tensor(start[:, :], expert_no[:, :], -float(REG // P), start[:, :], ALU.mult, ALU.add))
                then(v.tensor_tensor(past[:, :, :], slots, start[:, :].unsqueeze(1).to_broadcast(by_slot), ALU.subtract))
                then(v.tensor_tensor(past[:, :, :], past[:, :, :], within[:, :, :], ALU.mult))
                then(v.tensor_reduce(row_j[:, :], past[:, :, :], AX_X, ALU.add))
                then(v.tensor_scalar(none_left[:, :], rank_j[:, :], float(E), float(DUMMY // P), ALU.is_ge, ALU.mult))
                then(v.tensor_tensor(row_j[:, :], row_j[:, :], none_left[:, :], ALU.add))
                then(v.tensor_scalar(rank_j[:, :], rank_j[:, :], float(E - 1), None, ALU.min))
                v.tensor_copy(table[:, 0, :], rank_j[:, :])
                v.tensor_copy(table[:, 1, :], row_j[:, :]).then_inc(s["table"], 1)
                for n in range(2):
                    split_low(dve, 0, n)

        block = ctx.enter_context(nc.Block())

        @block.sync
        def _(sp):
            def slot(i, p):
                load_rows(sp, i + (p + 2) // RT, (p + 2) % RT)
                if p == 1:
                    sp.wait_ge(s["w_in"], 32 * (i + 2))
                    load_weights(sp, i + 2)

            load_weights(sp, 1)
            for p in range(RT):
                slot(0, p)
            with sp.Fori(1, E - 2) as i:
                for p in range(RT):
                    slot(i, p)
            with sp.Fori(E - 2, LOOPS) as i:
                for p in range(RT):
                    load_rows(sp, i + (p + 2) // RT, (p + 2) % RT)
            for j in range(RT * LOOPS + 2, MT):
                load_rows(sp, *divmod(j, RT))

        @block.gpsimd
        def _(pool):
            def tokens(i, p):
                j = RT * i + p
                pool.wait_ge(s["xq_in"][p % 2], 16 * ((RT // 2) * i + p // 2 + 1))
                at_least(pool, s["e_idx"], j - RT + 1)
                nc.gpsimd.tensor_tensor(tok[p][:, :], xq[p % 2][:, D:RW].bitcast(U32), no_offset[:, :], ALU.add).then_inc(s["e_tok"], 1)

            def scatter_add(i, p):
                j = RT * i + p
                pool.wait_ge(s["e_ysb"], j + 1)
                pool.wait_ge(s["e_tok"], j + 1)
                at_least(pool, s["e_add"], 16 * j)
                nc.gpsimd.tensor_tensor(to_row[:, :], tok[p][:, :], no_offset[:, :], ALU.add).then_inc(s["e_idx"], 1)
                nc.gpsimd.drain()
                nc.gpsimd.indirect_dma_start(out[:, :], bass.IndirectOffsetOnAxis(to_row[:, 0:1], 0), yq[p % 2][:, :], None,
                                             compute_op=ALU.add).then_inc(s["e_add"], 16)

            def slot(i, p):
                if not (isinstance(i, int) and RT * i + p + 2 >= MT):
                    tokens(i + (p + 2) // RT, (p + 2) % RT)
                scatter_add(i, p)

            nc.gpsimd.memset(no_offset[:, :], 0)
            nc.gpsimd.drain()
            tokens(0, 0)
            tokens(0, 1)
            for p in range(RT):
                slot(0, p)
            with pool.Fori(1, LOOPS) as i:
                for p in range(RT):
                    slot(i, p)
            for j in range(RT * LOOPS, MT):
                slot(*divmod(j, RT))
            pool.wait_ge(s["e_add"], 16 * MT)

        @block.tensor
        def _(pe):
            def transpose_rows(i, p):
                j = RT * i + p
                pe.wait_ge(s["xq_in"][p % 2], 16 * ((RT // 2) * i + p // 2 + 1))
                at_least(pe, s["eT_lo"], j)
                for c in range(KD):
                    last = nc.tensor.transpose(XT_BANK[:, c * P:(c + 1) * P], xq[p % 2][:, c * P:(c + 1) * P], ident[:, :])
                last.then_inc(s["eT_ps"], 1)

            def rank_of(i, p):
                j = RT * i + p
                return pe.value_load(table[0:1, 0, bass.ds(j, 1)] if not isinstance(j, int) else table[0:1, 0, j:j + 1], min_val=0, max_val=E - 1)

            def weights(part, rank, col, n):
                return part[:, bass.ds(rank, 1), col:col + n].rearrange("p a f -> p (a f)")

            def up(i, p, rank, half, at, done, free):
                j = RT * i + p
                pe.wait_ge(s["eT_lo"], j + 1)
                at_least(pe, s[free], j - 1)
                n = 0
                for c in range(KD):
                    for rows, w in ((xqT_hi, gu_hi), (xqT_lo, gu_hi), (xqT_hi, gu_lo)):
                        last = nc.tensor.matmul(at[p % 2][:, :], rows[:, c, :], weights(w, rank, c * FF2 + half * FF, FF),
                                                start=(n == 0), stop=(n == 3 * KD - 1))
                        n += 1
                last.then_inc(s[done], 1)

            def transpose_hidden(i, p):
                j = RT * i + p
                pe.wait_ge(s["e_hid"], j + 1)
                at_least(pe, s["e_hT_lo"], j)
                for c in range(KF):
                    last = nc.tensor.transpose(HT_BANK[:, c * P:(c + 1) * P], hid[p % 2][:, c * P:(c + 1) * P], ident[:, :])
                last.then_inc(s["e_hT_ps"], 1)

            def down(i, p, rank):
                j = RT * i + p
                pe.wait_ge(s["e_hT_lo"], j + 1)
                at_least(pe, s["e_ysb"], j - 1)
                n = 0
                for c in range(KF):
                    for h, w in ((hidT_hi, dn_hi), (hidT_lo, dn_hi), (hidT_hi, dn_lo)):
                        last = nc.tensor.matmul(Y_BANK[p % 2][:, 0:D], h[:, c, :], weights(w, rank, c * D, D),
                                                start=(n == 0), stop=(n == 3 * KF - 1))
                        n += 1
                last.then_inc(s["e_y"], 1)

            def slot(i, p, behind=True, more=True, new_rank=True):
                rank = rank_of(i, p)
                tile_before = (i - 1, RT - 1) if p == 0 else (i, p - 1)
                if p == 0 and new_rank:
                    first = isinstance(i, int)
                    pe.wait_ge(s["w_lo"], 2 if first else len(CHUNKS) * (i + 1))
                if p == 1 and new_rank and isinstance(i, int):
                    pe.wait_ge(s["w_lo"], len(CHUNKS))
                if behind:
                    transpose_hidden(*tile_before)
                up(i, p, rank, 0, G_BANK, "e_gate", "e_silu")
                if more:
                    transpose_rows(i + (p + 1) // RT, (p + 1) % RT)
                up(i, p, rank, 1, U_BANK, "e_up", "e_hid")
                if behind:
                    down(*tile_before, rank_of(*tile_before))

            transpose_rows(0, 0)
            for p in range(RT):
                slot(0, p, behind=(p > 0))
            with pe.Fori(1, E) as i:
                for p in range(RT):
                    slot(i, p)
            with pe.Fori(E, LOOPS) as i:
                for p in range(RT):
                    slot(i, p, new_rank=False)
            for j in range(RT * LOOPS, MT):
                slot(*divmod(j, RT), new_rank=False, more=(j < MT - 1))
            last_tile = divmod(MT - 1, RT)
            transpose_hidden(*last_tile)
            down(*last_tile, rank_of(*last_tile))

        @block.scalar
        def _(act):
            def rows_T(i, p):
                j = RT * i + p
                act.wait_ge(s["eT_ps"], j + 1)
                at_least(act, s["e_up"], j)
                nc.scalar.copy(xqT_hi[:, :, :].rearrange("p c t -> p (c t)"), XT_BANK[:, 0:KD * P]).then_inc(s["eT_hi"], 1)

            def silu(i, p):
                j = RT * i + p
                act.wait_ge(s["e_gate"], j + 1)
                at_least(act, s["e_hT_ps"], j - 1)
                nc.scalar.activation(hid[p % 2][:, :], G_BANK[p % 2][:, :], ACT.Silu).then_inc(s["e_silu"], 1)

            def hidden_T(i, p):
                j = RT * i + p
                act.wait_ge(s["e_hT_ps"], j + 1)
                at_least(act, s["e_y"], j)
                nc.scalar.copy(hidT_hi[:, :, :].rearrange("p c t -> p (c t)"), HT_BANK[:, :]).then_inc(s["e_hT_hi"], 1)

            def scaled(i, p):
                j = RT * i + p
                act.wait_ge(s["e_y"], j + 1)
                at_least(act, s["e_add"], 16 * (j - 1))
                nc.scalar.activation(yq[p % 2][:, :], Y_BANK[p % 2][:, 0:D], ACT.Copy, scale=tgf[:, 0:1]).then_inc(s["e_ysb"], 1)

            def slot(i, p, chunks=(), behind=True, more=True):
                tile_before = (i - 1, RT - 1) if p == 0 else (i, p - 1)
                if behind:
                    hidden_T(*tile_before)
                silu(i, p)
                if more:
                    rows_T(i + (p + 1) // RT, (p + 1) % RT)
                for n in chunks:
                    split_high(act, i + 1, n)
                if behind:
                    scaled(*tile_before)

            rows_T(0, 0)
            split_high(act, 0, 2)
            for p in range(RT):
                slot(0, p, FIRST_CHUNKS[p], behind=(p > 0))
            with act.Fori(1, E - 1) as i:
                for p in range(RT):
                    slot(i, p, (p,) if p < len(CHUNKS) else ())
            with act.Fori(E - 1, LOOPS) as i:
                for p in range(RT):
                    slot(i, p)
            for j in range(RT * LOOPS, MT):
                slot(*divmod(j, RT), more=(j < MT - 1))
            hidden_T(*divmod(MT - 1, RT))
            scaled(*divmod(MT - 1, RT))

        @block.vector
        def _(dve):
            def rows_T(i, p):
                j = RT * i + p
                dve.wait_ge(s["eT_hi"], j + 1)
                nc.vector.tensor_tensor(xqT_lo[:, :, :].rearrange("p c t -> p (c t)"), XT_BANK[:, 0:KD * P],
                                        xqT_hi[:, :, :].rearrange("p c t -> p (c t)").bitcast(F32), ALU.subtract).then_inc(s["eT_lo"], 1)

            def gated(i, p):
                j = RT * i + p
                dve.wait_ge(s["e_silu"], j + 1)
                dve.wait_ge(s["e_up"], j + 1)
                nc.vector.tensor_tensor(hid[p % 2][:, :], hid[p % 2][:, :], U_BANK[p % 2][:, :], ALU.mult).then_inc(s["e_hid"], 1)

            def hidden_T(i, p):
                j = RT * i + p
                dve.wait_ge(s["e_hT_hi"], j + 1)
                nc.vector.tensor_tensor(hidT_lo[:, :, :].rearrange("p c t -> p (c t)"), HT_BANK[:, :],
                                        hidT_hi[:, :, :].rearrange("p c t -> p (c t)").bitcast(F32), ALU.subtract).then_inc(s["e_hT_lo"], 1)

            def slot(i, p, chunks=(), behind=True, more=True):
                if behind:
                    hidden_T(*((i - 1, RT - 1) if p == 0 else (i, p - 1)))
                gated(i, p)
                if more:
                    rows_T(i + (p + 1) // RT, (p + 1) % RT)
                for n in chunks:
                    split_low(dve, i + 1, n)

            rows_T(0, 0)
            split_low(dve, 0, 2)
            for p in range(RT):
                slot(0, p, FIRST_CHUNKS[p], behind=(p > 0))
            with dve.Fori(1, E - 1) as i:
                for p in range(RT):
                    slot(i, p, (p,) if p < len(CHUNKS) else ())
            with dve.Fori(E - 1, LOOPS) as i:
                for p in range(RT):
                    slot(i, p)
            for j in range(RT * LOOPS, MT):
                slot(*divmod(j, RT), more=(j < MT - 1))
            hidden_T(*divmod(MT - 1, RT))


_INS = ['x', 'ctxT', 'g_xattn', 'g_ffn', 'L0_xattn_Wq', 'L0_xattn_Wk', 'L0_xattn_Wv', 'L0_xattn_Wo', 'L0_xattn_bo',
        'L0_ffn_ln_gamma', 'L0_ffn_ln_beta', 'router_wT', 'gate_up_wT', 'down_wT']


def kernel(**inputs):
    import numpy as _np
    import concourse.bacc as _bacc
    from concourse import mybir as _mybir
    from concourse.bass_utils import run_bass_kernel_spmd as _run

    laid = {k: _np.asarray(v) for k, v in inputs.items()}
    laid['ctxT'] = laid['ctx_768'].transpose(0, 2, 1)
    laid['router_wT'] = laid['L0_ffn_router_w'].transpose(1, 0)
    laid['gate_up_wT'] = laid['L0_ffn_gate_up_w'].transpose(0, 2, 1)
    laid['down_wT'] = laid['L0_ffn_down_w'].transpose(0, 2, 1)
    B, SEQ, D = laid['x'].shape
    nc = _bacc.Bacc("TRN2", target_bir_lowering=False, num_devices=1)
    arrays, args = {}, []
    for name in _INS:
        a = _np.ascontiguousarray(laid[name])
        arrays[f"in_{name}_dram"] = a
        args.append(nc.dram_tensor(f"in_{name}_dram", a.shape, _mybir.dt.from_np(a.dtype), kind="ExternalInput").ap())
    out = nc.dram_tensor("out_dram", (B * SEQ + 128, D), _mybir.dt.float32, kind="ExternalOutput").ap()
    gated_xattn_moe(nc, *args, out)
    r = _run(nc, [arrays], core_ids=[0])
    return r.results[0]["out_dram"][:B * SEQ].reshape(B, SEQ, D)
```
